# Optimizing a Trainium2 kernel written in Bass

```python
import numpy as np
import jax
import jax.numpy as jnp

def _softmax(x, axis=-1):
    return jax.nn.softmax(x, axis=axis)

def _gelu(x):
    return jax.nn.gelu(x, approximate=True)

def _silu(x):
    return jax.nn.silu(x)

def _sigmoid(x):
    return jax.nn.sigmoid(x)

def _layernorm(x, axis=-1, eps=1e-05):
    m = jnp.mean(x, axis=axis, keepdims=True)
    v = jnp.var(x, axis=axis, keepdims=True)
    return (x - m) / jnp.sqrt(v + eps)

def _scatter_add(tgt, idx, src, axis=0):
    return tgt.at[idx].add(src)

def _segment_sum(src, seg, n):
    return jax.ops.segment_sum(src, seg, n)
kernel_name = 'mk_seq_postln_d2_jaxref_r8_1966e7'

def setup_inputs(seed: int=0):
    np.random.seed(seed)
    _w = jnp.asarray

    def _L0_attn_setup():
        import jax, jax.numpy as jnp
        import numpy as np
        D_MODEL = 128
        NUM_HEADS = 16
        D_K = D_MODEL // NUM_HEADS
        THETA = 10000.0
        SEQ = 256
        BATCH = 2

        def _rope(t):
            half = D_K // 2
            inv = THETA ** (-2.0 * jnp.arange(half, dtype=jnp.float32) / D_K)
            pos = jnp.arange(t.shape[-2], dtype=jnp.float32)
            ang = pos[:, None] * inv[None, :]
            cos, sin = (jnp.cos(ang), jnp.sin(ang))
            tp = t.reshape(t.shape[:-1] + (half, 2))
            x0, x1 = (tp[..., 0], tp[..., 1])
            r0 = cos * x0 - sin * x1
            r1 = sin * x0 + cos * x1
            return jnp.stack([r0, r1], axis=-1).reshape(t.shape)
        key = jax.random.key(seed)
        ks = jax.random.split(key, 5)
        std = (2.0 / (D_MODEL + D_MODEL)) ** 0.5
        x = jax.random.normal(ks[0], (BATCH, SEQ, D_MODEL), dtype=jnp.float32)
        wq = jax.random.normal(ks[1], (D_MODEL, D_MODEL), dtype=jnp.float32) * std
        wk = jax.random.normal(ks[2], (D_MODEL, D_MODEL), dtype=jnp.float32) * std
        wv = jax.random.normal(ks[3], (D_MODEL, D_MODEL), dtype=jnp.float32) * std
        wo = jax.random.normal(ks[4], (D_MODEL, D_MODEL), dtype=jnp.float32) * std
        return {'x': x, 'wq': wq, 'wk': wk, 'wv': wv, 'wo': wo}
    _L0_attn_in = _L0_attn_setup()

    def _L0_ffn_setup():
        import jax, jax.numpy as jnp
        import numpy as np
        import math
        N_EMBD = 128
        HIDDEN = 4 * N_EMBD
        N_EXPERTS = 8
        TOP_K = 2
        B, T = (4, 256)

        def new_gelu(x):
            c = math.sqrt(2.0 / math.pi)
            return 0.5 * x * (1.0 + jnp.tanh(c * (x + 0.044715 * x * x * x)))

        def _moe_forward(x, Wfc_s, bfc_s, Wproj_s, bproj_s, Wr, Wfc, bfc, Wproj, bproj):
            Bb, Tt, C = x.shape
            xf = x.reshape(Bb * Tt, C)
            N = Bb * Tt
            shared = new_gelu(xf @ Wfc_s + bfc_s) @ Wproj_s + bproj_s
            logits = xf @ Wr
            probs = jax.nn.softmax(logits, axis=-1)
            topk_p, topk_i = jax.lax.top_k(probs, TOP_K)
            topk_p = topk_p / jnp.sum(topk_p, axis=-1, keepdims=True)
            gate = jnp.zeros((N, N_EXPERTS), dtype=xf.dtype)
            gate = gate.at[jnp.arange(N)[:, None], topk_i].add(topk_p)
            routed = jnp.zeros_like(xf)
            for e in range(N_EXPERTS):
                h = new_gelu(xf @ Wfc[e] + bfc[e]) @ Wproj[e] + bproj[e]
                routed = routed + h * gate[:, e:e + 1]
            return (shared + routed).reshape(Bb, Tt, C)
        key = jax.random.key(seed)
        ks = jax.random.split(key, 10)
        s = 0.02
        return {'x': jax.random.normal(ks[0], (B, T, N_EMBD), dtype=jnp.float32), 'Wfc_s': jax.random.normal(ks[1], (N_EMBD, HIDDEN), dtype=jnp.float32) * s, 'bfc_s': jnp.zeros((HIDDEN,), dtype=jnp.float32), 'Wproj_s': jax.random.normal(ks[2], (HIDDEN, N_EMBD), dtype=jnp.float32) * s, 'bproj_s': jnp.zeros((N_EMBD,), dtype=jnp.float32), 'Wr': jax.random.normal(ks[3], (N_EMBD, N_EXPERTS), dtype=jnp.float32) * s, 'Wfc': jax.random.normal(ks[4], (N_EXPERTS, N_EMBD, HIDDEN), dtype=jnp.float32) * s, 'bfc': jnp.zeros((N_EXPERTS, HIDDEN), dtype=jnp.float32), 'Wproj': jax.random.normal(ks[5], (N_EXPERTS, HIDDEN, N_EMBD), dtype=jnp.float32) * s, 'bproj': jnp.zeros((N_EXPERTS, N_EMBD), dtype=jnp.float32)}
    _L0_ffn_in = _L0_ffn_setup()

    def _L1_attn_setup():
        import math
        import jax, jax.numpy as jnp
        import numpy as np
        NHEAD = 16
        HEAD_DIM = 64
        D_MODEL = 128
        B, T = (2, 512)

        def _cosformer(x, Wq, bq, Wk, bk, Wv, bv, Wo, bo):
            Bsz, Tlen, _ = x.shape
            H, dh = (NHEAD, HEAD_DIM)
            Q = (x @ Wq + bq).reshape(Bsz, Tlen, H, dh)
            K = (x @ Wk + bk).reshape(Bsz, Tlen, H, dh)
            V = (x @ Wv + bv).reshape(Bsz, Tlen, H, dh)
            Qp = jax.nn.relu(Q)
            Kp = jax.nn.relu(K)
            angles = math.pi / (2.0 * Tlen) * jnp.arange(Tlen, dtype=jnp.float32)
            cosw = jnp.cos(angles)[None, :, None, None]
            sinw = jnp.sin(angles)[None, :, None, None]
            Qc, Qs = (Qp * cosw, Qp * sinw)
            Kc, Ks = (Kp * cosw, Kp * sinw)
            tm = lambda a: jnp.moveaxis(a, 1, 0)
            Qc, Qs, Kc, Ks, Vt = (tm(Qc), tm(Qs), tm(Kc), tm(Ks), tm(V))
            S0 = jnp.zeros((Bsz, H, dh, dh), dtype=x.dtype)
            z0 = jnp.zeros((Bsz, H, dh), dtype=x.dtype)

            def step(carry, inp):
                S_cos, S_sin, z_cos, z_sin = carry
                qc, qs, kc, ks_, v = inp
                S_cos = S_cos + kc[..., :, None] * v[..., None, :]
                S_sin = S_sin + ks_[..., :, None] * v[..., None, :]
                z_cos = z_cos + kc
                z_sin = z_sin + ks_
                num = jnp.einsum('bhi,bhij->bhj', qc, S_cos) + jnp.einsum('bhi,bhij->bhj', qs, S_sin)
                den = jnp.sum(qc * z_cos + qs * z_sin, axis=-1)
                den = jnp.maximum(den, 1e-06)[..., None]
                return ((S_cos, S_sin, z_cos, z_sin), num / den)
            _, out = jax.lax.scan(step, (S0, S0, z0, z0), (Qc, Qs, Kc, Ks, Vt))
            out = jnp.moveaxis(out, 0, 1).reshape(Bsz, Tlen, H * dh)
            return out @ Wo + bo
        key = jax.random.key(seed)
        ks = jax.random.split(key, 9)
        HD = NHEAD * HEAD_DIM
        s_in = 1.0 / math.sqrt(D_MODEL)
        s_out = 1.0 / math.sqrt(HD)
        return {'x': jax.random.normal(ks[0], (B, T, D_MODEL), dtype=jnp.float32), 'Wq': jax.random.normal(ks[1], (D_MODEL, HD), dtype=jnp.float32) * s_in, 'bq': jnp.zeros((HD,), dtype=jnp.float32), 'Wk': jax.random.normal(ks[2], (D_MODEL, HD), dtype=jnp.float32) * s_in, 'bk': jnp.zeros((HD,), dtype=jnp.float32), 'Wv': jax.random.normal(ks[3], (D_MODEL, HD), dtype=jnp.float32) * s_in, 'bv': jnp.zeros((HD,), dtype=jnp.float32), 'Wo': jax.random.normal(ks[4], (HD, D_MODEL), dtype=jnp.float32) * s_out, 'bo': jnp.zeros((D_MODEL,), dtype=jnp.float32)}
    _L1_attn_in = _L1_attn_setup()

    def _L1_ffn_setup():
        import jax, jax.numpy as jnp
        import numpy as np
        B, S, H, F, G = (8, 256, 128, 512, 128)
        EPS = 1e-05

        def _dequant(q, scales, g):
            K, N = q.shape
            w = (q.astype(jnp.float32) - 128.0).reshape(K // g, g, N) * scales[:, None, :]
            return w.reshape(K, N)
        key = jax.random.key(seed)
        ks = jax.random.split(key, 8)
        x = jax.random.normal(ks[0], (B, S, H), dtype=jnp.float32)
        ln_gamma = jnp.ones((H,), jnp.float32)
        ln_beta = jnp.zeros((H,), jnp.float32)
        fc1_q = jax.random.randint(ks[1], (H, F), 0, 32, dtype=jnp.int32)
        fc2_q = jax.random.randint(ks[2], (F, H), 0, 32, dtype=jnp.int32)
        fc1_scales = jax.random.uniform(ks[3], (H // G, F), jnp.float32) * 0.02 + 0.001
        fc2_scales = jax.random.uniform(ks[4], (F // G, H), jnp.float32) * 0.02 + 0.001
        fc1_bias = jax.random.normal(ks[5], (F,), jnp.float32) * 0.02
        fc2_bias = jax.random.normal(ks[6], (H,), jnp.float32) * 0.02
        return {'x': x, 'ln_gamma': ln_gamma, 'ln_beta': ln_beta, 'fc1_q': fc1_q, 'fc1_scales': fc1_scales, 'fc1_bias': fc1_bias, 'fc2_q': fc2_q, 'fc2_scales': fc2_scales, 'fc2_bias': fc2_bias}
    _L1_ffn_in = _L1_ffn_setup()
    _d = {'L0_attn_x': _L0_attn_in['x'], 'L0_attn_wq': _L0_attn_in['wq'], 'L0_attn_wk': _L0_attn_in['wk'], 'L0_attn_wv': _L0_attn_in['wv'], 'L0_attn_wo': _L0_attn_in['wo'], 'L0_ffn_Wfc_s': _L0_ffn_in['Wfc_s'], 'L0_ffn_bfc_s': _L0_ffn_in['bfc_s'], 'L0_ffn_Wproj_s': _L0_ffn_in['Wproj_s'], 'L0_ffn_bproj_s': _L0_ffn_in['bproj_s'], 'L0_ffn_Wr': _L0_ffn_in['Wr'], 'L0_ffn_Wfc': _L0_ffn_in['Wfc'], 'L0_ffn_bfc': _L0_ffn_in['bfc'], 'L0_ffn_Wproj': _L0_ffn_in['Wproj'], 'L0_ffn_bproj': _L0_ffn_in['bproj'], 'L1_attn_Wq': _L1_attn_in['Wq'], 'L1_attn_bq': _L1_attn_in['bq'], 'L1_attn_Wk': _L1_attn_in['Wk'], 'L1_attn_bk': _L1_attn_in['bk'], 'L1_attn_Wv': _L1_attn_in['Wv'], 'L1_attn_bv': _L1_attn_in['bv'], 'L1_attn_Wo': _L1_attn_in['Wo'], 'L1_attn_bo': _L1_attn_in['bo'], 'L1_ffn_ln_gamma': _L1_ffn_in['ln_gamma'], 'L1_ffn_ln_beta': _L1_ffn_in['ln_beta'], 'L1_ffn_fc1_q': _L1_ffn_in['fc1_q'], 'L1_ffn_fc1_scales': _L1_ffn_in['fc1_scales'], 'L1_ffn_fc1_bias': _L1_ffn_in['fc1_bias'], 'L1_ffn_fc2_q': _L1_ffn_in['fc2_q'], 'L1_ffn_fc2_scales': _L1_ffn_in['fc2_scales'], 'L1_ffn_fc2_bias': _L1_ffn_in['fc2_bias']}
    _x0 = _d['L0_attn_x']
    _d['L0_attn_x'] = jax.random.normal(jax.random.fold_in(jax.random.key(seed), 1), (16, 256, 128), dtype=_x0.dtype)
    del _x0
    return _d

def reference(L0_attn_x, L0_attn_wq, L0_attn_wk, L0_attn_wv, L0_attn_wo, L0_ffn_Wfc_s, L0_ffn_bfc_s, L0_ffn_Wproj_s, L0_ffn_bproj_s, L0_ffn_Wr, L0_ffn_Wfc, L0_ffn_bfc, L0_ffn_Wproj, L0_ffn_bproj, L1_attn_Wq, L1_attn_bq, L1_attn_Wk, L1_attn_bk, L1_attn_Wv, L1_attn_bv, L1_attn_Wo, L1_attn_bo, L1_ffn_ln_gamma, L1_ffn_ln_beta, L1_ffn_fc1_q, L1_ffn_fc1_scales, L1_ffn_fc1_bias, L1_ffn_fc2_q, L1_ffn_fc2_scales, L1_ffn_fc2_bias):

    def _L0_attn_ref(x, wq, wk, wv, wo):
        import jax, jax.numpy as jnp
        import numpy as np
        D_MODEL = 128
        NUM_HEADS = 16
        D_K = D_MODEL // NUM_HEADS
        THETA = 10000.0
        SEQ = 256
        BATCH = 2

        def _rope(t):
            half = D_K // 2
            inv = THETA ** (-2.0 * jnp.arange(half, dtype=jnp.float32) / D_K)
            pos = jnp.arange(t.shape[-2], dtype=jnp.float32)
            ang = pos[:, None] * inv[None, :]
            cos, sin = (jnp.cos(ang), jnp.sin(ang))
            tp = t.reshape(t.shape[:-1] + (half, 2))
            x0, x1 = (tp[..., 0], tp[..., 1])
            r0 = cos * x0 - sin * x1
            r1 = sin * x0 + cos * x1
            return jnp.stack([r0, r1], axis=-1).reshape(t.shape)
        B, S, D = x.shape
        H, dk = (NUM_HEADS, D_K)

        def split_heads(y):
            return y.reshape(B, S, H, dk).transpose(0, 2, 1, 3)
        Q = split_heads(x @ wq.T)
        K = split_heads(x @ wk.T)
        V = split_heads(x @ wv.T)
        Q = _rope(Q)
        K = _rope(K)
        scores = jnp.einsum('bhqd,bhkd->bhqk', Q, K) / dk ** 0.5
        causal = jnp.tril(jnp.ones((S, S), dtype=bool))
        scores = jnp.where(causal, scores, -jnp.inf)
        probs = jax.nn.softmax(scores, axis=-1)
        out = jnp.einsum('bhqk,bhkd->bhqd', probs, V)
        out = out.transpose(0, 2, 1, 3).reshape(B, S, D)
        return out @ wo.T

    def _L0_ffn_ref(x, Wfc_s, bfc_s, Wproj_s, bproj_s, Wr, Wfc, bfc, Wproj, bproj):
        import jax, jax.numpy as jnp
        import numpy as np
        import math
        N_EMBD = 128
        HIDDEN = 4 * N_EMBD
        N_EXPERTS = 8
        TOP_K = 2
        B, T = (4, 256)

        def new_gelu(x):
            c = math.sqrt(2.0 / math.pi)
            return 0.5 * x * (1.0 + jnp.tanh(c * (x + 0.044715 * x * x * x)))

        def _moe_forward(x, Wfc_s, bfc_s, Wproj_s, bproj_s, Wr, Wfc, bfc, Wproj, bproj):
            Bb, Tt, C = x.shape
            xf = x.reshape(Bb * Tt, C)
            N = Bb * Tt
            shared = new_gelu(xf @ Wfc_s + bfc_s) @ Wproj_s + bproj_s
            logits = xf @ Wr
            probs = jax.nn.softmax(logits, axis=-1)
            topk_p, topk_i = jax.lax.top_k(probs, TOP_K)
            topk_p = topk_p / jnp.sum(topk_p, axis=-1, keepdims=True)
            gate = jnp.zeros((N, N_EXPERTS), dtype=xf.dtype)
            gate = gate.at[jnp.arange(N)[:, None], topk_i].add(topk_p)
            routed = jnp.zeros_like(xf)
            for e in range(N_EXPERTS):
                h = new_gelu(xf @ Wfc[e] + bfc[e]) @ Wproj[e] + bproj[e]
                routed = routed + h * gate[:, e:e + 1]
            return (shared + routed).reshape(Bb, Tt, C)
        return _moe_forward(x, Wfc_s, bfc_s, Wproj_s, bproj_s, Wr, Wfc, bfc, Wproj, bproj)

    def _L1_attn_ref(x, Wq, bq, Wk, bk, Wv, bv, Wo, bo):
        import math
        import jax, jax.numpy as jnp
        import numpy as np
        NHEAD = 16
        HEAD_DIM = 64
        D_MODEL = 128
        B, T = (2, 512)

        def _cosformer(x, Wq, bq, Wk, bk, Wv, bv, Wo, bo):
            Bsz, Tlen, _ = x.shape
            H, dh = (NHEAD, HEAD_DIM)
            Q = (x @ Wq + bq).reshape(Bsz, Tlen, H, dh)
            K = (x @ Wk + bk).reshape(Bsz, Tlen, H, dh)
            V = (x @ Wv + bv).reshape(Bsz, Tlen, H, dh)
            Qp = jax.nn.relu(Q)
            Kp = jax.nn.relu(K)
            angles = math.pi / (2.0 * Tlen) * jnp.arange(Tlen, dtype=jnp.float32)
            cosw = jnp.cos(angles)[None, :, None, None]
            sinw = jnp.sin(angles)[None, :, None, None]
            Qc, Qs = (Qp * cosw, Qp * sinw)
            Kc, Ks = (Kp * cosw, Kp * sinw)
            tm = lambda a: jnp.moveaxis(a, 1, 0)
            Qc, Qs, Kc, Ks, Vt = (tm(Qc), tm(Qs), tm(Kc), tm(Ks), tm(V))
            S0 = jnp.zeros((Bsz, H, dh, dh), dtype=x.dtype)
            z0 = jnp.zeros((Bsz, H, dh), dtype=x.dtype)

            def step(carry, inp):
                S_cos, S_sin, z_cos, z_sin = carry
                qc, qs, kc, ks_, v = inp
                S_cos = S_cos + kc[..., :, None] * v[..., None, :]
                S_sin = S_sin + ks_[..., :, None] * v[..., None, :]
                z_cos = z_cos + kc
                z_sin = z_sin + ks_
                num = jnp.einsum('bhi,bhij->bhj', qc, S_cos) + jnp.einsum('bhi,bhij->bhj', qs, S_sin)
                den = jnp.sum(qc * z_cos + qs * z_sin, axis=-1)
                den = jnp.maximum(den, 1e-06)[..., None]
                return ((S_cos, S_sin, z_cos, z_sin), num / den)
            _, out = jax.lax.scan(step, (S0, S0, z0, z0), (Qc, Qs, Kc, Ks, Vt))
            out = jnp.moveaxis(out, 0, 1).reshape(Bsz, Tlen, H * dh)
            return out @ Wo + bo
        return _cosformer(x, Wq, bq, Wk, bk, Wv, bv, Wo, bo)

    def _L1_ffn_ref(x, ln_gamma, ln_beta, fc1_q, fc1_scales, fc1_bias, fc2_q, fc2_scales, fc2_bias):
        import jax, jax.numpy as jnp
        import numpy as np
        B, S, H, F, G = (8, 256, 128, 512, 128)
        EPS = 1e-05

        def _dequant(q, scales, g):
            K, N = q.shape
            w = (q.astype(jnp.float32) - 128.0).reshape(K // g, g, N) * scales[:, None, :]
            return w.reshape(K, N)
        residual = x
        mu = jnp.mean(x, axis=-1, keepdims=True)
        var = jnp.mean(jnp.square(x - mu), axis=-1, keepdims=True)
        h = (x - mu) * jax.lax.rsqrt(var + EPS) * ln_gamma + ln_beta
        hf = h.reshape(-1, H)
        w1 = _dequant(fc1_q, fc1_scales, G)
        y = hf @ w1 + fc1_bias
        y = jax.nn.silu(y)
        w2 = _dequant(fc2_q, fc2_scales, G)
        z = y @ w2 + fc2_bias
        return residual + 0.5 * z.reshape(residual.shape)
    x = L0_attn_x
    x = _layernorm(x + _L0_attn_ref(x, L0_attn_wq, L0_attn_wk, L0_attn_wv, L0_attn_wo), axis=-1)
    x = _layernorm(x + _L0_ffn_ref(x, L0_ffn_Wfc_s, L0_ffn_bfc_s, L0_ffn_Wproj_s, L0_ffn_bproj_s, L0_ffn_Wr, L0_ffn_Wfc, L0_ffn_bfc, L0_ffn_Wproj, L0_ffn_bproj), axis=-1)
    x = _layernorm(x + _L1_attn_ref(x, L1_attn_Wq, L1_attn_bq, L1_attn_Wk, L1_attn_bk, L1_attn_Wv, L1_attn_bv, L1_attn_Wo, L1_attn_bo), axis=-1)
    x = _layernorm(x + _L1_ffn_ref(x, L1_ffn_ln_gamma, L1_ffn_ln_beta, L1_ffn_fc1_q, L1_ffn_fc1_scales, L1_ffn_fc1_bias, L1_ffn_fc2_q, L1_ffn_fc2_scales, L1_ffn_fc2_bias), axis=-1)
    return x

_drawn_inputs = setup_inputs


def setup_inputs(seed=0):
    import zlib

    import numpy as np

    out = dict(_drawn_inputs(seed))
    spreads = {'L0_ffn_bfc_s': (0.0, 0.289),
     'L0_ffn_bproj_s': (0.0, 0.1),
     'L0_ffn_bfc': (0.0, 0.1),
     'L0_ffn_bproj': (0.0, 0.1),
     'L1_attn_bq': (0.0, 0.561),
     'L1_attn_bk': (0.0, 0.63),
     'L1_attn_bv': (0.0, 0.1),
     'L1_attn_bo': (0.0, 0.1),
     'L1_ffn_ln_gamma': (1.0, 0.2),
     'L1_ffn_ln_beta': (0.0, 0.1)}
    factors = {'L1_ffn_fc1_bias': 8.0, 'L1_ffn_fc2_bias': 64.0}
    for name, (base, spread) in spreads.items():
        noise = np.random.default_rng([zlib.crc32(name.encode()), seed]).standard_normal(out[name].shape)
        drawn = base * np.exp(spread * noise) if base else spread * noise
        out[name] = jnp.asarray(drawn.astype(out[name].dtype))
    for name, factor in factors.items():
        out[name] = (out[name] * factor).astype(out[name].dtype)
    return out
```

```python
from contextlib import ExitStack

import numpy as np

import concourse.bass as bass
from concourse import mybir

F32 = mybir.dt.float32
BF16 = mybir.dt.bfloat16
I32 = mybir.dt.int32
ALU = mybir.AluOpType
ACT = mybir.ActivationFunctionType
AX = mybir.AxisListType

P = 128
D = 128
B, S = 16, 256
N = B * S
NT = N // P
TPB = S // P
H0, DK0 = 16, 8
NS = 3
SLOTS = 6
KST = SLOTS * DK0
VW = 32
NE, HID = 8, 512
EXP = NE + 1
HC = HID // P
H1, DH1 = 16, 64
BLK = 512
NBLK = N // BLK
TBK = BLK // P
EPS = 1e-5
BIG = -1e30
UNITS = 12
GRP = 4
HG = 4
GATE_STEPS = 24


class Batch:

    def __init__(self, quad, rem):
        self.quad, self.rem = quad, rem

    def plus(self, k):
        r = self.rem + k
        return Batch(self.quad + r // 4, r % 4)

    def count(self, per, k=0):
        return self.quad * (4 * per) + (self.rem * per + k)

    def fixed(self):
        return isinstance(self.quad, int)

    def index(self):
        return 4 * self.quad + self.rem if self.fixed() else None

    def valid(self):
        return not self.fixed() or 0 <= self.index() < B


def over_blocks(eng, step):
    step(0)
    with eng.Fori(1, NBLK) as n:
        step(n)
    step(NBLK)


def has(n):
    return not isinstance(n, int) or 0 <= n < NBLK


def wait(eng, sem, value):
    if not isinstance(value, int) or value > 0:
        eng.wait_ge(sem, value)


def over_sequences(eng, first, step):
    for b in range(first, 2):
        step(Batch(b // 4, b % 4))
    loops = (B - 4) // 4
    with eng.Fori(0, loops) as i:
        for r in range(4):
            step(Batch(i, 2 + r).plus(0))
    for b in range(2 + 4 * loops, B + 1):
        step(Batch(b // 4, b % 4))


def build(nc, t):
    ctx = ExitStack()
    with ctx:
        def sb(name, shape, dt=F32):
            return ctx.enter_context(nc.sbuf_tensor(name, shape, dt))

        def sem(name):
            return ctx.enter_context(nc.semaphore(name))

        bank = [ctx.enter_context(nc.psum_tensor(f"bank{i}", [P, 512], F32)) for i in range(8)]
        X = sb("X", [P, NT, D])
        XT = sb("XT", [P, N])
        w1 = sb("w1", [P, EXP, HID])
        w2 = sb("w2", [P, EXP, HC, D])
        b1 = sb("b1", [P, EXP, HC])
        wq = sb("wq", [P, H1 * DH1])
        wk = sb("wk", [P, H1 * DH1])
        wv = sb("wv", [P, H1 * DH1])
        wo = sb("wo", [P, 8, D])
        bq = sb("bq", [P, 8])
        bk = sb("bk", [P, 8])
        bv = sb("bv", [P, H1 * DH1])
        bo = sb("bo", [P, D])
        a0 = sb("a0", [P, 6, D])
        rope = sb("rope", [P, 2, S])
        identf = sb("identf", [P, P])
        identb = sb("identb", [P, P], BF16)
        maskb = sb("maskb", [P, P], BF16)
        oneh = sb("oneh", [P, H0, P], BF16)
        dtab = sb("dtab", [P, S])
        rank = sb("rank", [P, NE])
        wr = sb("wr", [P, NE])
        arenaA = sb("arenaA", [P, 8192])
        arenaB = sb("arenaB", [P, 6144])
        ET = sb("ET", [P, UNITS, 512])
        arenaC = sb("arenaC", [P, 2 * TPB * H1 * DH1])
        Vc = arenaC[:, :].rearrange("p (r t h d) -> p r t h d", r=2, t=TPB, h=H1)

        def carve(arena):
            at = [0]

            def piece(words, dt=F32):
                at[0] += words
                ap = arena[:, at[0] - words:at[0]]
                return ap if dt is F32 else ap.bitcast(dt)
            return piece
        pieceC, pieceB = carve(arenaC), carve(arenaB)
        piece2 = carve(arenaA)
        gate = piece2(NT * 32).rearrange("p (n e) -> p n e", e=32)
        gateT = piece2(NBLK * P).rearrange("p (n t) -> p n t", t=P)
        probs, ge, wt, sel1, sel2, prb2 = (piece2(NT * NE).rearrange("p (n e) -> p n e", e=NE) for _ in range(6))
        gmax, gsum, grec, top1, top2, wmax, wmax2, tsum, trec = (piece2(NT) for _ in range(9))
        hid = arenaB[:, :].rearrange("p (r c t) -> p r c t", r=3, c=HC)
        gb = piece2(TBK * EXP).rearrange("p (n e) -> p n e", e=EXP)
        gTb = piece2(P)
        b2 = piece2(TBK * D).rearrange("p (i d) -> p i d", d=D)
        QK = arenaA[:, :].rearrange("p (r k c t) -> p r k c t", r=2, k=2, c=8)
        pieceB3 = carve(arenaB)
        attT = pieceB3(8 * S).rearrange("p (c t) -> p c t", c=8)
        num = pieceB3(8 * S).rearrange("p (c t) -> p c t", c=8)
        xt3 = pieceB3(2 * S).rearrange("p (r t) -> p r t", r=2)
        den3, rec3 = pieceB3(S), pieceB3(S)
        spread = pieceB3(8 * P).rearrange("p (c n) -> p c n", c=8)

        def unit3(j):
            half, k = divmod(j, 6)
            u = k // 2
            return half, k % 2, u, range(4 * half, 4 * half + 4) if u == 2 else range(4 * half + 2 * u, 4 * half + 2 * u + 2)

        def weights3(pair, odd, k):
            half, q = divmod(pair, 4)
            if k == 0:
                return ET[:, 6 * half + 2 * (q // 2) + odd, (q % 2) * S:(q % 2 + 1) * S]
            return ET[:, 6 * half + 4 + odd, q * P:(q + 1) * P]

        den_step = sem("den_step")
        spread_ready = sem("spread_ready")
        ones3 = sb("ones3", [P, HG, 32])
        pieceB4 = carve(arenaB)
        hT = pieceB4(2 * BLK).rearrange("p (r t) -> p r t", r=2)
        yT = pieceB4(HC * BLK).rearrange("p (r c t) -> p r c t", r=1, c=HC)
        xn2 = pieceB4(BLK).rearrange("p (t d) -> p t d", d=D)
        f1 = sb("f1", [P, HID])
        f2 = sb("f2", [P, HC, D])
        fb1 = sb("fb1", [P, HC])
        fb2 = sb("fb2", [P, D])
        gam = sb("gam", [P, 1])
        bet = sb("bet", [P, 1])
        pieceC4 = carve(arenaC)
        fq = pieceC4(2 * HID, I32).rearrange("p (a n) -> p a n", a=2)
        fs = pieceC4(2 * HID).rearrange("p (a n) -> p a n", a=2)
        fd = pieceC4(2 * HID).rearrange("p (a n) -> p a n", a=2)
        zt = pieceC4(BLK).rearrange("p (t d) -> p t d", d=D)
        yo = pieceC4(BLK).rearrange("p (t d) -> p t d", d=D)
        stack = arenaA[:, :].bitcast(BF16).rearrange("p (r k h t) -> p r k h t", r=4, k=2, h=8)
        xb = pieceC(2 * S).rearrange("p (r t) -> p r t", r=2)
        ropet = pieceC(4 * S).rearrange("p (k a t) -> p k a t", k=2, a=2)
        qk = pieceC(2 * S).rearrange("p (k t) -> p k t", k=2)
        rem1 = pieceC(2 * S).rearrange("p (k t) -> p k t", k=2)
        parts = pieceC(NS * S, BF16).rearrange("p (s k t) -> p s k t", s=NS, k=2)
        V0 = pieceB(4 * TPB * H0 * VW).rearrange("p (r t h d) -> p r t h d", r=4, t=TPB, h=H0)
        av0 = pieceB(2 * 512).rearrange("p (a n) -> p a n", a=2)
        nm = sb("nm", [P, TPB, H0])
        nmr = sb("nmr", [P, TPB, H0])
        nmp = sb("nmp", [P, TPB, 2, 4, H0], BF16)
        nmt = sb("nmt", [P, S], BF16)
        rden = sb("rden", [P, 2, H0, 1])
        att0 = pieceB(TPB * D).rearrange("p (t d) -> p t d", t=TPB)
        attT0 = pieceB(S)
        yres = sb("yres", [P, TBK, D])
        bst = sb("bst", [P, TBK, 6])
        mv = sb("mv", [P, TBK, 2])
        veps = sb("veps", [P, TBK])
        rstd = sb("rstd", [P, TBK])
        mhalf = sb("mhalf", [P, TBK])
        epsc = sb("epsc", [P, TBK])
        beat = sb("beat", [P, UNITS + 1])
        xn = sb("xn", [P, TBK, D])

        scr = nc.dram_tensor("scr", (2, 2, NS, DK0, H0, S), BF16).ap()

        w_in = sem("w_in")
        x_in = sem("x_in")
        xb_in = [sem("xb_in0"), sem("xb_in1")]
        w1_in = sem("w1_in")
        w3_in = sem("w3_in")
        w4_in = sem("w4_in")
        consts = sem("consts")
        proj_done = sem("proj_done")
        rope_read = sem("rope_read")
        rope_step = sem("rope_step")
        part1 = sem("part1")
        part_step = sem("part_step")
        scr_out = sem("scr_out")
        stack_in = [sem(f"stack_in{i}") for i in range(4)]
        v_copied = sem("v_copied")
        max_ready = sem("max_ready")
        max_taken = sem("max_taken")
        nm_step = sem("nm_step")
        nmt_ready = sem("nmt_ready")
        nmt_copied = sem("nmt_copied")
        sc_ready = sem("sc_ready")
        exp_done = sem("exp_done")
        sel_done = sem("sel_done")
        av_ready = sem("av_ready")
        rden_done = sem("rden_done")
        att_done = sem("att_done")
        av_copied = sem("av_copied")
        avT_ready = sem("avT_ready")
        attT_ready = sem("attT_ready")
        attT_copied = sem("attT_copied")
        wo_ready = sem("wo_ready")
        ln_step = sem("ln_step")
        rstd_step = sem("rstd_step")
        xn_done = sem("xn_done")
        xn_kept = sem("xn_kept")
        xT_ready = sem("xT_ready")
        xT_copied = sem("xT_copied")
        out_done = sem("out_done")
        route_ready = sem("route_ready")
        gate_step = sem("gate_step")
        gate_exp = sem("gate_exp")
        gateT_ready = sem("gateT_ready")
        gateT_copied = sem("gateT_copied")
        gTb_done = sem("gTb_done")
        gb_done = sem("gb_done")
        up_ready = sem("up_ready")
        gelu_done = sem("gelu_done")
        down_ready = sem("down_ready")
        acc_done = sem("acc_done")
        ln2_step = sem("ln2_step")
        rstd2_step = sem("rstd2_step")
        xn2_done = sem("xn2_done")
        xn2_kept = sem("xn2_kept")
        xT2_ready = sem("xT2_ready")
        xT2_copied = sem("xT2_copied")
        xt3_done = sem("xt3_done")
        ones_step = sem("ones_step")
        p3_ready = sem("p3_ready")
        relu_done = sem("relu_done")
        v3_done = sem("v3_done")
        s3_ready = sem("s3_ready")
        s3_taken = sem("s3_taken")
        num_ready = sem("num_ready")
        num_copied = sem("num_copied")
        att3_done = sem("att3_done")
        o3_ready = sem("o3_ready")
        ln3_step = sem("ln3_step")
        rstd3_step = sem("rstd3_step")
        xn3_done = sem("xn3_done")
        fq_in = sem("fq_in")
        deq_step = sem("deq_step")
        pre_step = sem("pre_step")
        prstd_step = sem("prstd_step")
        h_done = sem("h_done")
        doubled = sem("doubled")
        hT_ready = sem("hT_ready")
        hT_copied = sem("hT_copied")
        up4_ready = sem("up4_ready")
        silu_done = sem("silu_done")
        down4_ready = sem("down4_ready")
        z_step = sem("z_step")
        rstd4_step = sem("rstd4_step")
        xo_done = sem("xo_done")

        block = ctx.enter_context(nc.Block())

        @block.sync
        def _(sp):
            def load_block(b):
                if not b.valid():
                    return
                wait(sp, proj_done, b.plus(-2).count(3, 3) if not b.fixed() or b.index() >= 2 else 0)
                at = b.count(S)
                src = t["xT"][:, at:at + S] if b.fixed() else t["xT"][:, bass.ds(at, S)]
                sp.dma_start(xb[:, b.rem % 2, :], src).then_inc(xb_in[b.rem % 2], 16)

            def load_later():
                for dst, src in ((wr, t["wr"]), (rank, t["rank"]), (w1[:, 0, :], t["w1s"]), (w1[:, 1:, :], t["w1"].rearrange("e p n -> p e n")),
                                 (w2[:, 0], t["w2s"].rearrange("(c p) n -> p c n", p=P)),
                                 (b1[:, :, :], t["b1"])):
                    sp.dma_start(dst[:, :] if dst in (wr, rank) else dst, src).then_inc(w1_in, 16)
                for e in range(NE):
                    sp.dma_start(w2[:, e + 1], t["w2"][e].rearrange("(c p) n -> p c n", p=P)).then_inc(w1_in, 16)
                for dst, name in ((wq, "wq"), (wk, "wk"), (wv, "wv"), (bq, "bq"), (bk, "bk"), (dtab, "dtab")):
                    sp.dma_start(dst[:, :], t[name]).then_inc(w3_in, 16)
                sp.dma_start(wo[:, :, :], t["wo"].rearrange("(c p) n -> p c n", p=P)).then_inc(w3_in, 16)
                sp.dma_start(bv[:, :], t["bv"].partition_broadcast(P)).then_inc(w3_in, 16)
                sp.dma_start(bo[:, :], t["bo"].partition_broadcast(P)).then_inc(w3_in, 16)
                sp.dma_start(fb1[:, :], t["fb1"]).then_inc(w3_in, 16)
                sp.dma_start(fb2[:, :], t["fb2"].partition_broadcast(P)).then_inc(w3_in, 16)
                sp.dma_start(gam[:, :], t["gam"]).then_inc(w3_in, 16)
                sp.dma_start(bet[:, :], t["bet"]).then_inc(w3_in, 16)

            sp.dma_start(a0[:, :, :], t["a0"]).then_inc(w_in, 16)
            sp.dma_start(rope[:, :, :], t["rope"]).then_inc(w_in, 16)
            sp.dma_start(identf[:, :], t["identf"]).then_inc(w_in, 16)
            sp.dma_start(identb[:, :], t["identb"]).then_inc(w_in, 16)
            sp.dma_start(maskb[:, :], t["maskb"]).then_inc(w_in, 16)
            sp.dma_start(oneh[:, :, :], t["oneh"]).then_inc(w_in, 16)
            sp.dma_start(X[:, :, :], t["x"].rearrange("(n p) d -> p n d", p=P)).then_inc(x_in, 16)

            def step(b):
                n2 = b.plus(2)
                load_block(n2)
                if b.fixed() and b.index() == 1:
                    load_later()
                if n2.valid():
                    slot = n2.rem % 2
                    wait(sp, part_step, n2.count(3, 3))
                    for k in range(2):
                        for s in range(NS):
                            if (k, s) == (1, NS - 1):
                                wait(sp, sc_ready, b.plus(-2).count(UNITS, UNITS) if not b.fixed() or b.index() >= 2 else 0)
                            at = s if k == 0 else NS - 1 - s
                            sp.dma_start(scr[slot, k, at].rearrange("d h t -> h d t"),
                                         parts[:, s, k, :]).then_inc(scr_out, 16)
                    wait(sp, scr_out, n2.count(96, 96))
                    for k in range(2):
                        src = scr[slot, k].rearrange("s d (q h) t -> q (s d) h t", q=2)
                        for q in range(2):
                            row = 64 * q
                            for n in (3, 2, 1):
                                f = 0 if k == 0 else NS - n
                                sp.dma_start(stack[row:row + n * DK0, n2.rem, k, :, :],
                                             src[q, f * DK0:(f + n) * DK0]).then_inc(stack_in[n2.rem], 16)
                                row += n * DK0
            over_sequences(sp, -2, step)
            sp.wait_ge(xT_copied, B)
            sp.dma_start(b2, t["b2"]).then_inc(w1_in, 16)
            sp.dma_start(fq[:, 0, :], t["fc1_q"]).then_inc(fq_in, 16)
            sp.dma_start(fq[:, 1, :].rearrange("p (c n) -> p c n", c=HC),
                         t["fc2_q"].rearrange("(c p) n -> p c n", p=P)).then_inc(fq_in, 16)
            sp.dma_start(fs[:, 0, :], t["fc1_scales"].partition_broadcast(P)).then_inc(fq_in, 16)
            sp.dma_start(fs[:, 1, :], t["fc2_scales"].partition_broadcast(P)).then_inc(fq_in, 16)

            sp.wait_ge(acc_done, NBLK * EXP)
            sp.dma_start(spread, t["spread"]).then_inc(w3_in, 16)

            def store(n):
                if has(n):
                    sp.wait_ge(xo_done, n + 1)
                    out = t["out"].rearrange("(n p) d -> p n d", p=P)
                    out = out[:, n * TBK:(n + 1) * TBK, :] if isinstance(n, int) else out[:, bass.ds(n * TBK, TBK), :]
                    sp.dma_start(out, xn[:, :, :]).then_inc(out_done, 16)
            over_blocks(sp, store)
            sp.wait_ge(out_done, NBLK * 16)

        @block.tensor
        def _(pe):
            def head_rows(h):
                lo = 64 * (h // 8)
                return slice(lo, lo + KST), h % 8

            def project(b):
                x = xb[:, b.rem % 2, :]
                if b.fixed():
                    wait(pe, v_copied, b.count(1, 0))
                    wait(pe, rope_read, b.count(2, 0))
                pe.wait_ge(xb_in[b.rem % 2], (b.quad * 2 + b.rem // 2) * 16 + 16)
                wait(pe, nmt_copied, b.count(1, -1))
                nc.tensor.matmul(bank[6][:, 0:S], a0[:, 0, :], x, start=True, stop=True)
                nc.tensor.matmul(bank[6][:, S:2 * S], a0[:, 1, :], x, start=True, stop=True).then_inc(proj_done, 1)
                wait(pe, xT_copied, b.count(1, -3))
                nc.tensor.matmul(bank[7][:, 0:S], a0[:, 2, :], x, start=True, stop=True)
                nc.tensor.matmul(bank[7][:, S:2 * S], a0[:, 3, :], x, start=True, stop=True).then_inc(proj_done, 1)
                pe.wait_ge(rope_read, b.count(2, 1))
                for i in range(TPB):
                    last = nc.tensor.matmul(bank[6][:, i * D:(i + 1) * D], x[:, i * P:(i + 1) * P], a0[:, 4, :],
                                            start=True, stop=True)
                last.then_inc(proj_done, 1)

            def max_unit(b, j):
                if j == 0:
                    pe.wait_ge(stack_in[b.rem], (b.quad + 1) * 192)
                g, u = divmod(j, 3)
                ps = bank[2 + j % 2]
                wait(pe, max_taken, b.count(UNITS, j - 1))
                heads = range(4 * g, 4 * g + 4) if u == 0 else range(4 * g + 2 * u - 2, 4 * g + 2 * u)
                keys = P if u == 0 else S
                q0 = 0 if u == 0 else P
                for n, h in enumerate(heads):
                    rows, hp = head_rows(h)
                    nc.tensor.matmul(ps[:, n * keys:(n + 1) * keys], stack[rows, b.rem, 0, hp, q0:q0 + P],
                                     stack[rows, b.rem, 1, hp, 0:keys], start=(n == 0), stop=False,
                                     skip_group_check=True)
                diag = ps[:, :].rearrange("p (h k) -> p h k", k=keys)[:, :, keys - P:keys]
                nc.tensor.matmul(diag, identb[:, :], maskb[:, None, :].to_broadcast([P, len(heads), P]),
                                 start=False, stop=True, skip_group_check=True).then_inc(max_ready, 1)

            def score_unit(b, j):
                if j == 0:
                    pe.wait_ge(stack_in[b.rem], (b.quad + 1) * 192)
                    pe.wait_ge(nmt_copied, b.count(1, 1))
                g, u = divmod(j, 3)
                ps = bank[j % 2]
                wait(pe, exp_done, b.count(UNITS, j - 1))
                heads = range(4 * g, 4 * g + 4) if u == 2 else range(4 * g + 2 * u, 4 * g + 2 * u + 2)
                k0 = P if u == 2 else 0
                n_q = S - k0
                for n, h in enumerate(heads):
                    rows, hp = head_rows(h)
                    nc.tensor.matmul(ps[:, n * n_q:(n + 1) * n_q], stack[rows, b.rem, 1, hp, k0:k0 + P],
                                     stack[rows, b.rem, 0, hp, k0:S], start=(n == 0), stop=False,
                                     skip_group_check=True)
                    last = nc.tensor.matmul(ps[:, n * n_q:(n + 1) * n_q], oneh[:, h, :], nmt[:, k0:S],
                                            start=False, stop=True, skip_group_check=True)
                last.then_inc(sc_ready, 1)

            def weigh_values(b, g):
                pe.wait_ge(sel_done, b.count(UNITS, 3 * g + 3))
                if g == 0:
                    pe.wait_ge(v_copied, b.count(1, 1))
                if g % 2 == 0:
                    wait(pe, av_copied, b.count(2, g // 2 - 1))
                out = bank[4 + g // 2][:, (g % 2) * S:(g % 2 + 1) * S]
                v = V0[:, b.rem]
                for r in range(HG):
                    h = HG * g + r
                    q = slice(VW * r, VW * (r + 1))
                    nc.tensor.matmul(out[q, :], v[:, 0, h, :], ET[:, 3 * g + r // 2, (r % 2) * S:(r % 2 + 1) * S],
                                     start=(g % 2 == 0), stop=False, skip_group_check=True)
                for r in range(HG):
                    h = HG * g + r
                    q = slice(VW * r, VW * (r + 1))
                    last = nc.tensor.matmul(out[q, P:S], v[:, 1, h, :], ET[:, 3 * g + 2, r * P:(r + 1) * P],
                                            start=False, stop=True, skip_group_check=True)
                last.then_inc(av_ready, 1)

            def transpose_values(b, a):
                pe.wait_ge(av_copied, b.count(2, a + 1))
                if a == 0:
                    pe.wait_ge(rope_read, b.plus(3).count(2, 2) if b.plus(3).valid() else 2 * B)
                else:
                    pe.wait_ge(v_copied, b.plus(3).count(1, 1) if b.plus(3).valid() else B)
                for g in range(2):
                    for i in range(TPB):
                        at = (i * 2 + g) * P
                        last = nc.tensor.transpose(bank[7 - a][:, at:at + P],
                                                   av0[:, a, g * S + i * P:g * S + (i + 1) * P], identf[:, :])
                last.then_inc(avT_ready, 1)

            def transpose_max(b):
                pe.wait_ge(nm_step, b.count(5, 5))
                wait(pe, ln_step, b.count(5, -9))
                if b.fixed():
                    wait(pe, v_copied, min(b.index() + 2, B))
                ps = bank[6][:, 0:S // 2].bitcast(BF16)
                for i in range(TPB):
                    last = nc.tensor.transpose(ps[:, i * P:(i + 1) * P],
                                               nmp[:, i].rearrange("p a s h -> p (a s h)"), identb[:, :])
                last.then_inc(nmt_ready, 1)

            def transpose_att(b):
                pe.wait_ge(att_done, b.count(2, 2))
                for i in range(TPB):
                    last = nc.tensor.transpose(bank[7][:, i * P:(i + 1) * P], att0[:, i, :], identf[:, :])
                last.then_inc(attT_ready, 1)

            def out_project(b):
                pe.wait_ge(attT_copied, b.count(1, 1))
                for i in range(TPB):
                    last = nc.tensor.matmul(bank[6][:, i * D:(i + 1) * D], attT0[:, i * P:(i + 1) * P], a0[:, 5, :],
                                            start=True, stop=True)
                last.then_inc(wo_ready, 1)

            def transpose_norm(b):
                pe.wait_ge(xn_done, b.count(1, 1))
                for i in range(TPB):
                    last = nc.tensor.transpose(bank[7][:, i * P:(i + 1) * P], xn[:, i, :], identf[:, :])
                last.then_inc(xT_ready, 1)

            def step(b):
                now, nxt, nxt2, prev = b, b.plus(1), b.plus(2), b.plus(-1)
                done = {"s": 0, "m": 0}

                def scores(n):
                    for _ in range(n):
                        if now.valid():
                            score_unit(now, done["s"])
                        done["s"] += 1

                def maxima(n):
                    for _ in range(n):
                        if nxt.valid():
                            max_unit(nxt, done["m"])
                        done["m"] += 1

                scores(3)
                if nxt2.valid():
                    project(nxt2)
                scores(1)
                maxima(2)
                if prev.valid():
                    transpose_values(prev, 0)
                scores(1)
                maxima(1)
                if prev.valid():
                    transpose_values(prev, 1)
                scores(1)
                maxima(1)
                if now.valid():
                    weigh_values(now, 0)
                scores(1)
                maxima(2)
                if prev.valid():
                    transpose_att(prev)
                scores(1)
                maxima(1)
                if prev.valid():
                    out_project(prev)
                scores(1)
                maxima(1)
                if now.valid():
                    weigh_values(now, 1)
                scores(1)
                maxima(2)
                scores(1)
                maxima(1)
                if prev.valid():
                    transpose_norm(prev)
                scores(1)
                maxima(1)
                if now.valid():
                    weigh_values(now, 2)
                if nxt.valid():
                    transpose_max(nxt)
                if now.valid():
                    weigh_values(now, 3)

            pe.wait_ge(w_in, 96)
            over_sequences(pe, -2, step)

            pe.wait_ge(xT_copied, B)
            pe.wait_ge(exp_done, B * UNITS)
            pe.wait_ge(max_taken, B * UNITS)
            pe.wait_ge(av_copied, 2 * B)
            pe.wait_ge(ln_step, 5 * B)
            pe.wait_ge(w1_in, 15 * 16)
            for i in range(NT):
                last = nc.tensor.matmul(bank[7][:, i * NE:(i + 1) * NE], XT[:, i * P:(i + 1) * P], wr[:, :],
                                        start=True, stop=True)
            last.then_inc(route_ready, 1)
            pe.wait_ge(gate_step, GATE_STEPS)
            for n in range(NBLK):
                wait(pe, gateT_copied, n - 1)
                nc.tensor.transpose(bank[6 + n % 2][:, 0:P], gate[:, n * TBK:(n + 1) * TBK, :]
                                    .rearrange("p n e -> p (n e)"), identf[:, :]).then_inc(gateT_ready, 1)
            pe.wait_ge(gateT_copied, NBLK)

            def up(n, e):
                x = XT[:, n * BLK:(n + 1) * BLK] if isinstance(n, int) else XT[:, bass.ds(n * BLK, BLK)]
                for c in range(HC):
                    wait(pe, gelu_done, n * (EXP * HC) + (e * HC + c - 3))
                    nc.tensor.matmul(bank[c][:, :], w1[:, e, c * P:(c + 1) * P], x, start=True, stop=True).then_inc(up_ready, 1)

            def down(n, e):
                pe.wait_ge(gelu_done, n * (EXP * HC) + (e * HC + HC))
                wait(pe, acc_done, n * EXP + (e - 2))
                ps = bank[4 + e % 3]
                if e == 0:
                    pe.wait_ge(gTb_done, n + 1)
                for i in range(TBK):
                    out = ps[:, i * D:(i + 1) * D]
                    if e == 0:
                        nc.tensor.matmul(out, gTb[:, :], b2[:, i, :], start=True, stop=False, skip_group_check=True)
                    for c in range(HC):
                        last = nc.tensor.matmul(out, hid[:, e % 3, c, i * P:(i + 1) * P], w2[:, e, c, :],
                                                start=(e > 0 and c == 0), stop=(c == HC - 1), skip_group_check=True)
                last.then_inc(down_ready, 1)

            def transpose_block(n):
                pe.wait_ge(xn2_done, n + 1)
                wait(pe, xT2_copied, n)
                for i in range(TBK):
                    last = nc.tensor.transpose(bank[7][:, i * P:(i + 1) * P], xn[:, i, :], identf[:, :])
                last.then_inc(xT2_ready, 1)

            def moe(n):
                if has(n):
                    up(n, 0)
                for e in range(1, EXP):
                    if has(n):
                        up(n, e)
                    if e == 3 and has(n - 1):
                        transpose_block(n - 1)
                    if has(n):
                        down(n, e - 1)
                if has(n):
                    down(n, EXP - 1)
            over_blocks(pe, moe)

            pe.wait_ge(xT2_copied, NBLK)
            pe.wait_ge(acc_done, NBLK * EXP)
            pe.wait_ge(w3_in, 14 * 16)

            def project3(b, j):
                if j == 0:
                    pe.wait_ge(xt3_done, b.count(1, 1))
                if j < 10:
                    wait(pe, relu_done, b.count(16, 2 * (j - 1)) if j >= 2 else 0)
                if j < 2:
                    wait(pe, v3_done, b.count(4, -1 + j))
                if j >= 10:
                    pe.wait_ge(v3_done, b.count(4, j - 9))
                ps = bank[j % 2]
                x = xt3[:, b.rem % 2, :]
                if j < 8:
                    nc.tensor.matmul(ps[:, 0:S], wq[:, j * P:(j + 1) * P], x, start=True, stop=True)
                    last = nc.tensor.matmul(ps[:, S:2 * S], wk[:, j * P:(j + 1) * P], x, start=True, stop=True)
                else:
                    i, half = divmod(j - 8, 2)
                    last = nc.tensor.matmul(ps[:, :], x[:, i * P:(i + 1) * P], wv[:, half * 512:(half + 1) * 512],
                                            start=True, stop=True)
                last.then_inc(p3_ready, 1)

            def scores3(b, j):
                half, odd, u, pairs = unit3(j)
                pe.wait_ge(relu_done, b.count(16, 2 * pairs[-1] + 2))
                wait(pe, s3_taken, b.count(UNITS, j - 1))
                ps = bank[2 + j % 2]
                k0 = P if u == 2 else 0
                n_q = S - k0
                rows = slice(DH1 * odd, DH1 * (odd + 1))
                for n, pair in enumerate(pairs):
                    last = nc.tensor.matmul(ps[:, n * n_q:(n + 1) * n_q], QK[rows, b.rem % 2, 1, pair, k0:k0 + P],
                                            QK[rows, b.rem % 2, 0, pair, k0:S], start=True, stop=True)
                last.then_inc(s3_ready, 1)

            def weigh3(b, g):
                pe.wait_ge(s3_taken, b.count(UNITS, 6 * (g // 2) + 6))
                if g == 0:
                    pe.wait_ge(v3_done, b.count(4, 4))
                wait(pe, num_copied, b.count(HG, g))
                if g == 0:
                    wait(pe, den_step, b.count(2, -1))
                for what in range(2):
                    for k in range(TPB):
                        for r in range(HG):
                            h = HG * g + r
                            w = weights3(2 * g + r // 2, r % 2, k)
                            if what == 0:
                                rows = slice(DH1 * (r % 2), DH1 * (r % 2 + 1))
                                last = nc.tensor.matmul(bank[4][rows, (r // 2) * S + k * P:(r // 2 + 1) * S],
                                                        Vc[:, b.rem % 2, k, h, :], w, start=(k == 0 and r < 2),
                                                        stop=(k == 1), skip_group_check=True)
                            else:
                                last = nc.tensor.matmul(bank[5][32 * r:32 * r + 32, k * P:S], ones3[:, g, :], w,
                                                        start=(k == 0 and g == 0), stop=(k == 1 and g == HG - 1),
                                                        skip_group_check=True)
                    last.then_inc(num_ready, 1)

            def spread3(b, v):
                if v == 0:
                    pe.wait_ge(den_step, b.count(2, 2))
                    wait(pe, ln3_step, b.count(6, -5))
                wait(pe, att3_done, b.count(HG, v - 1))
                for i in range(2):
                    last = nc.tensor.matmul(bank[6 + v % 2][:, i * S:(i + 1) * S], spread[:, 2 * v + i, :], rec3,
                                            start=True, stop=True)
                last.then_inc(spread_ready, 1)

            def out_project3(b):
                pe.wait_ge(att3_done, b.count(HG, HG))
                for i in range(TPB):
                    for c in range(8):
                        last = nc.tensor.matmul(bank[6][:, i * D:(i + 1) * D], attT[:, c, i * P:(i + 1) * P],
                                                wo[:, c, :], start=(c == 0), stop=(c == 7), skip_group_check=True)
                last.then_inc(o3_ready, 1)

            def cosformer(b):
                nxt, prev = b.plus(1), b.plus(-1)
                if prev.valid():
                    weigh3(prev, 2)
                for j in range(UNITS):
                    if nxt.valid():
                        project3(nxt, j)
                    if b.valid():
                        scores3(b, j)
                    if j == 0 and prev.valid():
                        weigh3(prev, 3)
                    if j in (2, 3, 4, 5) and prev.valid():
                        spread3(prev, j - 2)
                    if j == 6 and prev.valid():
                        out_project3(prev)
                    if j in (6, 8) and b.valid():
                        weigh3(b, j // 2 - 3)
            over_sequences(pe, -1, cosformer)

            pe.wait_ge(ln3_step, 6 * B)
            pe.wait_ge(deq_step, 4)

            def transpose4(n):
                pe.wait_ge(h_done, n + 1)
                wait(pe, hT_copied, n)
                for i in range(TBK):
                    last = nc.tensor.transpose(bank[7][:, i * P:(i + 1) * P], xn2[:, i, :], identf[:, :])
                last.then_inc(hT_ready, 1)

            def ffn(n):
                if has(n):
                    transpose4(n)
                    pe.wait_ge(hT_copied, n + 1)
                    for c in range(HC):
                        wait(pe, silu_done, n * HC + (c - 3))
                        nc.tensor.matmul(bank[c][:, :], f1[:, c * P:(c + 1) * P], hT[:, 0, :],
                                         start=True, stop=True).then_inc(up4_ready, 1)
                    pe.wait_ge(silu_done, n * HC + HC)
                    wait(pe, z_step, n * 10 - 9)
                    for i in range(TBK):
                        for c in range(HC):
                            last = nc.tensor.matmul(bank[4][:, i * D:(i + 1) * D], yT[:, 0, c, i * P:(i + 1) * P],
                                                    f2[:, c, :], start=(c == 0), stop=(c == HC - 1))
                    last.then_inc(down4_ready, 1)
            over_blocks(pe, ffn)

        @block.vector
        def _(dve):
            nc.vector.memset(V0[:, :, :, :, DK0 + 1:VW], 0.0)
            nc.vector.memset(V0[:, :, :, :, DK0:DK0 + 1], 1.0)
            nc.vector.memset(nmp[:, :, :, :, :], 0.0)
            nc.vector.memset(ones3[:, :, :], 0.0).then_inc(ones_step, 1)
            dve.wait_ge(ones_step, 1)
            for g in range(HG):
                nc.vector.memset(ones3[:, g, g:g + 1], 1.0)
            nc.vector.memset(epsc[:, :], EPS)
            nc.vector.memset(mhalf[:, :], -0.5).then_inc(consts, 1)

            def pass_on():
                nc.vector.tensor_copy(beat[:, UNITS:UNITS + 1], mhalf[:, 0:1])

            def rotate(b):
                for k in range(2):
                    dve.wait_ge(proj_done, b.count(3, k + 1))
                    nc.vector.tensor_tensor(ropet[:, k], bank[6 + k][:, :].rearrange("p (a t) -> p a t", a=2),
                                            rope[:, :, :], op=ALU.mult).then_inc(rope_read, 1)
                dve.wait_ge(rope_read, b.count(2, 2))
                wait(dve, part_step, b.count(3, 0))
                nc.vector.tensor_tensor(qk[:, :, :], ropet[:, :, 0, :], ropet[:, :, 1, :], op=ALU.add).then_inc(rope_step, 1)
                dve.wait_ge(rope_step, b.count(1, 1))
                wait(dve, scr_out, b.count(96, 0))
                nc.vector.tensor_copy(parts[:, 0], qk[:, :, :]).then_inc(part1, 1)

            def take_max(b, j):
                g, u = divmod(j, 3)
                dve.wait_ge(max_ready, b.count(UNITS, j + 1))
                if j == 0:
                    wait(dve, nm_step, b.count(5, 0))
                if u == 0:
                    out, keys = nm[:, 0, 4 * g:4 * g + 4], P
                else:
                    out, keys = nm[:, 1, 4 * g + 2 * u - 2:4 * g + 2 * u], S
                nc.vector.tensor_reduce(out, bank[2 + j % 2][:, :].rearrange("p (h k) -> p h k", k=keys),
                                        axis=AX.X, op=ALU.max, negate=True).then_inc(max_taken, 1)

            def split_max(b):
                dve.wait_ge(max_taken, b.count(UNITS, UNITS))
                wait(dve, nmt_ready, b.count(1, 0))
                two = [P, TPB, 2, H0]
                nc.vector.tensor_copy(nmp[:, :, :, 0, :], nm[:, :, None, :].to_broadcast(two)).then_inc(nm_step, 1)
                dve.wait_ge(nm_step, b.count(5, 1))
                nc.vector.tensor_tensor(nmr[:, :, :], nm[:, :, :], nmp[:, :, 0, 0, :], op=ALU.subtract).then_inc(nm_step, 1)
                dve.wait_ge(nm_step, b.count(5, 2))
                nc.vector.tensor_copy(nmp[:, :, :, 1, :], nmr[:, :, None, :].to_broadcast(two)).then_inc(nm_step, 1)
                dve.wait_ge(nm_step, b.count(5, 3))
                nc.vector.tensor_tensor(nm[:, :, :], nmr[:, :, :], nmp[:, :, 0, 1, :], op=ALU.subtract).then_inc(nm_step, 1)
                dve.wait_ge(nm_step, b.count(5, 4))
                nc.vector.tensor_copy(nmp[:, :, :, 2, :], nm[:, :, None, :].to_broadcast(two)).then_inc(nm_step, 1)

            def normalise(b, a):
                dve.wait_ge(avT_ready, b.count(2, a + 1))
                av = bank[7 - a][:, :].rearrange("p (n d) -> p n d", d=VW)
                nc.vector.reciprocal(rden[:, a], av[:, :, DK0:DK0 + 1]).then_inc(rden_done, 1)
                dve.wait_ge(rden_done, b.count(2, a + 1))
                if a == 0:
                    wait(dve, attT_ready, b.count(1, 0))
                half = att0[:, :, a * D // 2:(a + 1) * D // 2].rearrange("p t (h d) -> p t h d", d=DK0)
                nc.vector.tensor_tensor(half, av[:, :, 0:DK0].rearrange("p (t h) d -> p t h d", t=TPB),
                                        rden[:, a].rearrange("p (t h) d -> p t h d", t=TPB)
                                        .to_broadcast([P, TPB, H0 // 2, DK0]), op=ALU.mult).then_inc(att_done, 1)

            def residual(b):
                dve.wait_ge(wo_ready, b.count(1, 1))
                at = b.count(TPB)
                x = X[:, at:at + TPB, :] if b.fixed() else X[:, bass.ds(at, TPB), :]
                nc.vector.tensor_tensor(yres[:, 0:TPB, :], bank[6][:, 0:TPB * D].rearrange("p (t d) -> p t d", d=D),
                                        x, op=ALU.add).then_inc(ln_step, 1)
                dve.wait_ge(ln_step, b.count(5, 1))
                for i in range(TPB):
                    nc.vector.bn_stats(bst[:, i, :], yres[:, i, :]).then_inc(ln_step, 1)
                dve.wait_ge(ln_step, b.count(5, 3))
                pass_on()
                for i in range(TPB):
                    nc.vector.bn_aggr(mv[:, i, :], bst[:, i, :]).then_inc(ln_step, 1)

            def apply_norm(b):
                dve.wait_ge(rstd_step, b.count(2, 2))
                wait(dve, xT_ready, b.count(1, 0))
                wait(dve, xn_kept, b.count(1, 0))
                for i in range(TPB):
                    last = nc.vector.tensor_scalar(xn[:, i, :], yres[:, i, :], mv[:, i, 0:1], rstd[:, i:i + 1],
                                                   ALU.subtract, ALU.mult)
                last.then_inc(xn_done, 1)

            def step(b):
                nxt, nxt2, prev = b.plus(1), b.plus(2), b.plus(-1)
                if nxt2.valid():
                    rotate(nxt2)
                for j in range(UNITS):
                    if j in (1, 3) and prev.valid():
                        normalise(prev, j // 2)
                    if nxt.valid():
                        take_max(nxt, j)
                    if j == 6 and prev.valid():
                        residual(prev)
                    if j == 8 and prev.valid():
                        apply_norm(prev)
                if nxt.valid():
                    split_max(nxt)

            dve.wait_ge(w_in, 96)
            dve.wait_ge(x_in, 16)
            over_sequences(dve, -2, step)

            steps = [0]

            def gated(ins):
                steps[0] += 1
                ins.then_inc(gate_step, 1)
                dve.wait_ge(gate_step, steps[0])

            def every(ap):
                return ap.rearrange("p (n o) -> p n o", o=1).to_broadcast([P, NT, NE])

            logits = bank[7][:, 0:NT * NE].rearrange("p (n e) -> p n e", e=NE)
            ranks = rank[:, None, :].to_broadcast([P, NT, NE])
            gated(nc.vector.memset(gate[:, :, :], 0.0))
            gated(nc.vector.memset(gate[:, :, 0:1], 1.0))
            dve.wait_ge(route_ready, 1)
            gated(nc.vector.tensor_reduce(gmax, logits, axis=AX.X, op=ALU.max))
            gated(nc.vector.tensor_tensor(probs, logits, every(gmax), op=ALU.subtract))
            dve.wait_ge(gate_exp, 1)
            gated(nc.vector.tensor_reduce(gsum, prb2, axis=AX.X, op=ALU.add))
            gated(nc.vector.reciprocal(grec, gsum))
            gated(nc.vector.tensor_tensor(probs, prb2, every(grec), op=ALU.mult))
            for p, top, wm, sel in ((probs, top1, wmax, sel1), (prb2, top2, wmax2, sel2)):
                gated(nc.vector.tensor_reduce(top, p, axis=AX.X, op=ALU.max))
                gated(nc.vector.tensor_tensor(ge, p, every(top), op=ALU.is_ge))
                gated(nc.vector.tensor_tensor(wt, ge, ranks, op=ALU.mult))
                gated(nc.vector.tensor_reduce(wm, wt, axis=AX.X, op=ALU.max))
                gated(nc.vector.tensor_tensor(sel, wt, every(wm), op=ALU.is_equal))
                if sel is sel1:
                    gated(nc.vector.scalar_tensor_tensor(prb2, sel1, -4.0, probs, op0=ALU.mult, op1=ALU.add))
            gated(nc.vector.tensor_tensor(tsum, top1, top2, op=ALU.add))
            gated(nc.vector.reciprocal(trec, tsum))
            gated(nc.vector.tensor_tensor(ge, sel1, every(top1), op=ALU.mult))
            gated(nc.vector.tensor_tensor(wt, sel2, every(top2), op=ALU.mult))
            gated(nc.vector.tensor_tensor(probs, ge, wt, op=ALU.add))
            gated(nc.vector.tensor_tensor(gate[:, :, 1:EXP], probs, every(trec), op=ALU.mult))
            assert steps[0] == GATE_STEPS

            def block_of(n):
                return X[:, n * TBK:(n + 1) * TBK, :] if isinstance(n, int) else X[:, bass.ds(n * TBK, TBK), :]

            def accumulate(n, e):
                dve.wait_ge(down_ready, n * EXP + (e + 1))
                ps = bank[4 + e % 3]
                if e == 0:
                    wait(dve, xn2_done, n)
                    nc.vector.tensor_tensor(yres[:, :, :], ps[:, :].rearrange("p (t d) -> p t d", d=D), block_of(n),
                                            op=ALU.add).then_inc(acc_done, 1)
                    return
                dve.wait_ge(acc_done, n * EXP + e)
                for i in range(TBK):
                    last = nc.vector.scalar_tensor_tensor(yres[:, i, :], ps[:, i * D:(i + 1) * D], gb[:, i, e:e + 1],
                                                          yres[:, i, :], op0=ALU.mult, op1=ALU.add)
                last.then_inc(acc_done, 1)

            def moe(n):
                if not has(n):
                    return
                wait(dve, acc_done, n * EXP)
                g = gate[:, n * TBK:(n + 1) * TBK, 0:EXP] if isinstance(n, int) else gate[:, bass.ds(n * TBK, TBK), 0:EXP]
                nc.vector.tensor_copy(gb[:, :, :], g).then_inc(gb_done, 1)
                dve.wait_ge(gb_done, n + 1)
                for e in range(EXP):
                    accumulate(n, e)
                dve.wait_ge(acc_done, n * EXP + EXP)
                for i in range(TBK):
                    nc.vector.bn_stats(bst[:, i, :], yres[:, i, :]).then_inc(ln2_step, 1)
                dve.wait_ge(ln2_step, n * 8 + 4)
                pass_on()
                for i in range(TBK):
                    nc.vector.bn_aggr(mv[:, i, :], bst[:, i, :]).then_inc(ln2_step, 1)
                dve.wait_ge(rstd2_step, n * 2 + 2)
                wait(dve, xT2_ready, n)
                wait(dve, xn2_kept, n)
                for i in range(TBK):
                    last = nc.vector.tensor_scalar(xn[:, i, :], yres[:, i, :], mv[:, i, 0:1], rstd[:, i:i + 1],
                                                   ALU.subtract, ALU.mult)
                last.then_inc(xn2_done, 1)
            dve.wait_ge(xn_kept, B)
            over_blocks(dve, moe)

            dve.wait_ge(w3_in, 14 * 16)
            dve.wait_ge(deq_step, 4)
            dve.wait_ge(xn2_kept, NBLK)

            def add_bias3(b, u):
                dve.wait_ge(p3_ready, b.count(UNITS, u + 9))
                if u == 0:
                    wait(dve, num_ready, b.count(8, -8))
                i, half = divmod(u, 2)
                out = Vc[:, b.rem % 2, i, half * 8:(half + 1) * 8, :].rearrange("p h d -> p (h d)")
                nc.vector.tensor_tensor(out, bank[u % 2][:, :], bv[:, half * 512:(half + 1) * 512],
                                        op=ALU.add).then_inc(v3_done, 1)

            def weight3(b, j):
                dve.wait_ge(s3_ready, b.count(UNITS, j + 1))
                half, odd, u, pairs = unit3(j)
                if j % 6 == 0:
                    wait(dve, num_ready, b.count(8, 4 * half - 4))
                if u == 2:
                    shape, tab = [P, 4, P], dtab[:, 0:P]
                else:
                    shape, tab = [P, 2, S], dtab[:, :]
                nc.vector.tensor_tensor(ET[:, j, :].rearrange("p (h q) -> p h q", h=shape[1]),
                                        bank[2 + j % 2][:, :].rearrange("p (h q) -> p h q", h=shape[1]),
                                        tab[:, None, :].to_broadcast(shape), op=ALU.mult).then_inc(s3_taken, 1)

            def divide3(b, g):
                dve.wait_ge(num_copied, b.count(HG, g + 1))
                dve.wait_ge(spread_ready, b.count(HG, g + 1))
                if g == 0:
                    wait(dve, o3_ready, b.count(1, 0))
                nc.vector.tensor_tensor(attT[:, 2 * g:2 * g + 2, :].rearrange("p c t -> p (c t)"),
                                        num[:, 2 * g:2 * g + 2, :].rearrange("p c t -> p (c t)"), bank[6 + g % 2][:, :],
                                        op=ALU.mult).then_inc(att3_done, 1)

            def invert3(b):
                dve.wait_ge(num_ready, b.count(8, 8))
                wait(dve, spread_ready, b.count(HG, 0))
                nc.vector.tensor_scalar(den3, bank[5][:, 0:S], 1e-6, None, ALU.max).then_inc(den_step, 1)
                dve.wait_ge(den_step, b.count(2, 1))
                nc.vector.reciprocal(rec3, den3).then_inc(den_step, 1)

            def residual3(b):
                dve.wait_ge(o3_ready, b.count(1, 1))
                at = b.count(TPB)
                x = X[:, at:at + TPB, :] if b.fixed() else X[:, bass.ds(at, TPB), :]
                wait(dve, xn3_done, b.count(1, 0))
                nc.vector.tensor_tensor(yres[:, 0:TPB, :], bank[6][:, 0:TPB * D].rearrange("p (t d) -> p t d", d=D),
                                        x, op=ALU.add).then_inc(ln3_step, 1)
                dve.wait_ge(ln3_step, b.count(6, 1))
                nc.vector.tensor_tensor(yres[:, 0:TPB, :], yres[:, 0:TPB, :],
                                        bo[:, None, :].to_broadcast([P, TPB, D]), op=ALU.add).then_inc(ln3_step, 1)
                dve.wait_ge(ln3_step, b.count(6, 2))
                for i in range(TPB):
                    nc.vector.bn_stats(bst[:, i, :], yres[:, i, :]).then_inc(ln3_step, 1)
                dve.wait_ge(ln3_step, b.count(6, 4))
                pass_on()
                for i in range(TPB):
                    nc.vector.bn_aggr(mv[:, i, :], bst[:, i, :]).then_inc(ln3_step, 1)

            def apply3(b):
                dve.wait_ge(rstd3_step, b.count(2, 2))
                at = b.count(TPB)
                for i in range(TPB):
                    x = X[:, at + i, :] if b.fixed() else X[:, bass.ds(at + i, 1), :].rearrange("p o d -> p (o d)")
                    last = nc.vector.tensor_scalar(x, yres[:, i, :], mv[:, i, 0:1], rstd[:, i:i + 1],
                                                   ALU.subtract, ALU.mult)
                last.then_inc(xn3_done, 1)

            def cosformer(b):
                nxt, prev = b.plus(1), b.plus(-1)
                for j in range(UNITS):
                    if j == 8 and prev.valid():
                        residual3(prev)
                    if j == 10 and prev.valid():
                        apply3(prev)
                    if b.valid():
                        weight3(b, j)
                    if j == 1 and prev.valid():
                        invert3(prev)
                    if j in (3, 4, 5, 6) and prev.valid():
                        divide3(prev, j - 3)
                    if j >= 8 and nxt.valid():
                        add_bias3(nxt, j - 8)
            over_sequences(dve, -1, cosformer)

            dve.wait_ge(xn3_done, B)

            def ffn(n):
                if not has(n):
                    return
                x = block_of(n)
                nc.vector.tensor_copy(yres[:, :, :], x).then_inc(pre_step, 1)
                dve.wait_ge(pre_step, n * 9 + 1)
                for i in range(TBK):
                    nc.vector.bn_stats(bst[:, i, :], yres[:, i, :]).then_inc(pre_step, 1)
                dve.wait_ge(pre_step, n * 9 + 5)
                pass_on()
                for i in range(TBK):
                    nc.vector.bn_aggr(mv[:, i, :], bst[:, i, :]).then_inc(pre_step, 1)
                dve.wait_ge(prstd_step, n * 2 + 2)
                for i in range(TBK):
                    last = nc.vector.tensor_scalar(xn2[:, i, :], yres[:, i, :], mv[:, i, 0:1], rstd[:, i:i + 1],
                                                   ALU.subtract, ALU.mult)
                last.then_inc(h_done, 1)
                dve.wait_ge(h_done, n + 1)
                nc.vector.tensor_scalar(yres[:, :, :], yres[:, :, :], 2.0, None, ALU.mult).then_inc(doubled, 1)
                dve.wait_ge(doubled, n + 1)
                dve.wait_ge(down4_ready, n + 1)
                nc.vector.tensor_tensor(zt[:, :, :], bank[4][:, :].rearrange("p (t d) -> p t d", d=D),
                                        fb2[:, None, :].to_broadcast([P, TBK, D]), op=ALU.add).then_inc(z_step, 1)
                dve.wait_ge(z_step, n * 10 + 1)
                nc.vector.scalar_tensor_tensor(yo[:, :, :], zt[:, :, :], 0.5, yres[:, :, :],
                                               op0=ALU.mult, op1=ALU.add).then_inc(z_step, 1)
                dve.wait_ge(z_step, n * 10 + 2)
                for i in range(TBK):
                    nc.vector.bn_stats(bst[:, i, :], yo[:, i, :]).then_inc(z_step, 1)
                dve.wait_ge(z_step, n * 10 + 6)
                pass_on()
                for i in range(TBK):
                    nc.vector.bn_aggr(mv[:, i, :], bst[:, i, :]).then_inc(z_step, 1)
                dve.wait_ge(rstd4_step, n * 2 + 2)
                wait(dve, out_done, n * 16)
                for i in range(TBK):
                    last = nc.vector.tensor_scalar(xn[:, i, :], yo[:, i, :], mv[:, i, 0:1], rstd[:, i:i + 1],
                                                   ALU.subtract, ALU.mult)
                last.then_inc(xo_done, 1)
            over_blocks(dve, ffn)

        @block.scalar
        def _(act):
            def exponentials(b, j):
                act.wait_ge(sc_ready, b.count(UNITS, j + 1))
                if j % 3 == 0:
                    wait(act, av_ready, b.count(4, j // 3 - 3))
                nc.scalar.activation(ET[:, j, :], bank[j % 2][:, :], ACT.Exp, scale=DK0 ** -0.5).then_inc(exp_done, 1)

            def copy_values(b):
                act.wait_ge(proj_done, b.count(3, 3))
                wait(act, av_ready, b.count(4, -12))
                nc.scalar.activation(V0[:, b.rem, :, :, 0:DK0],
                                     bank[6][:, 0:TPB * D].rearrange("p (t h d) -> p t h d", t=TPB, d=DK0),
                                     ACT.Copy).then_inc(v_copied, 1)

            def copy_av(b, a):
                act.wait_ge(av_ready, b.count(4, 2 * a + 2))
                wait(act, avT_ready, b.count(2, a - 1))
                nc.scalar.activation(av0[:, a], bank[4 + a][:, :], ACT.Copy).then_inc(av_copied, 1)

            def second_part(b):
                act.wait_ge(part_step, b.count(3, 1))
                nc.scalar.activation(parts[:, 1], rem1[:, :, :], ACT.Copy).then_inc(part_step, 1)

            def copy_att(b):
                act.wait_ge(attT_ready, b.count(1, 1))
                wait(act, wo_ready, b.count(1, 0))
                nc.scalar.activation(attT0[:, :], bank[7][:, 0:S], ACT.Copy).then_inc(attT_copied, 1)

            def copy_tokens(b):
                act.wait_ge(xT_ready, b.count(1, 1))
                at = b.count(S)
                x = XT[:, at:at + S] if b.fixed() else XT[:, bass.ds(at, S)]
                nc.scalar.activation(x, bank[7][:, 0:S], ACT.Copy).then_inc(xT_copied, 1)

            def copy_max(b):
                act.wait_ge(nmt_ready, b.count(1, 1))
                nc.scalar.activation(nmt[:, :], bank[6][:, 0:S // 2].bitcast(BF16), ACT.Copy).then_inc(nmt_copied, 1)

            def step(b):
                nxt, nxt2, prev = b.plus(1), b.plus(2), b.plus(-1)
                for j in range(UNITS):
                    if j == 3 and nxt2.valid():
                        copy_values(nxt2)
                    if j == 5 and nxt2.valid():
                        second_part(nxt2)
                    if j == 7 and prev.valid():
                        copy_att(prev)
                    if j == 11 and prev.valid():
                        copy_tokens(prev)
                    if b.valid():
                        exponentials(b, j)
                    if j == 9 and b.valid():
                        copy_av(b, 0)
                if nxt.valid():
                    copy_max(nxt)
                if b.valid():
                    copy_av(b, 1)

            act.wait_ge(consts, 1)
            over_sequences(act, -2, step)

            act.wait_ge(gate_step, 4)
            nc.scalar.activation(prb2, probs, ACT.Exp).then_inc(gate_exp, 1)
            for n in range(NBLK):
                act.wait_ge(gateT_ready, n + 1)
                nc.scalar.activation(gateT[:, n, :], bank[6 + n % 2][:, 0:P], ACT.Copy).then_inc(gateT_copied, 1)

            def moe(n):
                for e in range(EXP):
                    if has(n):
                        for c in range(HC):
                            act.wait_ge(up_ready, n * (EXP * HC) + (e * HC + c + 1))
                            if c == 0:
                                wait(act, down_ready, n * EXP + (e - 2))
                            nc.scalar.activation(hid[:, e % 3, c, :], bank[c][:, :], ACT.Gelu_apprx_tanh,
                                                 bias=b1[:, e, c:c + 1]).then_inc(gelu_done, 1)
                    if e == 3 and has(n - 1):
                        act.wait_ge(xT2_ready, n)
                        m = n - 1
                        x = XT[:, m * BLK:(m + 1) * BLK] if isinstance(m, int) else XT[:, bass.ds(m * BLK, BLK)]
                        nc.scalar.activation(x, bank[7][:, :], ACT.Copy).then_inc(xT2_copied, 1)
            over_blocks(act, moe)

            def cosformer(b):
                nxt, prev = b.plus(1), b.plus(-1)

                def copy_num(b, g):
                    act.wait_ge(num_ready, b.count(8, 2 * g + 2))
                    wait(act, att3_done, b.count(HG, g - 3))
                    nc.scalar.activation(num[:, 2 * g:2 * g + 2, :].rearrange("p c t -> p (c t)"), bank[4][:, :], ACT.Copy).then_inc(num_copied, 1)

                if prev.valid():
                    copy_num(prev, 2)
                for j in range(UNITS):
                    if j < 8 and nxt.valid():
                        act.wait_ge(p3_ready, nxt.count(UNITS, j + 1))
                        if j == 0:
                            wait(act, s3_ready, nxt.count(UNITS, -UNITS))
                        for k, bias in enumerate((bq, bk)):
                            nc.scalar.activation(QK[:, nxt.rem % 2, k, j, :], bank[j % 2][:, k * S:(k + 1) * S],
                                                 ACT.Relu, bias=bias[:, j:j + 1]).then_inc(relu_done, 1)
                    if j == 0 and prev.valid():
                        copy_num(prev, 3)
                    if j in (6, 8) and b.valid():
                        copy_num(b, j // 2 - 3)
            over_sequences(act, -1, cosformer)

            def ffn(n):
                if not has(n):
                    return
                act.wait_ge(hT_ready, n + 1)
                wait(act, up4_ready, n * HC)
                nc.scalar.activation(hT[:, 0, :], bank[7][:, :], ACT.Identity, bias=bet[:, :], scale=gam[:, :]).then_inc(hT_copied, 1)
                for c in range(HC):
                    act.wait_ge(up4_ready, n * HC + c + 1)
                    if c == 0:
                        wait(act, down4_ready, n)
                    nc.scalar.activation(yT[:, 0, c, :], bank[c][:, :], ACT.Silu, bias=fb1[:, c:c + 1]).then_inc(silu_done, 1)
            over_blocks(act, ffn)

        @block.gpsimd
        def _(pool):
            zero = pool.to_reg(0.0)

            def split(b):
                pool.wait_ge(part1, b.count(1, 1))
                nc.gpsimd.tensor_tensor(rem1[:, :, :], qk[:, :, :], parts[:, 0], op=ALU.subtract).then_inc(part_step, 1)
                pool.wait_ge(part_step, b.count(3, 2))
                nc.gpsimd.tensor_tensor(parts[:, 2], rem1[:, :, :], parts[:, 1], op=ALU.subtract).then_inc(part_step, 1)

            def select(b, j):
                pool.wait_ge(exp_done, b.count(UNITS, j + 1))
                nc.gpsimd.tensor_tensor(beat[:, j:j + 1], mhalf[:, 0:1], mhalf[:, 0:1], op=ALU.add)
                if j % 3 == 2:
                    e, n = ET[:, j, :].rearrange("p (h q) -> p h q", q=P), 4
                else:
                    e, n = ET[:, j, :].rearrange("p (h q) -> p h q", q=S)[:, :, 0:P], 2
                nc.gpsimd.affine_select(out=e, in_=e, compare_op=ALU.is_ge, fill=zero, base=0,
                                        pattern=[[0, n], [1, P]], channel_multiplier=-1).then_inc(sel_done, 1)

            def deviation(b):
                pool.wait_ge(ln_step, b.count(5, 5))
                nc.gpsimd.tensor_tensor(veps[:, 0:TPB], mv[:, 0:TPB, 1], epsc[:, 0:TPB], op=ALU.add).then_inc(rstd_step, 1)
                pool.wait_ge(rstd_step, b.count(2, 1))
                nc.gpsimd.tensor_tensor(rstd[:, 0:TPB], veps[:, 0:TPB], mhalf[:, 0:TPB], op=ALU.pow).then_inc(rstd_step, 1)

            def keep(b):
                pool.wait_ge(xn_done, b.count(1, 1))
                at = b.count(TPB)
                x = X[:, at:at + TPB, :] if b.fixed() else X[:, bass.ds(at, TPB), :]
                nc.gpsimd.tensor_copy(x, xn[:, 0:TPB, :]).then_inc(xn_kept, 1)

            def step(b):
                nxt2, prev = b.plus(2), b.plus(-1)
                for j in range(UNITS):
                    if b.valid():
                        select(b, j)
                    if j == 3 and nxt2.valid():
                        split(nxt2)
                    if j == 7 and prev.valid():
                        deviation(prev)
                    if j == 10 and prev.valid():
                        keep(prev)

            pool.wait_ge(consts, 1)
            over_sequences(pool, -2, step)

            pool.wait_ge(fq_in, 64)
            for a in range(2):
                nc.gpsimd.tensor_scalar(fd[:, a], fq[:, a], -128.0, None, ALU.add).then_inc(deq_step, 1)
                pool.wait_ge(deq_step, 2 * a + 1)
                w = f1[:, :] if a == 0 else f2[:, :, :].rearrange("p c n -> p (c n)")
                nc.gpsimd.tensor_tensor(w, fd[:, a], fs[:, a], op=ALU.mult).then_inc(deq_step, 1)

            def deviations(ready, at, step_sem, n, tiles, base):
                pool.wait_ge(ready, at)
                nc.gpsimd.tensor_tensor(veps[:, 0:tiles], mv[:, 0:tiles, 1], epsc[:, 0:tiles], op=ALU.add).then_inc(step_sem, 1)
                pool.wait_ge(step_sem, base + 1)
                nc.gpsimd.tensor_tensor(rstd[:, 0:tiles], veps[:, 0:tiles], mhalf[:, 0:tiles], op=ALU.pow).then_inc(step_sem, 1)

            def moe(n):
                if has(n):
                    wait(pool, down_ready, (n - 1) * EXP + 1)
                    if isinstance(n, int) and n == 0:
                        pool.wait_ge(gateT_copied, NBLK)
                    g = gateT[:, n, :] if isinstance(n, int) else gateT[:, bass.ds(n, 1), :].rearrange("p o t -> p (o t)")
                    nc.gpsimd.tensor_copy(gTb[:, :], g).then_inc(gTb_done, 1)
                    deviations(ln2_step, n * 8 + 8, rstd2_step, n, TBK, n * 2)
                    pool.wait_ge(xn2_done, n + 1)
                    x = X[:, n * TBK:(n + 1) * TBK, :] if isinstance(n, int) else X[:, bass.ds(n * TBK, TBK), :]
                    nc.gpsimd.tensor_copy(x, xn[:, :, :]).then_inc(xn2_kept, 1)
            over_blocks(pool, moe)

            pool.wait_ge(xT2_copied, NBLK)

            def cosformer(b):
                nxt, prev = b.plus(1), b.plus(-1)
                if nxt.valid():
                    wait(pool, p3_ready, nxt.count(UNITS, -UNITS))
                    at = nxt.count(S)
                    x = XT[:, at:at + S] if nxt.fixed() else XT[:, bass.ds(at, S)]
                    nc.gpsimd.tensor_copy(xt3[:, nxt.rem % 2, :], x).then_inc(xt3_done, 1)
                if prev.valid():
                    deviations(ln3_step, prev.count(6, 6), rstd3_step, 0, TPB, prev.count(2, 0))
            over_sequences(pool, -1, cosformer)

            def ffn(n):
                if has(n):
                    deviations(pre_step, n * 9 + 9, prstd_step, n, TBK, n * 2)
                    deviations(z_step, n * 10 + 10, rstd4_step, n, TBK, n * 2)
            over_blocks(pool, ffn)


def constants():
    bf16 = mybir.dt.np(BF16)
    half = DK0 // 2
    inv = np.float32(10000.0) ** (np.float32(-2.0) * np.arange(half, dtype=np.float32) / np.float32(DK0))
    ang = np.arange(S, dtype=np.float32)[None, :] * inv[:, None]
    d = np.arange(P) % DK0
    sign = np.where(d % 2 == 0, -1.0, 1.0)[:, None]
    rope = np.stack([np.cos(ang)[d // 2], sign * np.sin(ang)[d // 2]], 1).astype(np.float32)
    at = np.arange(P)
    mask = np.where(at[None, :] <= at[:, None], 0.0, BIG).astype(bf16)
    oneh = np.zeros((P, H0, P))
    for s in range(NS):
        for h in range(H0):
            oneh[H0 * s + h, h] = 1.0
    apart = np.arange(S)[None, :] - at[:, None]
    dtab = np.where(apart >= 0, np.cos(np.pi / (2.0 * S) * apart), 0.0).astype(np.float32)
    spread = np.zeros((P, 8, P), np.float32)
    for h in range(H1):
        spread[32 * (h % 4) + h // 4, h // 2, DH1 * (h % 2):DH1 * (h % 2 + 1)] = 1.0
    rank = np.broadcast_to(np.arange(NE, 0, -1, dtype=np.float32), (P, NE))
    return {"rope": rope, "identf": np.eye(P, dtype=np.float32), "identb": np.eye(P).astype(bf16), "maskb": mask,
            "oneh": oneh.astype(bf16), "dtab": dtab, "rank": np.ascontiguousarray(rank), "spread": spread}


def layout(i):
    x = i["L0_attn_x"].reshape(N, D)
    swap = np.arange(D) ^ 1
    a0 = [i["L0_attn_wq"], i["L0_attn_wq"][swap], i["L0_attn_wk"], i["L0_attn_wk"][swap], i["L0_attn_wv"], i["L0_attn_wo"]]
    b1 = np.concatenate([i["L0_ffn_bfc_s"][None], i["L0_ffn_bfc"]]).reshape(EXP, HC, P).transpose(2, 0, 1)
    b2 = np.zeros((TBK, 32, TBK, D), np.float32)
    for k in range(TBK):
        b2[k, 0, k] = i["L0_ffn_bproj_s"]
        b2[k, 1:EXP, k] = i["L0_ffn_bproj"]
    return {
        "x": x, "xT": x.T, "a0": np.stack([w.T for w in a0], 1),
        "wr": i["L0_ffn_Wr"], "w1s": i["L0_ffn_Wfc_s"], "w1": i["L0_ffn_Wfc"], "w2s": i["L0_ffn_Wproj_s"],
        "w2": i["L0_ffn_Wproj"], "b1": b1, "b2": b2.reshape(P, TBK, D),
        "wq": i["L1_attn_Wq"], "wk": i["L1_attn_Wk"], "wv": i["L1_attn_Wv"], "wo": i["L1_attn_Wo"],
        "bq": i["L1_attn_bq"].reshape(8, P).T, "bk": i["L1_attn_bk"].reshape(8, P).T,
        "bv": i["L1_attn_bv"], "bo": i["L1_attn_bo"],
        "fc1_q": i["L1_ffn_fc1_q"], "fc2_q": i["L1_ffn_fc2_q"], "fc1_scales": i["L1_ffn_fc1_scales"].reshape(-1),
        "fc2_scales": i["L1_ffn_fc2_scales"].reshape(-1), "fb1": i["L1_ffn_fc1_bias"].reshape(HC, P).T,
        "fb2": i["L1_ffn_fc2_bias"], "gam": i["L1_ffn_ln_gamma"].reshape(D, 1), "bet": i["L1_ffn_ln_beta"].reshape(D, 1),
    }


def kernel(**inputs):
    import concourse.bacc as bacc
    from concourse.bass_utils import run_bass_kernel_spmd

    given = layout({k: np.asarray(v) for k, v in inputs.items()}) | constants()
    given = {k: np.ascontiguousarray(v) for k, v in given.items()}
    nc = bacc.Bacc("TRN2", target_bir_lowering=False, num_devices=1)
    t = {k: nc.dram_tensor(f"in_{k}", v.shape, mybir.dt.from_np(v.dtype), kind="ExternalInput").ap()
         for k, v in given.items()}
    t["out"] = nc.dram_tensor("out", (N, D), F32, kind="ExternalOutput").ap()
    build(nc, t)
    r = run_bass_kernel_spmd(nc, [{f"in_{k}": v for k, v in given.items()}], core_ids=[0])
    return r.results[0]["out"].reshape(B, S, D)
```

```python
from contextlib import ExitStack

import numpy as np

import concourse.bass as bass
from concourse import mybir

F32 = mybir.dt.float32
BF16 = mybir.dt.bfloat16
I32 = mybir.dt.int32
ALU = mybir.AluOpType
ACT = mybir.ActivationFunctionType
AX = mybir.AxisListType

P = 128
D = 128
B, S = 16, 256
N = B * S
NT = N // P
TPB = S // P
H0, DK0 = 16, 8
NS = 3
SLOTS = 6
KST = SLOTS * DK0
VW = 32
NE, HID = 8, 512
EXP = NE + 1
HC = HID // P
H1, DH1 = 16, 64
BLK = 512
NBLK = N // BLK
TBK = BLK // P
EPS = 1e-5
BIG = -1e30
UNITS = 12
GRP = 4
HG = 4
GATE_STEPS = 24


class Batch:

    def __init__(self, quad, rem, of=4, total=B):
        self.quad, self.rem, self.of, self.total = quad, rem, of, total

    def plus(self, k):
        r = self.rem + k
        return Batch(self.quad + r // self.of, r % self.of, self.of, self.total)

    def count(self, per, k=0):
        return self.quad * (self.of * per) + (self.rem * per + k)

    def fixed(self):
        return isinstance(self.quad, int)

    def index(self):
        return self.of * self.quad + self.rem if self.fixed() else None

    def valid(self):
        return not self.fixed() or 0 <= self.index() < self.total


def over_blocks(eng, step):
    step(0)
    with eng.Fori(1, NBLK) as n:
        step(n)
    step(NBLK)


def has(n):
    return not isinstance(n, int) or 0 <= n < NBLK


def wait(eng, sem, value):
    if not isinstance(value, int) or value > 0:
        eng.wait_ge(sem, value)


def over_sequences(eng, first, step):
    for b in range(first, 2):
        step(Batch(b // 4, b % 4))
    loops = (B - 4) // 4
    with eng.Fori(0, loops) as i:
        for r in range(4):
            step(Batch(i, 2 + r).plus(0))
    for b in range(2 + 4 * loops, B + 1):
        step(Batch(b // 4, b % 4))


def over_pairs(eng, step):
    for n in range(-2, 2):
        step(Batch(n // 2, n % 2, 2, NBLK))
    loops = (NBLK - 4) // 2
    with eng.Fori(0, loops) as i:
        for k in range(2, 4):
            step(Batch(i, 0, 2, NBLK).plus(k))
    for n in range(2 + 2 * loops, NBLK + 1):
        step(Batch(n // 2, n % 2, 2, NBLK))


def expert(k):
    return (k + 1) % EXP


def build(nc, t):
    ctx = ExitStack()
    with ctx:
        def sb(name, shape, dt=F32):
            return ctx.enter_context(nc.sbuf_tensor(name, shape, dt))

        def sem(name):
            return ctx.enter_context(nc.semaphore(name))

        bank = [ctx.enter_context(nc.psum_tensor(f"bank{i}", [P, 512], F32)) for i in range(8)]
        X = sb("X", [P, NT, D])
        XT = sb("XT", [P, N])
        w1 = sb("w1", [P, EXP, HID])
        w2 = sb("w2", [P, EXP, HC, D])
        b1 = sb("b1", [P, EXP, HC])
        wq = sb("wq", [P, H1 * DH1])
        wk = sb("wk", [P, H1 * DH1])
        wv = sb("wv", [P, H1 * DH1])
        wo = sb("wo", [P, 8, D])
        bq = sb("bq", [P, 8])
        bk = sb("bk", [P, 8])
        bv = sb("bv", [P, H1 * DH1])
        bo = sb("bo", [P, D])
        a0 = sb("a0", [P, 6, D])
        rope = sb("rope", [P, 2, S])
        identf = sb("identf", [P, P])
        identb = sb("identb", [P, P], BF16)
        maskb = sb("maskb", [P, P], BF16)
        oneh = sb("oneh", [P, H0, P], BF16)
        dtab = sb("dtab", [P, S])
        rank = sb("rank", [P, NE])
        wr = sb("wr", [P, NE])
        arenaA = sb("arenaA", [P, 8192])
        arenaB = sb("arenaB", [P, 6144])
        ET = sb("ET", [P, UNITS, 512])
        arenaC = sb("arenaC", [P, 2 * TPB * H1 * DH1])
        Vc = arenaC[:, :].rearrange("p (r t h d) -> p r t h d", r=2, t=TPB, h=H1)

        def carve(arena):
            at = [0]

            def piece(words, dt=F32):
                at[0] += words
                ap = arena[:, at[0] - words:at[0]]
                return ap if dt is F32 else ap.bitcast(dt)
            return piece
        pieceC, pieceB = carve(arenaC), carve(arenaB)
        piece2 = carve(arenaA)
        gate = piece2(NT * 32).rearrange("p (n e) -> p n e", e=32)
        gateT = piece2(NBLK * P).rearrange("p (n t) -> p n t", t=P)
        probs, ge, wt, sel1, sel2, prb2 = (piece2(NT * NE).rearrange("p (n e) -> p n e", e=NE) for _ in range(6))
        gmax, gsum, grec, top1, top2, wmax, wmax2, tsum, trec = (piece2(NT) for _ in range(9))
        hid = arenaB[:, :].rearrange("p (r c t) -> p r c t", r=3, c=HC)
        gb = piece2(TBK * EXP).rearrange("p (n e) -> p n e", e=EXP)
        gTb = piece2(P)
        b2 = piece2(TBK * D).rearrange("p (i d) -> p i d", d=D)
        QK = arenaA[:, :].rearrange("p (r k c t) -> p r k c t", r=2, k=2, c=8)
        pieceB3 = carve(arenaB)
        attT = pieceB3(8 * S).rearrange("p (c t) -> p c t", c=8)
        num = pieceB3(8 * S).rearrange("p (c t) -> p c t", c=8)
        xt3 = pieceB3(2 * S).rearrange("p (r t) -> p r t", r=2)
        den3, rec3 = pieceB3(S), pieceB3(S)
        spread = pieceB3(8 * P).rearrange("p (c n) -> p c n", c=8)

        def unit3(j):
            half, k = divmod(j, 6)
            u = k // 2
            return half, k % 2, u, range(4 * half, 4 * half + 4) if u == 2 else range(4 * half + 2 * u, 4 * half + 2 * u + 2)

        def weights3(pair, odd, k):
            half, q = divmod(pair, 4)
            if k == 0:
                return ET[:, 6 * half + 2 * (q // 2) + odd, (q % 2) * S:(q % 2 + 1) * S]
            return ET[:, 6 * half + 4 + odd, q * P:(q + 1) * P]

        den_step = sem("den_step")
        spread_ready = sem("spread_ready")
        ones3 = sb("ones3", [P, HG, 32])
        pieceB4 = carve(arenaB)
        hT = pieceB4(2 * BLK).rearrange("p (r t) -> p r t", r=2)
        yT = pieceB4(2 * HC * BLK).rearrange("p (r c t) -> p r c t", r=2, c=HC)
        xn2 = pieceB4(BLK).rearrange("p (t d) -> p t d", d=D)
        f1 = sb("f1", [P, HID])
        f2 = sb("f2", [P, HC, D])
        fb1 = sb("fb1", [P, HC])
        fb2 = sb("fb2", [P, D])
        gam = sb("gam", [P, 1])
        bet = sb("bet", [P, 1])
        pieceC4 = carve(arenaC)
        fq = pieceC4(2 * HID, I32).rearrange("p (a n) -> p a n", a=2)
        fs = pieceC4(2 * HID).rearrange("p (a n) -> p a n", a=2)
        fd = pieceC4(2 * HID).rearrange("p (a n) -> p a n", a=2)
        pieceD4 = carve(arenaC)
        base4 = pieceD4(2 * BLK).rearrange("p (r t d) -> p r t d", r=2, d=D)
        yo = pieceD4(BLK).rearrange("p (t d) -> p t d", d=D)
        half_bias = pieceD4(D)
        bst4 = sb("bst4", [P, TBK, 6])
        mv4 = sb("mv4", [P, TBK, 2])
        veps4 = sb("veps4", [P, TBK])
        rstd4 = sb("rstd4", [P, TBK])
        stack = arenaA[:, :].bitcast(BF16).rearrange("p (r k h t) -> p r k h t", r=4, k=2, h=8)
        xb = pieceC(2 * S).rearrange("p (r t) -> p r t", r=2)
        ropet = pieceC(4 * S).rearrange("p (k a t) -> p k a t", k=2, a=2)
        qk = pieceC(2 * S).rearrange("p (k t) -> p k t", k=2)
        rem1 = pieceC(2 * S).rearrange("p (k t) -> p k t", k=2)
        parts = pieceC(NS * S, BF16).rearrange("p (s k t) -> p s k t", s=NS, k=2)
        V0 = pieceB(4 * TPB * H0 * VW).rearrange("p (r t h d) -> p r t h d", r=4, t=TPB, h=H0)
        av0 = pieceB(2 * 512).rearrange("p (a n) -> p a n", a=2)
        nm = sb("nm", [P, TPB, H0])
        nmr = sb("nmr", [P, TPB, H0])
        nmp = sb("nmp", [P, TPB, 2, 4, H0], BF16)
        nmt = sb("nmt", [P, S], BF16)
        rden = sb("rden", [P, 2, H0, 1])
        att0 = pieceB(TPB * D).rearrange("p (t d) -> p t d", t=TPB)
        attT0 = pieceB(S)
        yres = sb("yres", [P, TBK, D])
        bst = sb("bst", [P, TBK, 6])
        mv = sb("mv", [P, TBK, 2])
        veps = sb("veps", [P, TBK])
        rstd = sb("rstd", [P, TBK])
        mhalf = sb("mhalf", [P, TBK])
        epsc = sb("epsc", [P, TBK])
        beat = sb("beat", [P, UNITS + 1])
        xn = sb("xn", [P, TBK, D])

        scr = nc.dram_tensor("scr", (2, 2, NS, DK0, H0, S), BF16).ap()

        a0_in = sem("a0_in")
        rope_in = sem("rope_in")
        w_in = sem("w_in")
        wr_in = sem("wr_in")
        x_in = sem("x_in")
        xb_in = [sem("xb_in0"), sem("xb_in1")]
        w1_in = sem("w1_in")
        w3_in = sem("w3_in")
        w4_in = sem("w4_in")
        consts = sem("consts")
        proj_done = sem("proj_done")
        rope_read = sem("rope_read")
        rope_step = sem("rope_step")
        part1 = sem("part1")
        part_step = sem("part_step")
        scr_out = sem("scr_out")
        stack_in = [sem(f"stack_in{i}") for i in range(4)]
        v_copied = sem("v_copied")
        max_ready = sem("max_ready")
        max_taken = sem("max_taken")
        nm_step = sem("nm_step")
        nmt_ready = sem("nmt_ready")
        nmt_copied = sem("nmt_copied")
        sc_ready = sem("sc_ready")
        exp_done = sem("exp_done")
        sel_done = sem("sel_done")
        av_ready = sem("av_ready")
        rden_done = sem("rden_done")
        att_done = sem("att_done")
        av_copied = sem("av_copied")
        avT_ready = sem("avT_ready")
        attT_ready = sem("attT_ready")
        attT_copied = sem("attT_copied")
        wo_ready = sem("wo_ready")
        ln_step = sem("ln_step")
        rstd_step = sem("rstd_step")
        xn_done = sem("xn_done")
        xn_kept = sem("xn_kept")
        xT_ready = sem("xT_ready")
        xT_copied = sem("xT_copied")
        out_done = sem("out_done")
        route_ready = sem("route_ready")
        gate_step = sem("gate_step")
        gate_exp = sem("gate_exp")
        gateT_ready = sem("gateT_ready")
        gateT_copied = sem("gateT_copied")
        gTb_done = sem("gTb_done")
        gb_done = sem("gb_done")
        up_ready = sem("up_ready")
        gelu_done = sem("gelu_done")
        down_ready = sem("down_ready")
        acc_done = sem("acc_done")
        ln2_step = sem("ln2_step")
        rstd2_step = sem("rstd2_step")
        xn2_done = sem("xn2_done")
        xn2_kept = sem("xn2_kept")
        xT2_ready = sem("xT2_ready")
        xT2_copied = sem("xT2_copied")
        xt3_done = sem("xt3_done")
        ones_step = sem("ones_step")
        p3_ready = sem("p3_ready")
        relu_done = sem("relu_done")
        v3_done = sem("v3_done")
        s3_ready = sem("s3_ready")
        s3_taken = sem("s3_taken")
        num_ready = sem("num_ready")
        num_copied = sem("num_copied")
        att3_done = sem("att3_done")
        o3_ready = sem("o3_ready")
        ln3_step = sem("ln3_step")
        rstd3_step = sem("rstd3_step")
        xn3_done = sem("xn3_done")
        fq_in = sem("fq_in")
        deq_step = sem("deq_step")
        pre_step = sem("pre_step")
        prstd_step = sem("prstd_step")
        h_done = sem("h_done")
        bias_step = sem("bias_step")
        base_step = sem("base_step")
        hT_ready = sem("hT_ready")
        hT_copied = sem("hT_copied")
        up4_ready = sem("up4_ready")
        silu_done = sem("silu_done")
        down4_ready = sem("down4_ready")
        z_step = sem("z_step")
        rstd4_step = sem("rstd4_step")
        xo_done = sem("xo_done")

        block = ctx.enter_context(nc.Block())

        @block.sync
        def _(sp):
            def load_block(b):
                if not b.valid():
                    return
                wait(sp, proj_done, b.plus(-2).count(3, 3) if not b.fixed() or b.index() >= 2 else 0)
                at = b.count(S)
                src = t["xT"][:, at:at + S] if b.fixed() else t["xT"][:, bass.ds(at, S)]
                sp.dma_start(xb[:, b.rem % 2, :], src).then_inc(xb_in[b.rem % 2], 16)

            sp.dma_start(a0[:, :, :], t["a0"]).then_inc(a0_in, 16)
            load_block(Batch(0, 0))
            sp.dma_start(rope[:, :, :], t["rope"]).then_inc(rope_in, 16)
            load_block(Batch(0, 1))
            for dst, name in ((wr, "wr"), (rank, "rank")):
                sp.dma_start(dst[:, :], t[name]).then_inc(wr_in, 16)
            for dst, name in ((identb, "identb"), (maskb, "maskb"), (oneh, "oneh"), (identf, "identf")):
                sp.dma_start(dst[:, :, :] if dst is oneh else dst[:, :], t[name]).then_inc(w_in, 16)
            def step(b):
                n2 = b.plus(2)
                if not b.fixed() or b.index() >= 0:
                    load_block(n2)
                if n2.valid():
                    slot = n2.rem % 2
                    wait(sp, part_step, n2.count(3, 3))
                    for k in range(2):
                        for s in range(NS):
                            if (k, s) == (1, NS - 1):
                                wait(sp, sc_ready, b.plus(-2).count(UNITS, UNITS) if not b.fixed() or b.index() >= 2 else 0)
                            at = s if k == 0 else NS - 1 - s
                            sp.dma_start(scr[slot, k, at].rearrange("d h t -> h d t"),
                                         parts[:, s, k, :]).then_inc(scr_out, 16)
                    wait(sp, scr_out, n2.count(96, 96))
                    for k in range(2):
                        src = scr[slot, k].rearrange("s d (q h) t -> q (s d) h t", q=2)
                        for q in range(2):
                            row = 64 * q
                            for n in (3, 2, 1):
                                f = 0 if k == 0 else NS - n
                                sp.dma_start(stack[row:row + n * DK0, n2.rem, k, :, :],
                                             src[q, f * DK0:(f + n) * DK0]).then_inc(stack_in[n2.rem], 16)
                                row += n * DK0
                if b.fixed() and b.index() == -2:
                    sp.dma_start(X[:, :, :], t["x"].rearrange("(n p) d -> p n d", p=P)).then_inc(x_in, 16)
            over_sequences(sp, -2, step)
            for dst, name in ((wq, "wq"), (wk, "wk"), (wv, "wv"), (bq, "bq"), (bk, "bk"), (dtab, "dtab"),
                              (fb1, "fb1"), (gam, "gam"), (bet, "bet")):
                sp.dma_start(dst[:, :], t[name]).then_inc(w3_in, 16)
            sp.dma_start(wo[:, :, :], t["wo"].rearrange("(c p) n -> p c n", p=P)).then_inc(w3_in, 16)
            for dst, name in ((bv, "bv"), (bo, "bo"), (fb2, "fb2")):
                sp.dma_start(dst[:, :], t[name].partition_broadcast(P)).then_inc(w3_in, 16)
            sp.wait_ge(xT_copied, B)
            sp.dma_start(b2, t["b2"]).then_inc(w1_in, 16)
            sp.dma_start(fq[:, 0, :], t["fc1_q"]).then_inc(fq_in, 16)
            sp.dma_start(fq[:, 1, :].rearrange("p (c n) -> p c n", c=HC),
                         t["fc2_q"].rearrange("(c p) n -> p c n", p=P)).then_inc(fq_in, 16)
            sp.dma_start(fs[:, 0, :], t["fc1_scales"].partition_broadcast(P)).then_inc(fq_in, 16)
            sp.dma_start(fs[:, 1, :], t["fc2_scales"].partition_broadcast(P)).then_inc(fq_in, 16)

            sp.wait_ge(acc_done, NBLK * EXP)
            sp.dma_start(spread, t["spread"]).then_inc(w3_in, 16)

            def store(n):
                if has(n):
                    sp.wait_ge(xo_done, n + 1)
                    out = t["out"].rearrange("(n p) d -> p n d", p=P)
                    out = out[:, n * TBK:(n + 1) * TBK, :] if isinstance(n, int) else out[:, bass.ds(n * TBK, TBK), :]
                    sp.dma_start(out, xn[:, :, :]).then_inc(out_done, 16)
            over_blocks(sp, store)
            sp.wait_ge(out_done, NBLK * 16)

        @block.tensor
        def _(pe):
            def head_rows(h):
                lo = 64 * (h // 8)
                return slice(lo, lo + KST), h % 8

            def project(b):
                x = xb[:, b.rem % 2, :]
                if b.fixed():
                    wait(pe, v_copied, b.count(1, 0))
                    wait(pe, rope_read, b.count(2, 0))
                pe.wait_ge(xb_in[b.rem % 2], (b.quad * 2 + b.rem // 2) * 16 + 16)
                wait(pe, nmt_copied, b.count(1, -1))
                nc.tensor.matmul(bank[6][:, 0:S], a0[:, 0, :], x, start=True, stop=True)
                nc.tensor.matmul(bank[6][:, S:2 * S], a0[:, 1, :], x, start=True, stop=True).then_inc(proj_done, 1)
                wait(pe, xT_copied, b.count(1, -3))
                nc.tensor.matmul(bank[7][:, 0:S], a0[:, 2, :], x, start=True, stop=True)
                nc.tensor.matmul(bank[7][:, S:2 * S], a0[:, 3, :], x, start=True, stop=True).then_inc(proj_done, 1)
                pe.wait_ge(rope_read, b.count(2, 1))
                for i in range(TPB):
                    last = nc.tensor.matmul(bank[6][:, i * D:(i + 1) * D], x[:, i * P:(i + 1) * P], a0[:, 4, :],
                                            start=True, stop=True)
                last.then_inc(proj_done, 1)

            def max_unit(b, j):
                if b.fixed() and b.index() == 0 and j == 0:
                    pe.wait_ge(w_in, 64)
                if j == 0:
                    pe.wait_ge(stack_in[b.rem], (b.quad + 1) * 192)
                g, u = divmod(j, 3)
                ps = bank[2 + j % 2]
                wait(pe, max_taken, b.count(UNITS, j - 1))
                heads = range(4 * g, 4 * g + 4) if u == 0 else range(4 * g + 2 * u - 2, 4 * g + 2 * u)
                keys = P if u == 0 else S
                q0 = 0 if u == 0 else P
                for n, h in enumerate(heads):
                    rows, hp = head_rows(h)
                    nc.tensor.matmul(ps[:, n * keys:(n + 1) * keys], stack[rows, b.rem, 0, hp, q0:q0 + P],
                                     stack[rows, b.rem, 1, hp, 0:keys], start=(n == 0), stop=False,
                                     skip_group_check=True)
                diag = ps[:, :].rearrange("p (h k) -> p h k", k=keys)[:, :, keys - P:keys]
                nc.tensor.matmul(diag, identb[:, :], maskb[:, None, :].to_broadcast([P, len(heads), P]),
                                 start=False, stop=True, skip_group_check=True).then_inc(max_ready, 1)

            def score_unit(b, j):
                if j == 0:
                    pe.wait_ge(stack_in[b.rem], (b.quad + 1) * 192)
                    pe.wait_ge(nmt_copied, b.count(1, 1))
                g, u = divmod(j, 3)
                ps = bank[j % 2]
                wait(pe, exp_done, b.count(UNITS, j - 1))
                heads = range(4 * g, 4 * g + 4) if u == 2 else range(4 * g + 2 * u, 4 * g + 2 * u + 2)
                k0 = P if u == 2 else 0
                n_q = S - k0
                for n, h in enumerate(heads):
                    rows, hp = head_rows(h)
                    nc.tensor.matmul(ps[:, n * n_q:(n + 1) * n_q], stack[rows, b.rem, 1, hp, k0:k0 + P],
                                     stack[rows, b.rem, 0, hp, k0:S], start=(n == 0), stop=False,
                                     skip_group_check=True)
                    last = nc.tensor.matmul(ps[:, n * n_q:(n + 1) * n_q], oneh[:, h, :], nmt[:, k0:S],
                                            start=False, stop=True, skip_group_check=True)
                last.then_inc(sc_ready, 1)

            def weigh_values(b, g):
                pe.wait_ge(sel_done, b.count(UNITS, 3 * g + 3))
                if g == 0:
                    pe.wait_ge(v_copied, b.count(1, 1))
                if g % 2 == 0:
                    wait(pe, av_copied, b.count(2, g // 2 - 1))
                out = bank[4 + g // 2][:, (g % 2) * S:(g % 2 + 1) * S]
                v = V0[:, b.rem]
                for r in range(HG):
                    h = HG * g + r
                    q = slice(VW * r, VW * (r + 1))
                    nc.tensor.matmul(out[q, :], v[:, 0, h, :], ET[:, 3 * g + r // 2, (r % 2) * S:(r % 2 + 1) * S],
                                     start=(g % 2 == 0), stop=False, skip_group_check=True)
                for r in range(HG):
                    h = HG * g + r
                    q = slice(VW * r, VW * (r + 1))
                    last = nc.tensor.matmul(out[q, P:S], v[:, 1, h, :], ET[:, 3 * g + 2, r * P:(r + 1) * P],
                                            start=False, stop=True, skip_group_check=True)
                last.then_inc(av_ready, 1)

            def transpose_values(b, a):
                pe.wait_ge(av_copied, b.count(2, a + 1))
                if a == 0:
                    pe.wait_ge(rope_read, b.plus(3).count(2, 2) if b.plus(3).valid() else 2 * B)
                else:
                    pe.wait_ge(v_copied, b.plus(3).count(1, 1) if b.plus(3).valid() else B)
                for g in range(2):
                    for i in range(TPB):
                        at = (i * 2 + g) * P
                        last = nc.tensor.transpose(bank[7 - a][:, at:at + P],
                                                   av0[:, a, g * S + i * P:g * S + (i + 1) * P], identf[:, :])
                last.then_inc(avT_ready, 1)

            def transpose_max(b):
                pe.wait_ge(nm_step, b.count(5, 5))
                wait(pe, ln_step, b.count(5, -9))
                if b.fixed():
                    wait(pe, v_copied, min(b.index() + 2, B))
                ps = bank[6][:, 0:S // 2].bitcast(BF16)
                for i in range(TPB):
                    last = nc.tensor.transpose(ps[:, i * P:(i + 1) * P],
                                               nmp[:, i].rearrange("p a s h -> p (a s h)"), identb[:, :])
                last.then_inc(nmt_ready, 1)

            def transpose_att(b):
                pe.wait_ge(att_done, b.count(2, 2))
                for i in range(TPB):
                    last = nc.tensor.transpose(bank[7][:, i * P:(i + 1) * P], att0[:, i, :], identf[:, :])
                last.then_inc(attT_ready, 1)

            def out_project(b):
                pe.wait_ge(attT_copied, b.count(1, 1))
                for i in range(TPB):
                    last = nc.tensor.matmul(bank[6][:, i * D:(i + 1) * D], attT0[:, i * P:(i + 1) * P], a0[:, 5, :],
                                            start=True, stop=True)
                last.then_inc(wo_ready, 1)

            def transpose_norm(b):
                pe.wait_ge(xn_done, b.count(1, 1))
                for i in range(TPB):
                    last = nc.tensor.transpose(bank[7][:, i * P:(i + 1) * P], xn[:, i, :], identf[:, :])
                last.then_inc(xT_ready, 1)

            def route(first, end):
                for i in range(first, end):
                    last = nc.tensor.matmul(bank[2][:, i * NE:(i + 1) * NE], XT[:, i * P:(i + 1) * P], wr[:, :],
                                            start=True, stop=True)
                return last

            def step(b):
                now, nxt, nxt2, prev = b, b.plus(1), b.plus(2), b.plus(-1)
                done = {"s": 0, "m": 0}

                def scores(n):
                    for _ in range(n):
                        if now.valid():
                            score_unit(now, done["s"])
                        done["s"] += 1

                def maxima(n):
                    for _ in range(n):
                        if nxt.valid():
                            max_unit(nxt, done["m"])
                        done["m"] += 1

                if b.fixed() and b.index() == B:
                    pe.wait_ge(wr_in, 32)
                    pe.wait_ge(max_taken, B * UNITS)
                    pe.wait_ge(xT_copied, B - 1)
                    route(0, NT - TPB)
                scores(1)
                if prev.valid():
                    weigh_values(prev, 3)
                scores(2)
                if nxt2.valid():
                    project(nxt2)
                scores(1)
                maxima(2)
                if prev.valid():
                    transpose_values(prev, 0)
                scores(1)
                maxima(2)
                if prev.valid():
                    transpose_values(prev, 1)
                scores(1)
                maxima(2)
                if prev.valid():
                    transpose_att(prev)
                scores(1)
                if now.valid():
                    weigh_values(now, 0)
                if prev.valid():
                    out_project(prev)
                maxima(2)
                scores(1)
                maxima(2)
                scores(1)
                maxima(2)
                if now.valid():
                    weigh_values(now, 1)
                scores(1)
                if prev.valid():
                    transpose_norm(prev)
                scores(1)
                if now.valid():
                    weigh_values(now, 2)
                scores(1)
                if nxt.valid():
                    transpose_max(nxt)

            pe.wait_ge(a0_in, 16)
            over_sequences(pe, -2, step)

            pe.wait_ge(xT_copied, B)
            pe.wait_ge(exp_done, B * UNITS)
            pe.wait_ge(max_taken, B * UNITS)
            pe.wait_ge(av_copied, 2 * B)
            pe.wait_ge(ln_step, 5 * B)
            route(NT - TPB, NT).then_inc(route_ready, 1)
            pe.wait_ge(w1_in, (2 + 2 * EXP) * 16)
            pe.wait_ge(gate_step, 4)

            def transpose_gates(half):
                if half == 0:
                    pe.wait_ge(gate_step, GATE_STEPS)
                wait(pe, gateT_copied, half)
                for i in range(4):
                    n = 4 * half + i
                    last = nc.tensor.transpose(bank[7][:, i * P:(i + 1) * P], gate[:, n * TBK:(n + 1) * TBK, :]
                                               .rearrange("p n e -> p (n e)"), identf[:, :])
                last.then_inc(gateT_ready, 1)

            def up(n, e):
                x = XT[:, n * BLK:(n + 1) * BLK] if isinstance(n, int) else XT[:, bass.ds(n * BLK, BLK)]
                for c in range(HC):
                    wait(pe, gelu_done, n * (EXP * HC) + (e * HC + c - 3))
                    nc.tensor.matmul(bank[c][:, :], w1[:, expert(e), c * P:(c + 1) * P], x, start=True, stop=True).then_inc(up_ready, 1)

            def down(n, e):
                pe.wait_ge(gelu_done, n * (EXP * HC) + (e * HC + HC))
                wait(pe, acc_done, n * EXP + (e - 2))
                ps = bank[4 + e % 3]
                if e == EXP - 1:
                    pe.wait_ge(gTb_done, n + 1)
                for i in range(TBK):
                    out = ps[:, i * D:(i + 1) * D]
                    if e == EXP - 1:
                        nc.tensor.matmul(out, gTb[:, :], b2[:, i, :], start=True, stop=False, skip_group_check=True)
                    for c in range(HC):
                        last = nc.tensor.matmul(out, hid[:, e % 3, c, i * P:(i + 1) * P], w2[:, expert(e), c, :],
                                                start=(e < EXP - 1 and c == 0), stop=(c == HC - 1), skip_group_check=True)
                last.then_inc(down_ready, 1)

            def transpose_block(n):
                pe.wait_ge(xn2_done, n + 1)
                wait(pe, xT2_copied, n)
                for i in range(TBK):
                    last = nc.tensor.transpose(bank[7][:, i * P:(i + 1) * P], xn[:, i, :], identf[:, :])
                last.then_inc(xT2_ready, 1)

            def moe(n):
                if has(n):
                    up(n, 0)
                for e in range(1, EXP):
                    if has(n):
                        up(n, e)
                    if isinstance(n, int) and n == 0 and e in (3, 4):
                        transpose_gates(e - 3)
                    if e == 3 and has(n - 1):
                        transpose_block(n - 1)
                    if has(n):
                        down(n, e - 1)
                if has(n):
                    down(n, EXP - 1)
            over_blocks(pe, moe)

            pe.wait_ge(xT2_copied, NBLK)
            pe.wait_ge(acc_done, NBLK * EXP)
            pe.wait_ge(w3_in, 14 * 16)

            def project3(b, j):
                if j == 0:
                    pe.wait_ge(xt3_done, b.count(1, 1))
                if j < 10:
                    wait(pe, relu_done, b.count(16, 2 * (j - 1)) if j >= 2 else 0)
                if j < 2:
                    wait(pe, v3_done, b.count(4, -1 + j))
                if j >= 10:
                    pe.wait_ge(v3_done, b.count(4, j - 9))
                ps = bank[j % 2]
                x = xt3[:, b.rem % 2, :]
                if j < 8:
                    nc.tensor.matmul(ps[:, 0:S], wq[:, j * P:(j + 1) * P], x, start=True, stop=True)
                    last = nc.tensor.matmul(ps[:, S:2 * S], wk[:, j * P:(j + 1) * P], x, start=True, stop=True)
                else:
                    i, half = divmod(j - 8, 2)
                    last = nc.tensor.matmul(ps[:, :], x[:, i * P:(i + 1) * P], wv[:, half * 512:(half + 1) * 512],
                                            start=True, stop=True)
                last.then_inc(p3_ready, 1)

            def scores3(b, j):
                half, odd, u, pairs = unit3(j)
                pe.wait_ge(relu_done, b.count(16, 2 * pairs[-1] + 2))
                wait(pe, s3_taken, b.count(UNITS, j - 1))
                ps = bank[2 + j % 2]
                k0 = P if u == 2 else 0
                n_q = S - k0
                rows = slice(DH1 * odd, DH1 * (odd + 1))
                for n, pair in enumerate(pairs):
                    last = nc.tensor.matmul(ps[:, n * n_q:(n + 1) * n_q], QK[rows, b.rem % 2, 1, pair, k0:k0 + P],
                                            QK[rows, b.rem % 2, 0, pair, k0:S], start=True, stop=True)
                last.then_inc(s3_ready, 1)

            def weigh3(b, g):
                pe.wait_ge(s3_taken, b.count(UNITS, 6 * (g // 2) + 6))
                if g == 0:
                    pe.wait_ge(v3_done, b.count(4, 4))
                wait(pe, num_copied, b.count(HG, g))
                if g == 0:
                    wait(pe, den_step, b.count(3, -2))
                for what in range(2):
                    for k in range(TPB):
                        for r in range(HG):
                            h = HG * g + r
                            w = weights3(2 * g + r // 2, r % 2, k)
                            if what == 0:
                                rows = slice(DH1 * (r % 2), DH1 * (r % 2 + 1))
                                last = nc.tensor.matmul(bank[4][rows, (r // 2) * S + k * P:(r // 2 + 1) * S],
                                                        Vc[:, b.rem % 2, k, h, :], w, start=(k == 0 and r < 2),
                                                        stop=(k == 1), skip_group_check=True)
                            else:
                                last = nc.tensor.matmul(bank[5][32 * r:32 * r + 32, k * P:S], ones3[:, g, :], w,
                                                        start=(k == 0 and g == 0), stop=(k == 1 and g == HG - 1),
                                                        skip_group_check=True)
                    last.then_inc(num_ready, 1)

            def spread3(b, v):
                if v == 0:
                    pe.wait_ge(den_step, b.count(3, 3))
                    wait(pe, ln3_step, b.count(6, -5))
                wait(pe, att3_done, b.count(HG, v - 1))
                for i in range(2):
                    last = nc.tensor.matmul(bank[6 + v % 2][:, i * S:(i + 1) * S], spread[:, 2 * v + i, :], rec3,
                                            start=True, stop=True)
                last.then_inc(spread_ready, 1)

            def out_project3(b):
                pe.wait_ge(att3_done, b.count(HG, HG))
                for i in range(TPB):
                    for c in range(8):
                        last = nc.tensor.matmul(bank[6][:, i * D:(i + 1) * D], attT[:, c, i * P:(i + 1) * P],
                                                wo[:, c, :], start=(c == 0), stop=(c == 7), skip_group_check=True)
                last.then_inc(o3_ready, 1)

            def cosformer(b):
                nxt, prev = b.plus(1), b.plus(-1)
                for j in range(UNITS):
                    if nxt.valid():
                        project3(nxt, j)
                    if b.valid():
                        scores3(b, j)
                    if j in (0, 2) and prev.valid():
                        weigh3(prev, 2 + j // 2)
                    if 5 <= j < 9 and prev.valid():
                        spread3(prev, j - 5)
                    if j == 9 and prev.valid():
                        out_project3(prev)
                    if j in (7, 9) and b.valid():
                        weigh3(b, (j - 7) // 2)
            over_sequences(pe, -1, cosformer)

            pe.wait_ge(ln3_step, 6 * B)
            pe.wait_ge(deq_step, 4)

            def transpose4(n):
                pe.wait_ge(h_done, n.count(1, 1))
                wait(pe, hT_copied, n.count(1))
                for i in range(TBK):
                    last = nc.tensor.transpose(bank[7][:, i * P:(i + 1) * P], xn2[:, i, :], identf[:, :])
                last.then_inc(hT_ready, 1)

            def up4(n):
                pe.wait_ge(hT_copied, n.count(1, 1))
                for c in range(HC):
                    wait(pe, silu_done, n.count(HC, c - 3))
                    nc.tensor.matmul(bank[c][:, :], f1[:, c * P:(c + 1) * P], hT[:, n.rem, :],
                                     start=True, stop=True).then_inc(up4_ready, 1)

            def down4(n, half):
                if half == 0:
                    pe.wait_ge(silu_done, n.count(HC, HC))
                    wait(pe, z_step, n.count(9, -8))
                for i in (2 * half, 2 * half + 1):
                    for c in range(HC):
                        last = nc.tensor.matmul(bank[4 + n.rem][:, i * D:(i + 1) * D],
                                                yT[:, n.rem, c, i * P:(i + 1) * P], f2[:, c, :],
                                                start=(c == 0), stop=(c == HC - 1))
                if half == 1:
                    last.then_inc(down4_ready, 1)

            def ffn(n):
                nxt, prev = n.plus(1), n.plus(-1)
                if n.valid():
                    up4(n)
                if prev.valid():
                    down4(prev, 0)
                if nxt.valid():
                    transpose4(nxt)
                if prev.valid():
                    down4(prev, 1)
            over_pairs(pe, ffn)

        @block.vector
        def _(dve):
            nc.vector.memset(V0[:, :, :, :, DK0 + 1:VW], 0.0)
            nc.vector.memset(V0[:, :, :, :, DK0:DK0 + 1], 1.0)
            nc.vector.memset(nmp[:, :, :, :, :], 0.0)
            nc.vector.memset(ones3[:, :, :], 0.0).then_inc(ones_step, 1)
            dve.wait_ge(ones_step, 1)
            for g in range(HG):
                nc.vector.memset(ones3[:, g, g:g + 1], 1.0)
            nc.vector.memset(epsc[:, :], EPS)
            nc.vector.memset(mhalf[:, :], -0.5).then_inc(consts, 1)

            def pass_on():
                nc.vector.tensor_copy(beat[:, UNITS:UNITS + 1], mhalf[:, 0:1])

            def rotate(b):
                for k in range(2):
                    dve.wait_ge(proj_done, b.count(3, k + 1))
                    nc.vector.tensor_tensor(ropet[:, k], bank[6 + k][:, :].rearrange("p (a t) -> p a t", a=2),
                                            rope[:, :, :], op=ALU.mult).then_inc(rope_read, 1)
                dve.wait_ge(rope_read, b.count(2, 2))
                wait(dve, part_step, b.count(3, 0))
                nc.vector.tensor_tensor(qk[:, :, :], ropet[:, :, 0, :], ropet[:, :, 1, :], op=ALU.add).then_inc(rope_step, 1)
                dve.wait_ge(rope_step, b.count(1, 1))
                wait(dve, scr_out, b.count(96, 0))
                nc.vector.tensor_copy(parts[:, 0], qk[:, :, :]).then_inc(part1, 1)

            def take_max(b, j):
                g, u = divmod(j, 3)
                dve.wait_ge(max_ready, b.count(UNITS, j + 1))
                if j == 0:
                    wait(dve, nm_step, b.count(5, 0))
                if u == 0:
                    out, keys = nm[:, 0, 4 * g:4 * g + 4], P
                else:
                    out, keys = nm[:, 1, 4 * g + 2 * u - 2:4 * g + 2 * u], S
                nc.vector.tensor_reduce(out, bank[2 + j % 2][:, :].rearrange("p (h k) -> p h k", k=keys),
                                        axis=AX.X, op=ALU.max, negate=True).then_inc(max_taken, 1)

            def split_max(b):
                dve.wait_ge(max_taken, b.count(UNITS, UNITS))
                wait(dve, nmt_ready, b.count(1, 0))
                two = [P, TPB, 2, H0]
                nc.vector.tensor_copy(nmp[:, :, :, 0, :], nm[:, :, None, :].to_broadcast(two)).then_inc(nm_step, 1)
                dve.wait_ge(nm_step, b.count(5, 1))
                nc.vector.tensor_tensor(nmr[:, :, :], nm[:, :, :], nmp[:, :, 0, 0, :], op=ALU.subtract).then_inc(nm_step, 1)
                dve.wait_ge(nm_step, b.count(5, 2))
                nc.vector.tensor_copy(nmp[:, :, :, 1, :], nmr[:, :, None, :].to_broadcast(two)).then_inc(nm_step, 1)
                dve.wait_ge(nm_step, b.count(5, 3))
                nc.vector.tensor_tensor(nm[:, :, :], nmr[:, :, :], nmp[:, :, 0, 1, :], op=ALU.subtract).then_inc(nm_step, 1)
                dve.wait_ge(nm_step, b.count(5, 4))
                nc.vector.tensor_copy(nmp[:, :, :, 2, :], nm[:, :, None, :].to_broadcast(two)).then_inc(nm_step, 1)

            def normalise(b, a):
                dve.wait_ge(avT_ready, b.count(2, a + 1))
                av = bank[7 - a][:, :].rearrange("p (n d) -> p n d", d=VW)
                nc.vector.reciprocal(rden[:, a], av[:, :, DK0:DK0 + 1]).then_inc(rden_done, 1)
                dve.wait_ge(rden_done, b.count(2, a + 1))
                if a == 0:
                    wait(dve, attT_ready, b.count(1, 0))
                half = att0[:, :, a * D // 2:(a + 1) * D // 2].rearrange("p t (h d) -> p t h d", d=DK0)
                nc.vector.tensor_tensor(half, av[:, :, 0:DK0].rearrange("p (t h) d -> p t h d", t=TPB),
                                        rden[:, a].rearrange("p (t h) d -> p t h d", t=TPB)
                                        .to_broadcast([P, TPB, H0 // 2, DK0]), op=ALU.mult).then_inc(att_done, 1)

            def residual(b):
                if b.fixed() and b.index() == 0:
                    dve.wait_ge(x_in, 16)
                dve.wait_ge(wo_ready, b.count(1, 1))
                at = b.count(TPB)
                x = X[:, at:at + TPB, :] if b.fixed() else X[:, bass.ds(at, TPB), :]
                nc.vector.tensor_tensor(yres[:, 0:TPB, :], bank[6][:, 0:TPB * D].rearrange("p (t d) -> p t d", d=D),
                                        x, op=ALU.add).then_inc(ln_step, 1)
                dve.wait_ge(ln_step, b.count(5, 1))
                for i in range(TPB):
                    nc.vector.bn_stats(bst[:, i, :], yres[:, i, :]).then_inc(ln_step, 1)
                dve.wait_ge(ln_step, b.count(5, 3))
                pass_on()
                for i in range(TPB):
                    nc.vector.bn_aggr(mv[:, i, :], bst[:, i, :]).then_inc(ln_step, 1)

            def apply_norm(b):
                dve.wait_ge(rstd_step, b.count(2, 2))
                wait(dve, xT_ready, b.count(1, 0))
                wait(dve, xn_kept, b.count(1, 0))
                for i in range(TPB):
                    last = nc.vector.tensor_scalar(xn[:, i, :], yres[:, i, :], mv[:, i, 0:1], rstd[:, i:i + 1],
                                                   ALU.subtract, ALU.mult)
                last.then_inc(xn_done, 1)

            def step(b):
                nxt, nxt2, prev = b.plus(1), b.plus(2), b.plus(-1)
                if nxt2.valid():
                    rotate(nxt2)
                for j in range(UNITS):
                    if j in (2, 4) and prev.valid():
                        normalise(prev, j // 2 - 1)
                    if j == 7 and prev.valid():
                        residual(prev)
                    if nxt.valid():
                        take_max(nxt, j)
                    if j == 9 and prev.valid():
                        apply_norm(prev)
                if nxt.valid():
                    split_max(nxt)

            dve.wait_ge(rope_in, 16)
            over_sequences(dve, -2, step)

            steps = [0]

            def gated(ins):
                steps[0] += 1
                ins.then_inc(gate_step, 1)
                dve.wait_ge(gate_step, steps[0])

            def every(ap):
                return ap.rearrange("p (n o) -> p n o", o=1).to_broadcast([P, NT, NE])

            logits = bank[2][:, 0:NT * NE].rearrange("p (n e) -> p n e", e=NE)
            ranks = rank[:, None, :].to_broadcast([P, NT, NE])
            gated(nc.vector.memset(gate[:, :, :], 0.0))
            gated(nc.vector.memset(gate[:, :, 0:1], 1.0))
            dve.wait_ge(route_ready, 1)
            gated(nc.vector.tensor_reduce(gmax, logits, axis=AX.X, op=ALU.max))
            gated(nc.vector.tensor_tensor(probs, logits, every(gmax), op=ALU.subtract))
            dve.wait_ge(gate_exp, 1)
            gated(nc.vector.tensor_reduce(gsum, prb2, axis=AX.X, op=ALU.add))
            gated(nc.vector.reciprocal(grec, gsum))
            gated(nc.vector.tensor_tensor(probs, prb2, every(grec), op=ALU.mult))
            for p, top, wm, sel in ((probs, top1, wmax, sel1), (prb2, top2, wmax2, sel2)):
                gated(nc.vector.tensor_reduce(top, p, axis=AX.X, op=ALU.max))
                gated(nc.vector.tensor_tensor(ge, p, every(top), op=ALU.is_ge))
                gated(nc.vector.tensor_tensor(wt, ge, ranks, op=ALU.mult))
                gated(nc.vector.tensor_reduce(wm, wt, axis=AX.X, op=ALU.max))
                gated(nc.vector.tensor_tensor(sel, wt, every(wm), op=ALU.is_equal))
                if sel is sel1:
                    gated(nc.vector.scalar_tensor_tensor(prb2, sel1, -4.0, probs, op0=ALU.mult, op1=ALU.add))
            gated(nc.vector.tensor_tensor(tsum, top1, top2, op=ALU.add))
            gated(nc.vector.reciprocal(trec, tsum))
            gated(nc.vector.tensor_tensor(ge, sel1, every(top1), op=ALU.mult))
            gated(nc.vector.tensor_tensor(wt, sel2, every(top2), op=ALU.mult))
            gated(nc.vector.tensor_tensor(probs, ge, wt, op=ALU.add))
            gated(nc.vector.tensor_tensor(gate[:, :, 1:EXP], probs, every(trec), op=ALU.mult))
            assert steps[0] == GATE_STEPS

            def block_of(n):
                return X[:, n * TBK:(n + 1) * TBK, :] if isinstance(n, int) else X[:, bass.ds(n * TBK, TBK), :]

            def accumulate(n, e):
                dve.wait_ge(down_ready, n * EXP + (e + 1))
                ps = bank[4 + e % 3]
                if e == EXP - 1:
                    dve.wait_ge(acc_done, n * EXP + e)
                    nc.vector.tensor_tensor(yres[:, :, :], ps[:, :].rearrange("p (t d) -> p t d", d=D), yres[:, :, :],
                                            op=ALU.add).then_inc(acc_done, 1)
                    return
                if e == 0:
                    wait(dve, xn2_done, n)
                else:
                    dve.wait_ge(acc_done, n * EXP + e)
                for i in range(TBK):
                    if e > 0:
                        base = yres[:, i, :]
                    elif isinstance(n, int):
                        base = X[:, n * TBK + i, :]
                    else:
                        base = X[:, bass.ds(n * TBK + i, 1), :].rearrange("p o d -> p (o d)")
                    last = nc.vector.scalar_tensor_tensor(yres[:, i, :], ps[:, i * D:(i + 1) * D],
                                                          gb[:, i, e + 1:e + 2], base, op0=ALU.mult, op1=ALU.add)
                last.then_inc(acc_done, 1)

            def moe(n):
                if not has(n):
                    return
                wait(dve, acc_done, n * EXP)
                g = gate[:, n * TBK:(n + 1) * TBK, 0:EXP] if isinstance(n, int) else gate[:, bass.ds(n * TBK, TBK), 0:EXP]
                nc.vector.tensor_copy(gb[:, :, :], g).then_inc(gb_done, 1)
                dve.wait_ge(gb_done, n + 1)
                for e in range(EXP):
                    accumulate(n, e)
                dve.wait_ge(acc_done, n * EXP + EXP)
                for i in range(TBK):
                    nc.vector.bn_stats(bst[:, i, :], yres[:, i, :]).then_inc(ln2_step, 1)
                dve.wait_ge(ln2_step, n * 8 + 4)
                pass_on()
                for i in range(TBK):
                    nc.vector.bn_aggr(mv[:, i, :], bst[:, i, :]).then_inc(ln2_step, 1)
                dve.wait_ge(rstd2_step, n * 2 + 2)
                wait(dve, xT2_ready, n)
                wait(dve, xn2_kept, n)
                for i in range(TBK):
                    last = nc.vector.tensor_scalar(xn[:, i, :], yres[:, i, :], mv[:, i, 0:1], rstd[:, i:i + 1],
                                                   ALU.subtract, ALU.mult)
                last.then_inc(xn2_done, 1)
            dve.wait_ge(xn_kept, B)
            over_blocks(dve, moe)

            dve.wait_ge(w3_in, 14 * 16)
            dve.wait_ge(deq_step, 4)
            dve.wait_ge(xn2_kept, NBLK)

            def add_bias3(b, u):
                dve.wait_ge(p3_ready, b.count(UNITS, u + 9))
                if u == 0:
                    wait(dve, num_ready, b.count(8, -8))
                i, half = divmod(u, 2)
                out = Vc[:, b.rem % 2, i, half * 8:(half + 1) * 8, :].rearrange("p h d -> p (h d)")
                nc.vector.tensor_tensor(out, bank[u % 2][:, :], bv[:, half * 512:(half + 1) * 512],
                                        op=ALU.add).then_inc(v3_done, 1)

            def weight3(b, j):
                dve.wait_ge(s3_ready, b.count(UNITS, j + 1))
                half, odd, u, pairs = unit3(j)
                if j % 6 == 0:
                    wait(dve, num_ready, b.count(8, 4 * half - 4))
                if u == 2:
                    shape, tab = [P, 4, P], dtab[:, 0:P]
                else:
                    shape, tab = [P, 2, S], dtab[:, :]
                nc.vector.tensor_tensor(ET[:, j, :].rearrange("p (h q) -> p h q", h=shape[1]),
                                        bank[2 + j % 2][:, :].rearrange("p (h q) -> p h q", h=shape[1]),
                                        tab[:, None, :].to_broadcast(shape), op=ALU.mult).then_inc(s3_taken, 1)

            def divide3(b, g):
                dve.wait_ge(num_copied, b.count(HG, g + 1))
                dve.wait_ge(spread_ready, b.count(HG, g + 1))
                if g == 0:
                    wait(dve, o3_ready, b.count(1, 0))
                nc.vector.tensor_tensor(attT[:, 2 * g:2 * g + 2, :].rearrange("p c t -> p (c t)"),
                                        num[:, 2 * g:2 * g + 2, :].rearrange("p c t -> p (c t)"), bank[6 + g % 2][:, :],
                                        op=ALU.mult).then_inc(att3_done, 1)

            def invert3(b, half):
                q = slice(half * P, (half + 1) * P)
                if half == 0:
                    dve.wait_ge(num_ready, b.count(8, 8))
                    wait(dve, spread_ready, b.count(HG, 0))
                    nc.vector.tensor_scalar(den3, bank[5][:, 0:S], 1e-6, None, ALU.max).then_inc(den_step, 1)
                    dve.wait_ge(den_step, b.count(3, 1))
                nc.vector.reciprocal(rec3[:, q], den3[:, q]).then_inc(den_step, 1)

            def residual3(b):
                dve.wait_ge(o3_ready, b.count(1, 1))
                at = b.count(TPB)
                x = X[:, at:at + TPB, :] if b.fixed() else X[:, bass.ds(at, TPB), :]
                wait(dve, xn3_done, b.count(1, 0))
                nc.vector.tensor_tensor(yres[:, 0:TPB, :], bank[6][:, 0:TPB * D].rearrange("p (t d) -> p t d", d=D),
                                        x, op=ALU.add).then_inc(ln3_step, 1)
                dve.wait_ge(ln3_step, b.count(6, 1))
                nc.vector.tensor_tensor(yres[:, 0:TPB, :], yres[:, 0:TPB, :],
                                        bo[:, None, :].to_broadcast([P, TPB, D]), op=ALU.add).then_inc(ln3_step, 1)
                dve.wait_ge(ln3_step, b.count(6, 2))
                for i in range(TPB):
                    nc.vector.bn_stats(bst[:, i, :], yres[:, i, :]).then_inc(ln3_step, 1)
                dve.wait_ge(ln3_step, b.count(6, 4))
                pass_on()
                for i in range(TPB):
                    nc.vector.bn_aggr(mv[:, i, :], bst[:, i, :]).then_inc(ln3_step, 1)

            def apply3(b):
                dve.wait_ge(rstd3_step, b.count(2, 2))
                at = b.count(TPB)
                for i in range(TPB):
                    x = X[:, at + i, :] if b.fixed() else X[:, bass.ds(at + i, 1), :].rearrange("p o d -> p (o d)")
                    last = nc.vector.tensor_scalar(x, yres[:, i, :], mv[:, i, 0:1], rstd[:, i:i + 1],
                                                   ALU.subtract, ALU.mult)
                last.then_inc(xn3_done, 1)

            def cosformer(b):
                nxt, prev, prev2 = b.plus(1), b.plus(-1), b.plus(-2)
                for j in range(UNITS):
                    if b.valid():
                        weight3(b, j)
                    if j == 0 and prev2.valid():
                        apply3(prev2)
                    if j in (3, 4) and prev.valid():
                        invert3(prev, j - 3)
                    if 5 <= j < 9 and prev.valid():
                        divide3(prev, j - 5)
                    if j >= 8 and nxt.valid():
                        add_bias3(nxt, j - 8)
                if prev.valid():
                    residual3(prev)
            over_sequences(dve, -1, cosformer)
            apply3(Batch(0, B - 1).plus(0))

            dve.wait_ge(xn3_done, B)

            dve.wait_ge(num_ready, 8 * B)
            dve.wait_ge(o3_ready, B)

            def tile4(n, i):
                at = n.count(TBK, i)
                return X[:, at, :] if n.fixed() else X[:, bass.ds(at, 1), :].rearrange("p o d -> p (o d)")

            def moments(n):
                wait(dve, h_done, n.count(1))
                for i in range(TBK):
                    nc.vector.bn_stats(bst4[:, i, :], tile4(n, i)).then_inc(pre_step, 1)
                dve.wait_ge(pre_step, n.count(8, 4))
                pass_on()
                for i in range(TBK):
                    nc.vector.bn_aggr(mv4[:, i, :], bst4[:, i, :]).then_inc(pre_step, 1)

            def apply_pre(n):
                dve.wait_ge(prstd_step, n.count(2, 2))
                wait(dve, hT_ready, n.count(1))
                for i in range(TBK):
                    last = nc.vector.tensor_scalar(xn2[:, i, :], tile4(n, i), mv4[:, i, 0:1], rstd4[:, i:i + 1],
                                                   ALU.subtract, ALU.mult)
                last.then_inc(h_done, 1)

            def residual4(n):
                dve.wait_ge(down4_ready, n.count(1, 1))
                dve.wait_ge(base_step, n.count(2, 2))
                wait(dve, xo_done, n.count(1))
                nc.vector.scalar_tensor_tensor(yo[:, :, :], bank[4 + n.rem][:, :].rearrange("p (t d) -> p t d", d=D), 0.5,
                                               base4[:, n.rem], op0=ALU.mult, op1=ALU.add).then_inc(z_step, 1)
                dve.wait_ge(z_step, n.count(9, 1))
                for i in range(TBK):
                    nc.vector.bn_stats(bst[:, i, :], yo[:, i, :]).then_inc(z_step, 1)
                dve.wait_ge(z_step, n.count(9, 5))
                pass_on()
                for i in range(TBK):
                    nc.vector.bn_aggr(mv[:, i, :], bst[:, i, :]).then_inc(z_step, 1)

            def apply_last(n):
                dve.wait_ge(rstd4_step, n.count(2, 2))
                wait(dve, out_done, n.count(16))
                for i in range(TBK):
                    last = nc.vector.tensor_scalar(xn[:, i, :], yo[:, i, :], mv[:, i, 0:1], rstd[:, i:i + 1],
                                                   ALU.subtract, ALU.mult)
                last.then_inc(xo_done, 1)

            def ffn(n):
                nxt2, prev = n.plus(2), n.plus(-1)
                if prev.valid():
                    residual4(prev)
                if nxt2.valid():
                    moments(nxt2)
                if prev.valid():
                    apply_last(prev)
                if nxt2.valid():
                    apply_pre(nxt2)
            over_pairs(dve, ffn)

        @block.scalar
        def _(act):
            def load_later(b):
                part = {-1: 0, 0: 1, 1: 2, 14: 3, 15: 4}.get(b.index() if b.fixed() else None)
                if part is None:
                    return
                if part == 0:
                    act.dma_start(b1[:, :, :], t["b1"]).then_inc(w1_in, 16)
                for e in range(2 * part, min(2 * part + 2, EXP)):
                    act.dma_start(w1[:, e, :], t["w1s"] if e == 0 else t["w1"][e - 1]).then_inc(w1_in, 16)
                    act.dma_start(w2[:, e], (t["w2s"] if e == 0 else t["w2"][e - 1])
                                  .rearrange("(c p) n -> p c n", p=P)).then_inc(w1_in, 16)

            def exponentials(b, j):
                act.wait_ge(sc_ready, b.count(UNITS, j + 1))
                if j % 3 == 0:
                    wait(act, av_ready, b.count(4, j // 3 - 3))
                nc.scalar.activation(ET[:, j, :], bank[j % 2][:, :], ACT.Exp, scale=DK0 ** -0.5).then_inc(exp_done, 1)

            def copy_values(b):
                act.wait_ge(proj_done, b.count(3, 3))
                wait(act, av_ready, b.count(4, -12))
                nc.scalar.activation(V0[:, b.rem, :, :, 0:DK0],
                                     bank[6][:, 0:TPB * D].rearrange("p (t h d) -> p t h d", t=TPB, d=DK0),
                                     ACT.Copy).then_inc(v_copied, 1)

            def copy_av(b, a):
                act.wait_ge(av_ready, b.count(4, 2 * a + 2))
                wait(act, avT_ready, b.count(2, a - 1))
                nc.scalar.activation(av0[:, a], bank[4 + a][:, :], ACT.Copy).then_inc(av_copied, 1)

            def second_part(b):
                act.wait_ge(part_step, b.count(3, 1))
                nc.scalar.activation(parts[:, 1], rem1[:, :, :], ACT.Copy).then_inc(part_step, 1)

            def copy_att(b):
                act.wait_ge(attT_ready, b.count(1, 1))
                wait(act, wo_ready, b.count(1, 0))
                nc.scalar.activation(attT0[:, :], bank[7][:, 0:S], ACT.Copy).then_inc(attT_copied, 1)

            def copy_tokens(b):
                act.wait_ge(xT_ready, b.count(1, 1))
                at = b.count(S)
                x = XT[:, at:at + S] if b.fixed() else XT[:, bass.ds(at, S)]
                nc.scalar.activation(x, bank[7][:, 0:S], ACT.Copy).then_inc(xT_copied, 1)

            def copy_max(b):
                act.wait_ge(nmt_ready, b.count(1, 1))
                nc.scalar.activation(nmt[:, :], bank[6][:, 0:S // 2].bitcast(BF16), ACT.Copy).then_inc(nmt_copied, 1)

            def step(b):
                nxt, nxt2, prev = b.plus(1), b.plus(2), b.plus(-1)
                for j in range(UNITS):
                    if j == 3 and nxt2.valid():
                        copy_values(nxt2)
                    if j == 5 and nxt2.valid():
                        second_part(nxt2)
                    if j == 6 and prev.valid():
                        copy_att(prev)
                    if j == 10 and prev.valid():
                        copy_tokens(prev)
                    if b.valid():
                        exponentials(b, j)
                    if j == 1 and prev.valid():
                        copy_av(prev, 1)
                    if j == 9 and b.valid():
                        copy_av(b, 0)
                if nxt.valid():
                    copy_max(nxt)
                load_later(b)

            act.wait_ge(consts, 1)
            over_sequences(act, -2, step)

            act.wait_ge(gate_step, 4)
            nc.scalar.activation(prb2, probs, ACT.Exp).then_inc(gate_exp, 1)

            def moe(n):
                for e in range(EXP):
                    if has(n):
                        for c in range(HC):
                            act.wait_ge(up_ready, n * (EXP * HC) + (e * HC + c + 1))
                            if c == 0:
                                wait(act, down_ready, n * EXP + (e - 2))
                            nc.scalar.activation(hid[:, e % 3, c, :], bank[c][:, :], ACT.Gelu_apprx_tanh,
                                                 bias=b1[:, expert(e), c:c + 1]).then_inc(gelu_done, 1)
                    if isinstance(n, int) and n == 0 and e in (3, 4):
                        half = e - 3
                        act.wait_ge(gateT_ready, half + 1)
                        nc.scalar.activation(gateT[:, 4 * half:4 * half + 4, :].rearrange("p n t -> p (n t)"),
                                             bank[7][:, :], ACT.Copy).then_inc(gateT_copied, 1)
                    if e == 3 and has(n - 1):
                        act.wait_ge(xT2_ready, n)
                        m = n - 1
                        x = XT[:, m * BLK:(m + 1) * BLK] if isinstance(m, int) else XT[:, bass.ds(m * BLK, BLK)]
                        nc.scalar.activation(x, bank[7][:, :], ACT.Copy).then_inc(xT2_copied, 1)
            over_blocks(act, moe)

            def cosformer(b):
                nxt, prev = b.plus(1), b.plus(-1)

                def copy_num(b, g):
                    act.wait_ge(num_ready, b.count(8, 2 * g + 2))
                    wait(act, att3_done, b.count(HG, g - 3))
                    nc.scalar.activation(num[:, 2 * g:2 * g + 2, :].rearrange("p c t -> p (c t)"), bank[4][:, :], ACT.Copy).then_inc(num_copied, 1)

                for j in range(UNITS):
                    if j < 8 and nxt.valid():
                        act.wait_ge(p3_ready, nxt.count(UNITS, j + 1))
                        if j == 0:
                            wait(act, s3_ready, nxt.count(UNITS, -UNITS))
                        for k, bias in enumerate((bq, bk)):
                            nc.scalar.activation(QK[:, nxt.rem % 2, k, j, :], bank[j % 2][:, k * S:(k + 1) * S],
                                                 ACT.Relu, bias=bias[:, j:j + 1]).then_inc(relu_done, 1)
                    if j in (0, 2) and prev.valid():
                        copy_num(prev, 2 + j // 2)
                    if j in (7, 9) and b.valid():
                        copy_num(b, (j - 7) // 2)
            over_sequences(act, -1, cosformer)

            def ffn(n):
                nxt = n.plus(1)
                if n.valid():
                    for c in range(HC):
                        act.wait_ge(up4_ready, n.count(HC, c + 1))
                        if c == 0:
                            wait(act, down4_ready, n.count(1, -1))
                        nc.scalar.activation(yT[:, n.rem, c, :], bank[c][:, :], ACT.Silu,
                                             bias=fb1[:, c:c + 1]).then_inc(silu_done, 1)
                if nxt.valid():
                    act.wait_ge(hT_ready, nxt.count(1, 1))
                    wait(act, up4_ready, nxt.count(HC, -HC))
                    nc.scalar.activation(hT[:, nxt.rem, :], bank[7][:, :], ACT.Identity,
                                         bias=bet[:, :], scale=gam[:, :]).then_inc(hT_copied, 1)
            over_pairs(act, ffn)

        @block.gpsimd
        def _(pool):
            zero = pool.to_reg(0.0)

            def split(b):
                pool.wait_ge(part1, b.count(1, 1))
                nc.gpsimd.tensor_tensor(rem1[:, :, :], qk[:, :, :], parts[:, 0], op=ALU.subtract).then_inc(part_step, 1)
                pool.wait_ge(part_step, b.count(3, 2))
                nc.gpsimd.tensor_tensor(parts[:, 2], rem1[:, :, :], parts[:, 1], op=ALU.subtract).then_inc(part_step, 1)

            def select(b, j):
                pool.wait_ge(exp_done, b.count(UNITS, j + 1))
                nc.gpsimd.tensor_tensor(beat[:, j:j + 1], mhalf[:, 0:1], mhalf[:, 0:1], op=ALU.add)
                if j % 3 == 2:
                    e, n = ET[:, j, :].rearrange("p (h q) -> p h q", q=P), 4
                else:
                    e, n = ET[:, j, :].rearrange("p (h q) -> p h q", q=S)[:, :, 0:P], 2
                nc.gpsimd.affine_select(out=e, in_=e, compare_op=ALU.is_ge, fill=zero, base=0,
                                        pattern=[[0, n], [1, P]], channel_multiplier=-1).then_inc(sel_done, 1)

            def deviation(b):
                pool.wait_ge(ln_step, b.count(5, 5))
                nc.gpsimd.tensor_tensor(veps[:, 0:TPB], mv[:, 0:TPB, 1], epsc[:, 0:TPB], op=ALU.add).then_inc(rstd_step, 1)
                pool.wait_ge(rstd_step, b.count(2, 1))
                nc.gpsimd.tensor_tensor(rstd[:, 0:TPB], veps[:, 0:TPB], mhalf[:, 0:TPB], op=ALU.pow).then_inc(rstd_step, 1)

            def keep(b):
                pool.wait_ge(xn_done, b.count(1, 1))
                at = b.count(TPB)
                x = X[:, at:at + TPB, :] if b.fixed() else X[:, bass.ds(at, TPB), :]
                nc.gpsimd.tensor_copy(x, xn[:, 0:TPB, :]).then_inc(xn_kept, 1)

            def step(b):
                nxt2, prev = b.plus(2), b.plus(-1)
                for j in range(UNITS):
                    if b.valid():
                        select(b, j)
                    if j == 3 and nxt2.valid():
                        split(nxt2)
                    if j == 7 and prev.valid():
                        deviation(prev)
                    if j == 10 and prev.valid():
                        keep(prev)

            pool.wait_ge(consts, 1)
            over_sequences(pool, -2, step)

            pool.wait_ge(fq_in, 64)
            for a in range(2):
                nc.gpsimd.tensor_scalar(fd[:, a], fq[:, a], -128.0, None, ALU.add).then_inc(deq_step, 1)
                pool.wait_ge(deq_step, 2 * a + 1)
                w = f1[:, :] if a == 0 else f2[:, :, :].rearrange("p c n -> p (c n)")
                nc.gpsimd.tensor_tensor(w, fd[:, a], fs[:, a], op=ALU.mult).then_inc(deq_step, 1)

            def deviations(ready, at, step_sem, tiles, base, mv=mv, veps=veps, rstd=rstd):
                pool.wait_ge(ready, at)
                nc.gpsimd.tensor_tensor(veps[:, 0:tiles], mv[:, 0:tiles, 1], epsc[:, 0:tiles], op=ALU.add).then_inc(step_sem, 1)
                pool.wait_ge(step_sem, base + 1)
                nc.gpsimd.tensor_tensor(rstd[:, 0:tiles], veps[:, 0:tiles], mhalf[:, 0:tiles], op=ALU.pow).then_inc(step_sem, 1)

            def moe(n):
                if has(n):
                    wait(pool, down_ready, n * EXP)
                    if isinstance(n, int) and n == 0:
                        pool.wait_ge(gateT_copied, 2)
                    g = gateT[:, n, :] if isinstance(n, int) else gateT[:, bass.ds(n, 1), :].rearrange("p o t -> p (o t)")
                    nc.gpsimd.tensor_copy(gTb[:, :], g).then_inc(gTb_done, 1)
                    deviations(ln2_step, n * 8 + 8, rstd2_step, TBK, n * 2)
                    pool.wait_ge(xn2_done, n + 1)
                    x = X[:, n * TBK:(n + 1) * TBK, :] if isinstance(n, int) else X[:, bass.ds(n * TBK, TBK), :]
                    nc.gpsimd.tensor_copy(x, xn[:, :, :]).then_inc(xn2_kept, 1)
            over_blocks(pool, moe)

            pool.wait_ge(xT2_copied, NBLK)

            def cosformer(b):
                nxt2, prev = b.plus(2), b.plus(-1)
                if nxt2.valid():
                    wait(pool, p3_ready, nxt2.count(UNITS, -UNITS))
                    at = nxt2.count(S)
                    x = XT[:, at:at + S] if nxt2.fixed() else XT[:, bass.ds(at, S)]
                    nc.gpsimd.tensor_copy(xt3[:, nxt2.rem % 2, :], x).then_inc(xt3_done, 1)
                if prev.valid():
                    deviations(ln3_step, prev.count(6, 6), rstd3_step, TPB, prev.count(2, 0))
            over_sequences(pool, -2, cosformer)

            pool.wait_ge(xn3_done, B)
            pool.wait_ge(num_ready, 8 * B)
            nc.gpsimd.tensor_tensor(half_bias[:, :], fb2[:, :], mhalf[:, 0:1].to_broadcast([P, D]), op=ALU.mult).then_inc(bias_step, 1)

            def twice(n):
                at = n.count(TBK)
                x = X[:, at:at + TBK, :] if n.fixed() else X[:, bass.ds(at, TBK), :]
                wait(pool, z_step, n.count(9, -8))
                nc.gpsimd.tensor_tensor(base4[:, n.rem], x, x, op=ALU.add).then_inc(base_step, 1)
                pool.wait_ge(base_step, n.count(2, 1))
                nc.gpsimd.tensor_tensor(base4[:, n.rem], base4[:, n.rem], half_bias[:, None, :].to_broadcast([P, TBK, D]),
                                        op=ALU.subtract).then_inc(base_step, 1)

            def ffn(n):
                nxt2, prev = n.plus(2), n.plus(-1)
                if prev.valid():
                    deviations(z_step, prev.count(9, 9), rstd4_step, TBK, prev.count(2))
                if nxt2.valid():
                    deviations(pre_step, nxt2.count(8, 8), prstd_step, TBK, nxt2.count(2), mv4, veps4, rstd4)
                if n.valid():
                    if n.fixed() and n.index() == 0:
                        pool.wait_ge(bias_step, 1)
                    twice(n)
            over_pairs(pool, ffn)


def constants():
    bf16 = mybir.dt.np(BF16)
    half = DK0 // 2
    inv = np.float32(10000.0) ** (np.float32(-2.0) * np.arange(half, dtype=np.float32) / np.float32(DK0))
    ang = np.arange(S, dtype=np.float32)[None, :] * inv[:, None]
    d = np.arange(P) % DK0
    sign = np.where(d % 2 == 0, -1.0, 1.0)[:, None]
    rope = np.stack([np.cos(ang)[d // 2], sign * np.sin(ang)[d // 2]], 1).astype(np.float32)
    at = np.arange(P)
    mask = np.where(at[None, :] <= at[:, None], 0.0, BIG).astype(bf16)
    oneh = np.zeros((P, H0, P))
    for s in range(NS):
        for h in range(H0):
            oneh[H0 * s + h, h] = 1.0
    apart = np.arange(S)[None, :] - at[:, None]
    dtab = np.where(apart >= 0, np.cos(np.pi / (2.0 * S) * apart), 0.0).astype(np.float32)
    spread = np.zeros((P, 8, P), np.float32)
    for h in range(H1):
        spread[32 * (h % 4) + h // 4, h // 2, DH1 * (h % 2):DH1 * (h % 2 + 1)] = 1.0
    rank = np.broadcast_to(np.arange(NE, 0, -1, dtype=np.float32), (P, NE))
    return {"rope": rope, "identf": np.eye(P, dtype=np.float32), "identb": np.eye(P).astype(bf16), "maskb": mask,
            "oneh": oneh.astype(bf16), "dtab": dtab, "rank": np.ascontiguousarray(rank), "spread": spread}


def layout(i):
    x = i["L0_attn_x"].reshape(N, D)
    swap = np.arange(D) ^ 1
    a0 = [i["L0_attn_wq"], i["L0_attn_wq"][swap], i["L0_attn_wk"], i["L0_attn_wk"][swap], i["L0_attn_wv"], i["L0_attn_wo"]]
    b1 = np.concatenate([i["L0_ffn_bfc_s"][None], i["L0_ffn_bfc"]]).reshape(EXP, HC, P).transpose(2, 0, 1)
    b2 = np.zeros((TBK, 32, TBK, D), np.float32)
    for k in range(TBK):
        b2[k, 0, k] = i["L0_ffn_bproj_s"]
        b2[k, 1:EXP, k] = i["L0_ffn_bproj"]
    return {
        "x": x, "xT": x.T, "a0": np.stack([w.T for w in a0], 1),
        "wr": i["L0_ffn_Wr"], "w1s": i["L0_ffn_Wfc_s"], "w1": i["L0_ffn_Wfc"], "w2s": i["L0_ffn_Wproj_s"],
        "w2": i["L0_ffn_Wproj"], "b1": b1, "b2": b2.reshape(P, TBK, D),
        "wq": i["L1_attn_Wq"], "wk": i["L1_attn_Wk"], "wv": i["L1_attn_Wv"], "wo": i["L1_attn_Wo"],
        "bq": i["L1_attn_bq"].reshape(8, P).T, "bk": i["L1_attn_bk"].reshape(8, P).T,
        "bv": i["L1_attn_bv"], "bo": i["L1_attn_bo"],
        "fc1_q": i["L1_ffn_fc1_q"], "fc2_q": i["L1_ffn_fc2_q"], "fc1_scales": i["L1_ffn_fc1_scales"].reshape(-1),
        "fc2_scales": i["L1_ffn_fc2_scales"].reshape(-1), "fb1": i["L1_ffn_fc1_bias"].reshape(HC, P).T,
        "fb2": i["L1_ffn_fc2_bias"], "gam": i["L1_ffn_ln_gamma"].reshape(D, 1), "bet": i["L1_ffn_ln_beta"].reshape(D, 1),
    }


def kernel(**inputs):
    import concourse.bacc as bacc
    from concourse.bass_utils import run_bass_kernel_spmd

    given = layout({k: np.asarray(v) for k, v in inputs.items()}) | constants()
    given = {k: np.ascontiguousarray(v) for k, v in given.items()}
    nc = bacc.Bacc("TRN2", target_bir_lowering=False, num_devices=1)
    t = {k: nc.dram_tensor(f"in_{k}", v.shape, mybir.dt.from_np(v.dtype), kind="ExternalInput").ap()
         for k, v in given.items()}
    t["out"] = nc.dram_tensor("out", (N, D), F32, kind="ExternalOutput").ap()
    build(nc, t)
    r = run_bass_kernel_spmd(nc, [{f"in_{k}": v for k, v in given.items()}], core_ids=[0])
    return r.results[0]["out"].reshape(B, S, D)
```

```python
from contextlib import ExitStack

import numpy as np

import concourse.bass as bass
from concourse import mybir

F32 = mybir.dt.float32
BF16 = mybir.dt.bfloat16
F32R = mybir.dt.float32r
I32 = mybir.dt.int32
ALU = mybir.AluOpType
ACT = mybir.ActivationFunctionType
AX = mybir.AxisListType

P = 128
D = 128
B, S = 16, 256
N = B * S
NT = N // P
TPB = S // P
H0, DK0 = 16, 8
NS = 3
SLOTS = 6
KST = SLOTS * DK0
VW = 32
NE, HID = 8, 512
EXP = NE + 1
HC = HID // P
H1, DH1 = 16, 64
BLK = 512
NBLK = N // BLK
TBK = BLK // P
EPS = 1e-5
BIG = -1e30
UNITS = 12
GRP = 4
HG = 4
GATE_STEPS = 24
ARENA2 = -(-(NT * 32 + NBLK * P + 6 * NT * NE + 9 * NT + TBK * EXP + P + TBK * D) // 64) * 64


class Batch:

    def __init__(self, quad, rem, of=4, total=B):
        self.quad, self.rem, self.of, self.total = quad, rem, of, total

    def plus(self, k):
        r = self.rem + k
        return Batch(self.quad + r // self.of, r % self.of, self.of, self.total)

    def count(self, per, k=0):
        return self.quad * (self.of * per) + (self.rem * per + k)

    def fixed(self):
        return isinstance(self.quad, int)

    def index(self):
        return self.of * self.quad + self.rem if self.fixed() else None

    def valid(self):
        return not self.fixed() or 0 <= self.index() < self.total


def over_blocks(eng, step, tail=True):
    step(0)
    with eng.Fori(1, NBLK) as n:
        step(n)
    if tail:
        step(NBLK)


def has(n):
    return not isinstance(n, int) or 0 <= n < NBLK


def wait(eng, sem, value):
    if not isinstance(value, int) or value > 0:
        eng.wait_ge(sem, value)


def over_sequences(eng, first, step, end=B + 1):
    for b in range(first, 2):
        step(Batch(b // 4, b % 4))
    loops = (B - 4) // 4
    with eng.Fori(0, loops) as i:
        for r in range(4):
            step(Batch(i, 2 + r).plus(0))
    for b in range(2 + 4 * loops, end):
        step(Batch(b // 4, b % 4))


def over_pairs(eng, step):
    for n in range(1, 2):
        step(block4(n))
    loops = (NBLK - 4) // 2
    with eng.Fori(0, loops) as i:
        for k in range(2, 4):
            step(Batch(i, 0, 2, NBLK).plus(k))
    for n in range(2 + 2 * loops, NBLK + 1):
        step(block4(n))


def block4(n):
    return Batch(n // 2, n % 2, 2, NBLK)


def expert(k):
    return (k + 1) % EXP


def build(nc, t):
    ctx = ExitStack()
    with ctx:
        def sb(name, shape, dt=F32):
            return ctx.enter_context(nc.sbuf_tensor(name, shape, dt))

        def sem(name):
            return ctx.enter_context(nc.semaphore(name))

        bank = [ctx.enter_context(nc.psum_tensor(f"bank{i}", [P, 512], F32)) for i in range(8)]
        X = sb("X", [P, NT, D])
        XT = sb("XT", [P, N])
        b1 = sb("b1", [P, EXP, HC])
        wq = sb("wq", [P, H1 * DH1])
        wk = sb("wk", [P, H1 * DH1])
        wv = sb("wv", [P, H1 * DH1])
        wo = sb("wo", [P, 8, D])
        bq = sb("bq", [P, 8])
        bk = sb("bk", [P, 8])
        bv = sb("bv", [P, H1 * DH1])
        bo = sb("bo", [P, D])
        a0 = sb("a0", [P, 6, D])
        rope = sb("rope", [P, 2, S])
        identf = sb("identf", [P, P])
        identb = sb("identb", [P, P], BF16)
        maskb = sb("maskb", [P, P], BF16)
        oneh = sb("oneh", [P, H0, P], BF16)
        dtab = sb("dtab", [P, S])
        rank = sb("rank", [P, NE])
        wr = sb("wr", [P, NE])
        arenaB = sb("arenaB", [P, 6144])
        arenaC = sb("arenaC", [P, 2 * TPB * H1 * DH1])
        Vc = arenaC[:, :].rearrange("p (r t h d) -> p r t h d", r=2, t=TPB, h=H1)

        def carve(arena):
            at = [0]

            def piece(words, dt=F32):
                at[0] += words
                ap = arena[:, at[0] - words:at[0]]
                return ap if dt is F32 else ap.bitcast(dt)
            return piece
        pieceC, pieceB = carve(arenaC), carve(arenaB)
        pieceB3 = carve(arenaB)
        attT = pieceB3(8 * S).rearrange("p (c t) -> p c t", c=8)
        num = pieceB3(8 * S).rearrange("p (c t) -> p c t", c=8)
        den3, rec3 = pieceB3(S), pieceB3(S)
        PRODUCTS = ((0, 0), (0, 1), (1, 0))
        spread = pieceB3(8 * P).rearrange("p (c n) -> p c n", c=8)

        def unit3(j):
            half, k = divmod(j, 6)
            u = k // 2
            return half, k % 2, u, range(4 * half, 4 * half + 4) if u == 2 else range(4 * half + 2 * u, 4 * half + 2 * u + 2)

        def weights3(pair, odd, k):
            half, q = divmod(pair, 4)
            if k == 0:
                return ET3[:, 6 * half + 2 * (q // 2) + odd, (q % 2) * S:(q % 2 + 1) * S]
            return ET3[:, 6 * half + 4 + odd, q * P:(q + 1) * P]

        den_step = sem("den_step")
        spread_ready = sem("spread_ready")
        ones3 = sb("ones3", [P, HG, 32])
        f1 = sb("f1", [P, HID])
        f2 = sb("f2", [P, HC, D])
        fb1 = sb("fb1", [P, HC])
        fb2 = sb("fb2", [P, D])
        gam = sb("gam", [P, 1])
        bet = sb("bet", [P, 1])
        pieceC4 = carve(arenaC)
        fq = pieceC4(2 * HID, I32).rearrange("p (a n) -> p a n", a=2)
        fs = pieceC4(2 * HID).rearrange("p (a n) -> p a n", a=2)
        fd = pieceC4(2 * HID).rearrange("p (a n) -> p a n", a=2)
        bst4 = sb("bst4", [P, TBK, 6])
        mv4 = sb("mv4", [P, TBK, 2])
        veps4 = sb("veps4", [P, TBK])
        rstd4 = sb("rstd4", [P, TBK])
        xb = pieceC(2 * S).rearrange("p (r t) -> p r t", r=2)
        ropet = pieceC(4 * S).rearrange("p (k a t) -> p k a t", k=2, a=2)
        qk = pieceC(2 * S).rearrange("p (k t) -> p k t", k=2)
        rem1 = pieceC(2 * S).rearrange("p (k t) -> p k t", k=2)
        parts = pieceC(NS * S, BF16).rearrange("p (s k t) -> p s k t", s=NS, k=2)
        V0 = pieceB(4 * TPB * H0 * VW).rearrange("p (r t h d) -> p r t h d", r=4, t=TPB, h=H0)
        av0 = pieceB(2 * 512).rearrange("p (a n) -> p a n", a=2)
        nm = sb("nm", [P, TPB, H0])
        nmr = sb("nmr", [P, TPB, H0])
        nmp = sb("nmp", [P, TPB, 2, 4, H0], BF16)
        nmt = sb("nmt", [P, 2, S], BF16)
        rden = sb("rden", [P, 2, H0, 1])
        att0 = pieceB(TPB * D).rearrange("p (t d) -> p t d", t=TPB)
        attT0 = pieceB(S)
        yres = sb("yres", [P, TBK, D])
        bst = sb("bst", [P, TBK, 6])
        mv = sb("mv", [P, TBK, 2])
        veps = sb("veps", [P, TBK])
        rstd = sb("rstd", [P, TBK])
        mhalf = sb("mhalf", [P, TBK])
        epsc = sb("epsc", [P, TBK])
        beat = sb("beat", [P, UNITS + 1])
        xn = sb("xn", [P, TBK, D])

        with ExitStack() as stage1:
            def sb1(name, shape, dt=F32):
                return stage1.enter_context(nc.sbuf_tensor(name, shape, dt))
            arenaA = sb1("arenaA", [P, 8192])
            ET = sb1("ET", [P, UNITS, 512])
            w1 = sb1("w1", [P, EXP, HID])
        with ExitStack() as stage2:
            def sb2(name, shape, dt=F32):
                return stage2.enter_context(nc.sbuf_tensor(name, shape, dt))
            arena2 = sb2("arena2", [P, ARENA2])
            xp = sb2("xp", [P, 2, BLK], F32R)
            w1_coarse = sb2("w1_coarse", [P, EXP, HID], F32R)
            sb2("unused", [P, 8192 + UNITS * 512 - ARENA2 - 2 * BLK - EXP * HID])
            w1_fine = sb2("w1_fine", [P, EXP, HID], F32R)
            w2 = sb2("w2", [P, EXP, HC, D])
        w1p = (w1_coarse, w1_fine)
        arenaA3 = sb("arenaA3", [P, 8192])
        ET3 = sb("ET3", [P, UNITS, 512])
        wide = H1 * DH1
        wqkv0 = sb("wqkv0", [P, 3, wide], F32R)
        wqkv = [wqkv0, sb("wqkv1", [P, 3, wide], F32R)]
        spread_r = sb("spread_r", [P, 8, P], F32R)
        xt3 = sb("xt3", [P, 2, 2, S], F32R)
        recs = sb("recs", [P, 2, S], F32R)
        piece2 = carve(arena2)
        gate = piece2(NT * 32).rearrange("p (n e) -> p n e", e=32)
        gateT = piece2(NBLK * P).rearrange("p (n t) -> p n t", t=P)
        probs, ge, wt, sel1, sel2, prb2 = (piece2(NT * NE).rearrange("p (n e) -> p n e", e=NE) for _ in range(6))
        gmax, gsum, grec, top1, top2, wmax, wmax2, tsum, trec = (piece2(NT) for _ in range(9))
        hid = arenaB[:, :].rearrange("p (r c t) -> p r c t", r=3, c=HC)
        gb = piece2(TBK * EXP).rearrange("p (n e) -> p n e", e=EXP)
        gTb = piece2(P)
        b2 = piece2(TBK * D).rearrange("p (i d) -> p i d", d=D)
        QK = arenaA3[:, :].rearrange("p (r k c t) -> p r k c t", r=2, k=2, c=8)
        stack = arenaA[:, :].bitcast(BF16).rearrange("p (r k h t) -> p r k h t", r=4, k=2, h=8)

        piece4 = carve(arenaA3)
        hT = piece4(2 * BLK).rearrange("p (r t) -> p r t", r=2)
        yT = piece4(2 * HC * BLK).rearrange("p (r c t) -> p r c t", r=2, c=HC)
        xn2 = piece4(BLK).rearrange("p (t d) -> p t d", d=D)
        base4 = piece4(2 * BLK).rearrange("p (r t d) -> p r t d", r=2, d=D)
        yo = piece4(BLK).rearrange("p (t d) -> p t d", d=D)
        half_bias = piece4(D)

        scr = nc.dram_tensor("scr", (2, 2, NS, DK0, H0, S), BF16).ap()

        a0_in = sem("a0_in")
        rope_in = sem("rope_in")
        w_in = sem("w_in")
        wr_in = sem("wr_in")
        x_in = sem("x_in")
        xb_in = [sem("xb_in0"), sem("xb_in1")]
        w1_in = sem("w1_in")
        w3_in = sem("w3_in")
        w4_in = sem("w4_in")
        consts = sem("consts")
        proj_done = sem("proj_done")
        rope_read = sem("rope_read")
        rope_step = sem("rope_step")
        part1 = sem("part1")
        part_step = sem("part_step")
        scr_out = sem("scr_out")
        stack_in = [sem(f"stack_in{i}") for i in range(4)]
        v_copied = sem("v_copied")
        max_ready = sem("max_ready")
        max_taken = sem("max_taken")
        nm_step = sem("nm_step")
        nmt_ready = sem("nmt_ready")
        nmt_copied = sem("nmt_copied")
        sc_ready = sem("sc_ready")
        exp_done = sem("exp_done")
        sel_done = sem("sel_done")
        av_ready = sem("av_ready")
        rden_done = sem("rden_done")
        att_done = sem("att_done")
        av_copied = sem("av_copied")
        avT_ready = sem("avT_ready")
        attT_ready = sem("attT_ready")
        attT_copied = sem("attT_copied")
        wo_ready = sem("wo_ready")
        ln_step = sem("ln_step")
        rstd_step = sem("rstd_step")
        xn_done = sem("xn_done")
        xn_kept = sem("xn_kept")
        xT_ready = sem("xT_ready")
        xT_copied = sem("xT_copied")
        out_done = sem("out_done")
        route_ready = sem("route_ready")
        gate_step = sem("gate_step")
        gate_exp = sem("gate_exp")
        gateT_ready = sem("gateT_ready")
        gateT_copied = sem("gateT_copied")
        gTb_done = sem("gTb_done")
        gb_done = sem("gb_done")
        up_ready = sem("up_ready")
        gelu_done = sem("gelu_done")
        down_ready = sem("down_ready")
        acc_done = sem("acc_done")
        ln2_step = sem("ln2_step")
        rstd2_step = sem("rstd2_step")
        xn2_done = sem("xn2_done")
        xn2_kept = sem("xn2_kept")
        xT2_ready = sem("xT2_ready")
        xT2_copied = sem("xT2_copied")
        xt3_done = sem("xt3_done")
        w_coarse = sem("w_coarse")
        w1_split = sem("w1_split")
        w1_fined = sem("w1_fined")
        b2_in = sem("b2_in")
        xp_done = sem("xp_done")
        w_fine = sem("w_fine")
        wv_fine = sem("wv_fine")
        ones_step = sem("ones_step")
        p3_ready = sem("p3_ready")
        relu_done = sem("relu_done")
        v3_done = sem("v3_done")
        s3_ready = sem("s3_ready")
        s3_taken = sem("s3_taken")
        num_ready = sem("num_ready")
        num_copied = sem("num_copied")
        att3_done = sem("att3_done")
        o3_ready = sem("o3_ready")
        ln3_step = sem("ln3_step")
        rstd3_step = sem("rstd3_step")
        xn3_done = sem("xn3_done")
        fq_in = sem("fq_in")
        deq_step = sem("deq_step")
        pre_step = sem("pre_step")
        prstd_step = sem("prstd_step")
        h_done = sem("h_done")
        bias_step = sem("bias_step")
        base_step = sem("base_step")
        hT_ready = sem("hT_ready")
        hT_copied = sem("hT_copied")
        up4_ready = sem("up4_ready")
        silu_done = sem("silu_done")
        down4_ready = sem("down4_ready")
        z_step = sem("z_step")
        rstd4_step = sem("rstd4_step")
        xo_done = sem("xo_done")

        block = ctx.enter_context(nc.Block())

        @block.sync
        def _(sp):
            def load_block(b):
                if not b.valid():
                    return
                wait(sp, proj_done, b.plus(-2).count(3, 3) if not b.fixed() or b.index() >= 2 else 0)
                at = b.count(S)
                src = t["xT"][:, at:at + S] if b.fixed() else t["xT"][:, bass.ds(at, S)]
                sp.dma_start(xb[:, b.rem % 2, :], src).then_inc(xb_in[b.rem % 2], 16)

            sp.dma_start(a0[:, :, :], t["a0"]).then_inc(a0_in, 16)
            load_block(Batch(0, 0))
            sp.dma_start(rope[:, :, :], t["rope"]).then_inc(rope_in, 16)
            load_block(Batch(0, 1))
            for dst, name in ((wr, "wr"), (rank, "rank")):
                sp.dma_start(dst[:, :], t[name]).then_inc(wr_in, 16)
            for dst, name in ((identb, "identb"), (maskb, "maskb"), (oneh, "oneh"), (identf, "identf")):
                sp.dma_start(dst[:, :, :] if dst is oneh else dst[:, :], t[name]).then_inc(w_in, 16)
            def step(b):
                n2 = b.plus(2)
                if not b.fixed() or b.index() >= 0:
                    load_block(n2)
                if n2.valid():
                    slot = n2.rem % 2
                    wait(sp, part_step, n2.count(3, 3))
                    for k in range(2):
                        for s in range(NS):
                            if (k, s) == (1, NS - 1):
                                wait(sp, sc_ready, b.plus(-2).count(UNITS, UNITS) if not b.fixed() or b.index() >= 2 else 0)
                            at = s if k == 0 else NS - 1 - s
                            sp.dma_start(scr[slot, k, at].rearrange("d h t -> h d t"),
                                         parts[:, s, k, :]).then_inc(scr_out, 16)
                    wait(sp, scr_out, n2.count(96, 96))
                    for k in range(2):
                        src = scr[slot, k].rearrange("s d (q h) t -> q (s d) h t", q=2)
                        for q in range(2):
                            row = 64 * q
                            for n in (3, 2, 1):
                                f = 0 if k == 0 else NS - n
                                sp.dma_start(stack[row:row + n * DK0, n2.rem, k, :, :],
                                             src[q, f * DK0:(f + n) * DK0]).then_inc(stack_in[n2.rem], 16)
                                row += n * DK0
                if b.fixed() and b.index() == -2:
                    sp.dma_start(X[:, :, :], t["x"].rearrange("(n p) d -> p n d", p=P)).then_inc(x_in, 16)
            over_sequences(sp, -2, step)
            for dst, name in ((wq, "wq"), (wk, "wk"), (wv, "wv"), (bq, "bq"), (bk, "bk"), (dtab, "dtab"),
                              (fb1, "fb1"), (gam, "gam"), (bet, "bet")):
                sp.dma_start(dst[:, :], t[name]).then_inc(w3_in, 16)
            sp.dma_start(wo[:, :, :], t["wo"].rearrange("(c p) n -> p c n", p=P)).then_inc(w3_in, 16)
            for dst, name in ((bv, "bv"), (bo, "bo"), (fb2, "fb2")):
                sp.dma_start(dst[:, :], t[name].partition_broadcast(P)).then_inc(w3_in, 16)
            sp.wait_ge(sc_ready, UNITS * B)
            sp.wait_ge(max_ready, UNITS * B)
            sp.dma_start(b2, t["b2"]).then_inc(b2_in, 16)
            sp.wait_ge(xT_copied, B)
            sp.dma_start(fq[:, 0, :], t["fc1_q"]).then_inc(fq_in, 16)
            sp.dma_start(fq[:, 1, :].rearrange("p (c n) -> p c n", c=HC),
                         t["fc2_q"].rearrange("(c p) n -> p c n", p=P)).then_inc(fq_in, 16)
            sp.dma_start(fs[:, 0, :], t["fc1_scales"].partition_broadcast(P)).then_inc(fq_in, 16)
            sp.dma_start(fs[:, 1, :], t["fc2_scales"].partition_broadcast(P)).then_inc(fq_in, 16)

            sp.wait_ge(acc_done, NBLK * EXP)
            sp.dma_start(spread, t["spread"]).then_inc(w3_in, 16)

            def store(n):
                if has(n):
                    sp.wait_ge(xo_done, n + 1)
                    out = t["out"].rearrange("(n p) d -> p n d", p=P)
                    out = out[:, n * TBK:(n + 1) * TBK, :] if isinstance(n, int) else out[:, bass.ds(n * TBK, TBK), :]
                    sp.dma_start(out, xn[:, :, :]).then_inc(out_done, 16)
            over_blocks(sp, store)
            sp.wait_ge(out_done, NBLK * 16)

        @block.tensor
        def _(pe):
            def head_rows(h):
                lo = 64 * (h // 8)
                return slice(lo, lo + KST), h % 8

            def project(b):
                x = xb[:, b.rem % 2, :]
                if b.fixed():
                    wait(pe, v_copied, b.count(1, 0))
                    wait(pe, rope_read, b.count(2, 0))
                pe.wait_ge(xb_in[b.rem % 2], (b.quad * 2 + b.rem // 2) * 16 + 16)
                wait(pe, nmt_copied, b.count(1, -1))
                nc.tensor.matmul(bank[6][:, 0:S], a0[:, 0, :], x, start=True, stop=True)
                nc.tensor.matmul(bank[6][:, S:2 * S], a0[:, 1, :], x, start=True, stop=True).then_inc(proj_done, 1)
                wait(pe, xT_copied, b.count(1, -3))
                nc.tensor.matmul(bank[7][:, 0:S], a0[:, 2, :], x, start=True, stop=True)
                nc.tensor.matmul(bank[7][:, S:2 * S], a0[:, 3, :], x, start=True, stop=True).then_inc(proj_done, 1)
                pe.wait_ge(rope_read, b.count(2, 1))
                for i in range(TPB):
                    last = nc.tensor.matmul(bank[6][:, i * D:(i + 1) * D], x[:, i * P:(i + 1) * P], a0[:, 4, :],
                                            start=True, stop=True)
                last.then_inc(proj_done, 1)

            def max_unit(b, j):
                if b.fixed() and b.index() == 0 and j == 0:
                    pe.wait_ge(w_in, 64)
                if j == 0:
                    pe.wait_ge(stack_in[b.rem], (b.quad + 1) * 192)
                g, u = divmod(j, 3)
                ps = bank[2 + j % 2]
                wait(pe, max_taken, b.count(UNITS, j - 1))
                heads = range(4 * g, 4 * g + 4) if u == 0 else range(4 * g + 2 * u - 2, 4 * g + 2 * u)
                keys = P if u == 0 else S
                q0 = 0 if u == 0 else P
                for n, h in enumerate(heads):
                    rows, hp = head_rows(h)
                    nc.tensor.matmul(ps[:, n * keys:(n + 1) * keys], stack[rows, b.rem, 0, hp, q0:q0 + P],
                                     stack[rows, b.rem, 1, hp, 0:keys], start=(n == 0), stop=False,
                                     skip_group_check=True)
                diag = ps[:, :].rearrange("p (h k) -> p h k", k=keys)[:, :, keys - P:keys]
                nc.tensor.matmul(diag, identb[:, :], maskb[:, None, :].to_broadcast([P, len(heads), P]),
                                 start=False, stop=True, skip_group_check=True).then_inc(max_ready, 1)

            def score_unit(b, j):
                if j == 0:
                    pe.wait_ge(stack_in[b.rem], (b.quad + 1) * 192)
                    pe.wait_ge(nmt_copied, b.count(1, 1))
                g, u = divmod(j, 3)
                ps = bank[j % 2]
                wait(pe, exp_done, b.count(UNITS, j - 1))
                heads = range(4 * g, 4 * g + 4) if u == 2 else range(4 * g + 2 * u, 4 * g + 2 * u + 2)
                k0 = P if u == 2 else 0
                n_q = S - k0
                for n, h in enumerate(heads):
                    rows, hp = head_rows(h)
                    nc.tensor.matmul(ps[:, n * n_q:(n + 1) * n_q], stack[rows, b.rem, 1, hp, k0:k0 + P],
                                     stack[rows, b.rem, 0, hp, k0:S], start=(n == 0), stop=False,
                                     skip_group_check=True)
                    last = nc.tensor.matmul(ps[:, n * n_q:(n + 1) * n_q], oneh[:, h, :], nmt[:, b.rem % 2, k0:S],
                                            start=False, stop=True, skip_group_check=True)
                last.then_inc(sc_ready, 1)

            def weigh_values(b, g):
                pe.wait_ge(sel_done, b.count(UNITS, 3 * g + 3))
                if g == 0:
                    pe.wait_ge(v_copied, b.count(1, 1))
                if g % 2 == 0:
                    wait(pe, av_copied, b.count(2, g // 2 - 1))
                out = bank[4 + g // 2][:, (g % 2) * S:(g % 2 + 1) * S]
                v = V0[:, b.rem]
                for r in range(HG):
                    h = HG * g + r
                    q = slice(VW * r, VW * (r + 1))
                    nc.tensor.matmul(out[q, :], v[:, 0, h, :], ET[:, 3 * g + r // 2, (r % 2) * S:(r % 2 + 1) * S],
                                     start=(g % 2 == 0), stop=False, skip_group_check=True)
                for r in range(HG):
                    h = HG * g + r
                    q = slice(VW * r, VW * (r + 1))
                    last = nc.tensor.matmul(out[q, P:S], v[:, 1, h, :], ET[:, 3 * g + 2, r * P:(r + 1) * P],
                                            start=False, stop=True, skip_group_check=True)
                last.then_inc(av_ready, 1)

            def transpose_values(b, a):
                pe.wait_ge(av_copied, b.count(2, a + 1))
                if a == 0:
                    pe.wait_ge(rope_read, b.plus(3).count(2, 2) if b.plus(3).valid() else 2 * B)
                else:
                    pe.wait_ge(v_copied, b.plus(3).count(1, 1) if b.plus(3).valid() else B)
                for g in range(2):
                    for i in range(TPB):
                        at = (i * 2 + g) * P
                        last = nc.tensor.transpose(bank[7 - a][:, at:at + P],
                                                   av0[:, a, g * S + i * P:g * S + (i + 1) * P], identf[:, :])
                last.then_inc(avT_ready, 1)

            def transpose_max(b):
                pe.wait_ge(nm_step, b.count(5, 5))
                wait(pe, ln_step, b.count(5, -9))
                if b.fixed():
                    wait(pe, v_copied, min(b.index() + 2, B))
                ps = bank[6][:, 0:S // 2].bitcast(BF16)
                for i in range(TPB):
                    last = nc.tensor.transpose(ps[:, i * P:(i + 1) * P],
                                               nmp[:, i].rearrange("p a s h -> p (a s h)"), identb[:, :])
                last.then_inc(nmt_ready, 1)

            def transpose_att(b):
                pe.wait_ge(att_done, b.count(2, 2))
                for i in range(TPB):
                    last = nc.tensor.transpose(bank[7][:, i * P:(i + 1) * P], att0[:, i, :], identf[:, :])
                last.then_inc(attT_ready, 1)

            def out_project(b):
                pe.wait_ge(attT_copied, b.count(1, 1))
                for i in range(TPB):
                    last = nc.tensor.matmul(bank[6][:, i * D:(i + 1) * D], attT0[:, i * P:(i + 1) * P], a0[:, 5, :],
                                            start=True, stop=True)
                last.then_inc(wo_ready, 1)

            def transpose_norm(b):
                pe.wait_ge(xn_done, b.count(1, 1))
                for i in range(TPB):
                    last = nc.tensor.transpose(bank[7][:, i * P:(i + 1) * P], xn[:, i, :], identf[:, :])
                last.then_inc(xT_ready, 1)

            def route(first, end):
                if first == 0:
                    pe.wait_ge(wr_in, 32)
                    pe.wait_ge(max_taken, B * UNITS)
                pe.wait_ge(xT_copied, -(-end // TPB))
                for i in range(first, end):
                    last = nc.tensor.matmul(bank[2][:, i * NE:(i + 1) * NE], XT[:, i * P:(i + 1) * P], wr[:, :],
                                            start=True, stop=True)
                return last

            def step(b):
                now, nxt, nxt2, prev = b, b.plus(1), b.plus(2), b.plus(-1)
                done = {"s": 0, "m": 0}

                def scores(n):
                    for _ in range(n):
                        if now.valid():
                            score_unit(now, done["s"])
                        if b.fixed() and b.index() == B - 1:
                            early = NT - 2 * TPB
                            route(early * done["s"] // UNITS, early * (done["s"] + 1) // UNITS)
                        done["s"] += 1

                def maxima(n):
                    for _ in range(n):
                        if nxt.valid():
                            max_unit(nxt, done["m"])
                        done["m"] += 1

                scores(2)
                if prev.valid():
                    weigh_values(prev, 3)
                scores(1)
                if nxt2.valid():
                    project(nxt2)
                maxima(1)
                if prev.valid():
                    transpose_values(prev, 0)
                scores(1)
                maxima(1)
                scores(1)
                maxima(2)
                if prev.valid():
                    transpose_values(prev, 1)
                maxima(1)
                scores(1)
                maxima(1)
                if prev.valid():
                    transpose_att(prev)
                scores(1)
                maxima(1)
                if now.valid():
                    weigh_values(now, 0)
                if prev.valid():
                    out_project(prev)
                scores(1)
                maxima(1)
                scores(1)
                maxima(1)
                scores(1)
                maxima(2)
                if now.valid():
                    weigh_values(now, 1)
                scores(1)
                maxima(1)
                if prev.valid():
                    transpose_norm(prev)
                if now.valid():
                    weigh_values(now, 2)
                if nxt.valid():
                    transpose_max(nxt)
                scores(1)

            pe.wait_ge(a0_in, 16)
            over_sequences(pe, -2, step, end=B)

            last_b = Batch(0, B - 1).plus(0)
            weigh_values(last_b, 3)
            route(NT - 2 * TPB, NT - TPB)
            transpose_values(last_b, 0)
            transpose_values(last_b, 1)
            transpose_att(last_b)
            out_project(last_b)
            transpose_norm(last_b)
            route(NT - TPB, NT).then_inc(route_ready, 1)

            pe.wait_ge(exp_done, B * UNITS)
            pe.wait_ge(av_copied, 2 * B)
            pe.wait_ge(ln_step, 5 * B)

            def transpose_gates(half):
                if half == 0:
                    pe.wait_ge(gate_step, GATE_STEPS)
                wait(pe, gateT_copied, half)
                for i in range(4):
                    n = 4 * half + i
                    last = nc.tensor.transpose(bank[7][:, i * P:(i + 1) * P], gate[:, n * TBK:(n + 1) * TBK, :]
                                               .rearrange("p n e -> p (n e)"), identf[:, :])
                last.then_inc(gateT_ready, 1)

            def up(n, e):
                if e == 0:
                    pe.wait_ge(xp_done, 2 * n + 2)
                if isinstance(n, int) and n == 0:
                    pe.wait_ge(w1_fined, e + 1)
                for c in range(HC):
                    wait(pe, gelu_done, n * (EXP * HC) + (e * HC + c - 3))
                    if isinstance(n, int) and n == 0 and (e, c) == (0, 2):
                        pe.wait_ge(gate_step, 4)
                    for k, (v, u) in enumerate(PRODUCTS):
                        last = nc.tensor.matmul(bank[c][:, :], w1p[v][:, e, c * P:(c + 1) * P], xp[:, u, :],
                                                start=(k == 0), stop=(k == 2))
                    last.then_inc(up_ready, 1)

            def down(n, e):
                pe.wait_ge(gelu_done, n * (EXP * HC) + (e * HC + HC))
                wait(pe, acc_done, n * EXP + (e - 2))
                ps = bank[4 + e % 3]
                if e == EXP - 1:
                    pe.wait_ge(gTb_done, n + 1)
                    if isinstance(n, int) and n == 0:
                        pe.wait_ge(b2_in, 16)
                for i in range(TBK):
                    out = ps[:, i * D:(i + 1) * D]
                    if e == EXP - 1:
                        nc.tensor.matmul(out, gTb[:, :], b2[:, i, :], start=True, stop=False, skip_group_check=True)
                    for c in range(HC):
                        last = nc.tensor.matmul(out, hid[:, e % 3, c, i * P:(i + 1) * P], w2[:, e, c, :],
                                                start=(e < EXP - 1 and c == 0), stop=(c == HC - 1), skip_group_check=True)
                last.then_inc(down_ready, 1)

            def transpose_block(n):
                pe.wait_ge(xn2_done, n + 1)
                wait(pe, xT2_copied, n)
                for i in range(TBK):
                    last = nc.tensor.transpose(bank[7][:, i * P:(i + 1) * P], xn[:, i, :], identf[:, :])
                last.then_inc(xT2_ready, 1)

            def moe(n):
                if has(n):
                    up(n, 0)
                for e in range(1, EXP):
                    if has(n):
                        up(n, e)
                    if isinstance(n, int) and n == 0 and e in (3, 4):
                        transpose_gates(e - 3)
                    if e == 3 and has(n - 1):
                        transpose_block(n - 1)
                    if has(n):
                        down(n, e - 1)
                if has(n):
                    down(n, EXP - 1)
            over_blocks(pe, moe, tail=False)

            pe.wait_ge(w_coarse, 3)
            pe.wait_ge(w_fine, 2)
            pe.wait_ge(gelu_done, NBLK * EXP * HC)

            def project3(b, j):
                if j == 0:
                    pe.wait_ge(xt3_done, b.count(2, 2))
                if j < 10:
                    wait(pe, relu_done, b.count(16, 2 * (j - 1)) if j >= 2 else 0)
                if j < 2:
                    wait(pe, v3_done, b.count(4, -1 + j))
                if j >= 10:
                    pe.wait_ge(v3_done, b.count(4, j - 9))
                ps = bank[j % 2]
                x = xt3[:, b.rem % 2]
                if j < 8:
                    for k in range(2):
                        for n, (v, u) in enumerate(PRODUCTS):
                            last = nc.tensor.matmul(ps[:, k * S:(k + 1) * S], wqkv[v][:, k, j * P:(j + 1) * P],
                                                    x[:, u, :], start=(n == 0), stop=(n == 2))
                else:
                    if b.fixed() and b.index() == 0 and j == 8:
                        pe.wait_ge(wv_fine, 1)
                    i, half = divmod(j - 8, 2)
                    for n, (v, u) in enumerate(PRODUCTS):
                        last = nc.tensor.matmul(ps[:, :], x[:, u, i * P:(i + 1) * P],
                                                wqkv[v][:, 2, half * 512:(half + 1) * 512], start=(n == 0), stop=(n == 2))
                last.then_inc(p3_ready, 1)

            def scores3(b, j):
                half, odd, u, pairs = unit3(j)
                pe.wait_ge(relu_done, b.count(16, 2 * pairs[-1] + 2))
                wait(pe, s3_taken, b.count(UNITS, j - 1))
                ps = bank[2 + j % 2]
                k0 = P if u == 2 else 0
                n_q = S - k0
                rows = slice(DH1 * odd, DH1 * (odd + 1))
                for n, pair in enumerate(pairs):
                    last = nc.tensor.matmul(ps[:, n * n_q:(n + 1) * n_q], QK[rows, b.rem % 2, 1, pair, k0:k0 + P],
                                            QK[rows, b.rem % 2, 0, pair, k0:S], start=True, stop=True)
                last.then_inc(s3_ready, 1)

            def weigh3(b, g):
                pe.wait_ge(s3_taken, b.count(UNITS, 6 * (g // 2) + 6))
                if g == 0:
                    pe.wait_ge(v3_done, b.count(4, 4))
                wait(pe, num_copied, b.count(HG, g))
                if g == 0:
                    wait(pe, den_step, b.count(7, -6))
                for what in range(2):
                    for k in range(TPB):
                        for r in range(HG):
                            h = HG * g + r
                            w = weights3(2 * g + r // 2, r % 2, k)
                            if what == 0:
                                rows = slice(DH1 * (r % 2), DH1 * (r % 2 + 1))
                                last = nc.tensor.matmul(bank[4][rows, (r // 2) * S + k * P:(r // 2 + 1) * S],
                                                        Vc[:, b.rem % 2, k, h, :], w, start=(k == 0 and r < 2),
                                                        stop=(k == 1), skip_group_check=True)
                            else:
                                last = nc.tensor.matmul(bank[5][32 * r:32 * r + 32, k * P:S], ones3[:, g, :], w,
                                                        start=(k == 0 and g == 0), stop=(k == 1 and g == HG - 1),
                                                        skip_group_check=True)
                    last.then_inc(num_ready, 1)

            def spread3(b, v):
                if v == 0:
                    pe.wait_ge(den_step, b.count(7, 7))
                    wait(pe, ln3_step, b.count(6, -5))
                wait(pe, att3_done, b.count(HG, v - 1))
                for i in range(2):
                    for part in range(2):
                        last = nc.tensor.matmul(bank[6 + v % 2][:, i * S:(i + 1) * S],
                                                spread_r[:, 2 * v + i, :], recs[:, part, :],
                                                start=(part == 0), stop=(part == 1))
                last.then_inc(spread_ready, 1)

            def out_project3(b):
                pe.wait_ge(att3_done, b.count(HG, HG))
                for i in range(TPB):
                    for c in range(8):
                        last = nc.tensor.matmul(bank[6][:, i * D:(i + 1) * D], attT[:, c, i * P:(i + 1) * P],
                                                wo[:, c, :], start=(c == 0), stop=(c == 7), skip_group_check=True)
                last.then_inc(o3_ready, 1)

            def cosformer(b, beside={}):
                nxt, prev = b.plus(1), b.plus(-1)
                for j in range(UNITS):
                    if j in beside:
                        beside[j]()
                    if nxt.valid():
                        project3(nxt, j)
                    if b.valid():
                        scores3(b, j)
                    if j in (0, 2) and prev.valid():
                        weigh3(prev, 2 + j // 2)
                    if 6 <= j < 10 and prev.valid():
                        spread3(prev, j - 6)
                    if j == 10 and prev.valid():
                        out_project3(prev)
                    if j in (7, 9) and b.valid():
                        weigh3(b, (j - 7) // 2)
            cosformer(Batch(-1, 3))
            transpose_block(NBLK - 1)
            pe.wait_ge(xT2_copied, NBLK)
            pe.wait_ge(acc_done, NBLK * EXP)
            pe.wait_ge(w_coarse, 4)
            over_sequences(pe, 0, cosformer, end=B)

            def transpose4(n):
                pe.wait_ge(h_done, n.count(1, 1))
                wait(pe, hT_copied, n.count(1))
                for i in range(TBK):
                    last = nc.tensor.transpose(bank[7][:, i * P:(i + 1) * P], xn2[:, i, :], identf[:, :])
                last.then_inc(hT_ready, 1)

            def up4(n):
                pe.wait_ge(hT_copied, n.count(1, 1))
                for c in range(HC):
                    wait(pe, silu_done, n.count(HC, c - 3))
                    nc.tensor.matmul(bank[c][:, :], f1[:, c * P:(c + 1) * P], hT[:, n.rem, :],
                                     start=True, stop=True).then_inc(up4_ready, 1)

            def down4(n, half):
                if half == 0:
                    pe.wait_ge(silu_done, n.count(HC, HC))
                    wait(pe, z_step, n.count(9, -8))
                for i in (2 * half, 2 * half + 1):
                    for c in range(HC):
                        last = nc.tensor.matmul(bank[4 + n.rem][:, i * D:(i + 1) * D],
                                                yT[:, n.rem, c, i * P:(i + 1) * P], f2[:, c, :],
                                                start=(c == 0), stop=(c == HC - 1))
                if half == 1:
                    last.then_inc(down4_ready, 1)

            def ffn(n):
                nxt, prev = n.plus(1), n.plus(-1)
                if n.valid():
                    up4(n)
                if prev.valid():
                    down4(prev, 0)
                if nxt.valid():
                    transpose4(nxt)
                if prev.valid():
                    down4(prev, 1)

            pe.wait_ge(relu_done, 16 * B)
            pe.wait_ge(v3_done, 4 * B)
            pe.wait_ge(s3_taken, UNITS * B)
            pe.wait_ge(att3_done, HG * (B - 1))
            pe.wait_ge(deq_step, 4)
            cosformer(Batch(B // 4, 0), {3: lambda: transpose4(block4(0)), 5: lambda: up4(block4(0))})
            transpose4(block4(1))
            pe.wait_ge(num_copied, HG * B)
            over_pairs(pe, ffn)

        @block.vector
        def _(dve):
            nc.vector.memset(V0[:, :, :, :, DK0 + 1:VW], 0.0)
            nc.vector.memset(V0[:, :, :, :, DK0:DK0 + 1], 1.0)
            nc.vector.memset(nmp[:, :, :, :, :], 0.0)
            nc.vector.memset(ones3[:, :, :], 0.0).then_inc(ones_step, 1)
            dve.wait_ge(ones_step, 1)
            for g in range(HG):
                nc.vector.memset(ones3[:, g, g:g + 1], 1.0)
            nc.vector.memset(epsc[:, :], EPS)
            nc.vector.memset(mhalf[:, :], -0.5).then_inc(consts, 1)

            def pass_on():
                nc.vector.tensor_copy(beat[:, UNITS:UNITS + 1], mhalf[:, 0:1])

            def rotate(b):
                for k in range(2):
                    dve.wait_ge(proj_done, b.count(3, k + 1))
                    nc.vector.tensor_tensor(ropet[:, k], bank[6 + k][:, :].rearrange("p (a t) -> p a t", a=2),
                                            rope[:, :, :], op=ALU.mult).then_inc(rope_read, 1)
                dve.wait_ge(rope_read, b.count(2, 2))
                wait(dve, part_step, b.count(3, 0))
                nc.vector.tensor_tensor(qk[:, :, :], ropet[:, :, 0, :], ropet[:, :, 1, :], op=ALU.add).then_inc(rope_step, 1)
                dve.wait_ge(rope_step, b.count(1, 1))
                wait(dve, scr_out, b.count(96, 0))
                nc.vector.tensor_copy(parts[:, 0], qk[:, :, :]).then_inc(part1, 1)

            def take_max(b, j):
                g, u = divmod(j, 3)
                dve.wait_ge(max_ready, b.count(UNITS, j + 1))
                if j == 0:
                    wait(dve, nm_step, b.count(5, 0))
                if u == 0:
                    out, keys = nm[:, 0, 4 * g:4 * g + 4], P
                else:
                    out, keys = nm[:, 1, 4 * g + 2 * u - 2:4 * g + 2 * u], S
                nc.vector.tensor_reduce(out, bank[2 + j % 2][:, :].rearrange("p (h k) -> p h k", k=keys),
                                        axis=AX.X, op=ALU.max, negate=True).then_inc(max_taken, 1)

            def split_max(b):
                dve.wait_ge(max_taken, b.count(UNITS, UNITS))
                wait(dve, nmt_ready, b.count(1, 0))
                two = [P, TPB, 2, H0]
                nc.vector.tensor_copy(nmp[:, :, :, 0, :], nm[:, :, None, :].to_broadcast(two)).then_inc(nm_step, 1)
                dve.wait_ge(nm_step, b.count(5, 1))
                nc.vector.tensor_tensor(nmr[:, :, :], nm[:, :, :], nmp[:, :, 0, 0, :], op=ALU.subtract).then_inc(nm_step, 1)
                dve.wait_ge(nm_step, b.count(5, 2))
                nc.vector.tensor_copy(nmp[:, :, :, 1, :], nmr[:, :, None, :].to_broadcast(two)).then_inc(nm_step, 1)
                dve.wait_ge(nm_step, b.count(5, 3))
                nc.vector.tensor_tensor(nm[:, :, :], nmr[:, :, :], nmp[:, :, 0, 1, :], op=ALU.subtract).then_inc(nm_step, 1)
                dve.wait_ge(nm_step, b.count(5, 4))
                nc.vector.tensor_copy(nmp[:, :, :, 2, :], nm[:, :, None, :].to_broadcast(two)).then_inc(nm_step, 1)

            def normalise(b, a):
                dve.wait_ge(avT_ready, b.count(2, a + 1))
                av = bank[7 - a][:, :].rearrange("p (n d) -> p n d", d=VW)
                nc.vector.reciprocal(rden[:, a], av[:, :, DK0:DK0 + 1]).then_inc(rden_done, 1)
                dve.wait_ge(rden_done, b.count(2, a + 1))
                if a == 0:
                    wait(dve, attT_ready, b.count(1, 0))
                half = att0[:, :, a * D // 2:(a + 1) * D // 2].rearrange("p t (h d) -> p t h d", d=DK0)
                nc.vector.tensor_tensor(half, av[:, :, 0:DK0].rearrange("p (t h) d -> p t h d", t=TPB),
                                        rden[:, a].rearrange("p (t h) d -> p t h d", t=TPB)
                                        .to_broadcast([P, TPB, H0 // 2, DK0]), op=ALU.mult).then_inc(att_done, 1)

            def residual(b):
                if b.fixed() and b.index() == 0:
                    dve.wait_ge(x_in, 16)
                dve.wait_ge(wo_ready, b.count(1, 1))
                at = b.count(TPB)
                x = X[:, at:at + TPB, :] if b.fixed() else X[:, bass.ds(at, TPB), :]
                nc.vector.tensor_tensor(yres[:, 0:TPB, :], bank[6][:, 0:TPB * D].rearrange("p (t d) -> p t d", d=D),
                                        x, op=ALU.add).then_inc(ln_step, 1)

            def statistics(b):
                dve.wait_ge(ln_step, b.count(5, 1))
                for i in range(TPB):
                    nc.vector.bn_stats(bst[:, i, :], yres[:, i, :]).then_inc(ln_step, 1)

            def aggregate(b):
                dve.wait_ge(ln_step, b.count(5, 3))
                pass_on()
                for i in range(TPB):
                    nc.vector.bn_aggr(mv[:, i, :], bst[:, i, :]).then_inc(ln_step, 1)

            def apply_norm(b):
                dve.wait_ge(rstd_step, b.count(2, 2))
                wait(dve, xT_ready, b.count(1, 0))
                wait(dve, xn_kept, b.count(1, 0))
                for i in range(TPB):
                    last = nc.vector.tensor_scalar(xn[:, i, :], yres[:, i, :], mv[:, i, 0:1], rstd[:, i:i + 1],
                                                   ALU.subtract, ALU.mult)
                last.then_inc(xn_done, 1)

            def step(b):
                nxt, nxt2, prev = b.plus(1), b.plus(2), b.plus(-1)
                for j in range(UNITS):
                    if j == 0 and nxt2.valid():
                        rotate(nxt2)
                    if j == 2 and prev.valid():
                        normalise(prev, 0)
                    if j == 4 and prev.valid():
                        normalise(prev, 1)
                    if j == 6 and prev.valid():
                        residual(prev)
                    if j == 8 and prev.valid():
                        statistics(prev)
                    if j == 9 and prev.valid():
                        aggregate(prev)
                    if nxt.valid():
                        take_max(nxt, j)
                    if j == 11 and prev.valid():
                        apply_norm(prev)
                if nxt.valid():
                    split_max(nxt)

            dve.wait_ge(rope_in, 16)
            over_sequences(dve, -2, step, end=B)

            steps = [0]

            def gated(ins):
                steps[0] += 1
                ins.then_inc(gate_step, 1)
                dve.wait_ge(gate_step, steps[0])

            def every(ap):
                return ap.rearrange("p (n o) -> p n o", o=1).to_broadcast([P, NT, NE])

            logits = bank[2][:, 0:NT * NE].rearrange("p (n e) -> p n e", e=NE)
            ranks = rank[:, None, :].to_broadcast([P, NT, NE])
            dve.wait_ge(sc_ready, UNITS * B)
            dve.wait_ge(max_ready, UNITS * B)
            gated(nc.vector.memset(gate[:, :, :], 0.0))
            gated(nc.vector.memset(gate[:, :, 0:1], 1.0))

            last_b = Batch(0, B - 1).plus(0)
            normalise(last_b, 0)
            normalise(last_b, 1)
            residual(last_b)
            statistics(last_b)
            aggregate(last_b)
            apply_norm(last_b)

            dve.wait_ge(route_ready, 1)
            gated(nc.vector.tensor_reduce(gmax, logits, axis=AX.X, op=ALU.max))
            gated(nc.vector.tensor_tensor(probs, logits, every(gmax), op=ALU.subtract))
            dve.wait_ge(gate_exp, 1)
            gated(nc.vector.tensor_reduce(gsum, prb2, axis=AX.X, op=ALU.add))
            gated(nc.vector.reciprocal(grec, gsum))
            gated(nc.vector.tensor_tensor(probs, prb2, every(grec), op=ALU.mult))
            for p, top, wm, sel in ((probs, top1, wmax, sel1), (prb2, top2, wmax2, sel2)):
                gated(nc.vector.tensor_reduce(top, p, axis=AX.X, op=ALU.max))
                gated(nc.vector.tensor_tensor(ge, p, every(top), op=ALU.is_ge))
                gated(nc.vector.tensor_tensor(wt, ge, ranks, op=ALU.mult))
                gated(nc.vector.tensor_reduce(wm, wt, axis=AX.X, op=ALU.max))
                gated(nc.vector.tensor_tensor(sel, wt, every(wm), op=ALU.is_equal))
                if sel is sel1:
                    gated(nc.vector.scalar_tensor_tensor(prb2, sel1, -4.0, probs, op0=ALU.mult, op1=ALU.add))
            gated(nc.vector.tensor_tensor(tsum, top1, top2, op=ALU.add))
            gated(nc.vector.reciprocal(trec, tsum))
            gated(nc.vector.tensor_tensor(ge, sel1, every(top1), op=ALU.mult))
            gated(nc.vector.tensor_tensor(wt, sel2, every(top2), op=ALU.mult))
            gated(nc.vector.tensor_tensor(probs, ge, wt, op=ALU.add))
            gated(nc.vector.tensor_tensor(gate[:, :, 1:EXP], probs, every(trec), op=ALU.mult))
            assert steps[0] == GATE_STEPS

            def block_of(n):
                return X[:, n * TBK:(n + 1) * TBK, :] if isinstance(n, int) else X[:, bass.ds(n * TBK, TBK), :]

            def accumulate(n, e):
                dve.wait_ge(down_ready, n * EXP + (e + 1))
                ps = bank[4 + e % 3]
                if e == EXP - 1:
                    dve.wait_ge(acc_done, n * EXP + e)
                    nc.vector.tensor_tensor(yres[:, :, :], ps[:, :].rearrange("p (t d) -> p t d", d=D), yres[:, :, :],
                                            op=ALU.add).then_inc(acc_done, 1)
                    return
                if e == 0:
                    wait(dve, xn2_done, n)
                else:
                    dve.wait_ge(acc_done, n * EXP + e)
                for i in range(TBK):
                    if e > 0:
                        base = yres[:, i, :]
                    elif isinstance(n, int):
                        base = X[:, n * TBK + i, :]
                    else:
                        base = X[:, bass.ds(n * TBK + i, 1), :].rearrange("p o d -> p (o d)")
                    last = nc.vector.scalar_tensor_tensor(yres[:, i, :], ps[:, i * D:(i + 1) * D],
                                                          gb[:, i, e + 1:e + 2], base, op0=ALU.mult, op1=ALU.add)
                last.then_inc(acc_done, 1)

            def moe(n):
                if not has(n):
                    return
                wait(dve, acc_done, n * EXP)
                g = gate[:, n * TBK:(n + 1) * TBK, 0:EXP] if isinstance(n, int) else gate[:, bass.ds(n * TBK, TBK), 0:EXP]
                nc.vector.tensor_copy(gb[:, :, :], g).then_inc(gb_done, 1)
                dve.wait_ge(gb_done, n + 1)
                for e in range(EXP):
                    accumulate(n, e)
                dve.wait_ge(acc_done, n * EXP + EXP)
                for i in range(TBK):
                    nc.vector.bn_stats(bst[:, i, :], yres[:, i, :]).then_inc(ln2_step, 1)
                dve.wait_ge(ln2_step, n * 8 + 4)
                pass_on()
                for i in range(TBK):
                    nc.vector.bn_aggr(mv[:, i, :], bst[:, i, :]).then_inc(ln2_step, 1)
                dve.wait_ge(rstd2_step, n * 2 + 2)
                wait(dve, xT2_ready, n)
                wait(dve, xn2_kept, n)
                for i in range(TBK):
                    last = nc.vector.tensor_scalar(xn[:, i, :], yres[:, i, :], mv[:, i, 0:1], rstd[:, i:i + 1],
                                                   ALU.subtract, ALU.mult)
                last.then_inc(xn2_done, 1)
            dve.wait_ge(xn_kept, B)
            over_blocks(dve, moe)

            dve.wait_ge(down_ready, NBLK * EXP)
            dve.wait_ge(w_coarse, 3)
            nc.vector.tensor_tensor(wqkv[1][:, 2, :], wv[:, :], wqkv[0][:, 2, :].bitcast(F32),
                                    op=ALU.subtract).then_inc(wv_fine, 1)
            dve.wait_ge(w3_in, 14 * 16)
            dve.wait_ge(deq_step, 4)
            dve.wait_ge(xn2_kept, NBLK)

            def add_bias3(b, u):
                dve.wait_ge(p3_ready, b.count(UNITS, u + 9))
                if u == 0:
                    wait(dve, num_ready, b.count(8, -8))
                i, half = divmod(u, 2)
                out = Vc[:, b.rem % 2, i, half * 8:(half + 1) * 8, :].rearrange("p h d -> p (h d)")
                nc.vector.tensor_tensor(out, bank[u % 2][:, :], bv[:, half * 512:(half + 1) * 512],
                                        op=ALU.add).then_inc(v3_done, 1)

            def weight3(b, j):
                dve.wait_ge(s3_ready, b.count(UNITS, j + 1))
                half, odd, u, pairs = unit3(j)
                if j % 6 == 0:
                    wait(dve, num_ready, b.count(8, 4 * half - 4))
                if u == 2:
                    shape, tab = [P, 4, P], dtab[:, 0:P]
                else:
                    shape, tab = [P, 2, S], dtab[:, :]
                nc.vector.tensor_tensor(ET3[:, j, :].rearrange("p (h q) -> p h q", h=shape[1]),
                                        bank[2 + j % 2][:, :].rearrange("p (h q) -> p h q", h=shape[1]),
                                        tab[:, None, :].to_broadcast(shape), op=ALU.mult).then_inc(s3_taken, 1)

            def divide3(b, g):
                dve.wait_ge(num_copied, b.count(HG, g + 1))
                dve.wait_ge(spread_ready, b.count(HG, g + 1))
                if g == 0:
                    wait(dve, o3_ready, b.count(1, 0))
                nc.vector.tensor_tensor(attT[:, 2 * g:2 * g + 2, :].rearrange("p c t -> p (c t)"),
                                        num[:, 2 * g:2 * g + 2, :].rearrange("p c t -> p (c t)"), bank[6 + g % 2][:, :],
                                        op=ALU.mult).then_inc(att3_done, 1)

            def invert3(b, half):
                q = slice(half * P, (half + 1) * P)
                if half == 0:
                    dve.wait_ge(num_ready, b.count(8, 8))
                    wait(dve, spread_ready, b.count(HG, 0))
                    nc.vector.tensor_scalar(den3, bank[5][:, 0:S], 1e-6, None, ALU.max).then_inc(den_step, 1)
                    dve.wait_ge(den_step, b.count(7, 1))
                nc.vector.reciprocal(rec3[:, q], den3[:, q]).then_inc(den_step, 1)
                dve.wait_ge(den_step, b.count(7, 3 * half + 2))
                nc.vector.tensor_copy(recs[:, 0, q], rec3[:, q]).then_inc(den_step, 1)
                dve.wait_ge(den_step, b.count(7, 3 * half + 3))
                nc.vector.tensor_tensor(recs[:, 1, q], rec3[:, q], recs[:, 0, q].bitcast(F32),
                                        op=ALU.subtract).then_inc(den_step, 1)

            def residual3(b):
                dve.wait_ge(o3_ready, b.count(1, 1))
                at = b.count(TPB)
                x = X[:, at:at + TPB, :] if b.fixed() else X[:, bass.ds(at, TPB), :]
                wait(dve, xn3_done, b.count(1, 0))
                nc.vector.tensor_tensor(yres[:, 0:TPB, :], bank[6][:, 0:TPB * D].rearrange("p (t d) -> p t d", d=D),
                                        x, op=ALU.add).then_inc(ln3_step, 1)
                dve.wait_ge(ln3_step, b.count(6, 1))
                nc.vector.tensor_tensor(yres[:, 0:TPB, :], yres[:, 0:TPB, :],
                                        bo[:, None, :].to_broadcast([P, TPB, D]), op=ALU.add).then_inc(ln3_step, 1)
                dve.wait_ge(ln3_step, b.count(6, 2))
                for i in range(TPB):
                    nc.vector.bn_stats(bst[:, i, :], yres[:, i, :]).then_inc(ln3_step, 1)
                dve.wait_ge(ln3_step, b.count(6, 4))
                pass_on()
                for i in range(TPB):
                    nc.vector.bn_aggr(mv[:, i, :], bst[:, i, :]).then_inc(ln3_step, 1)

            def apply3(b):
                dve.wait_ge(rstd3_step, b.count(2, 2))
                at = b.count(TPB)
                for i in range(TPB):
                    x = X[:, at + i, :] if b.fixed() else X[:, bass.ds(at + i, 1), :].rearrange("p o d -> p (o d)")
                    last = nc.vector.tensor_scalar(x, yres[:, i, :], mv[:, i, 0:1], rstd[:, i:i + 1],
                                                   ALU.subtract, ALU.mult)
                last.then_inc(xn3_done, 1)

            def cosformer(b, beside={}):
                nxt, prev, prev2 = b.plus(1), b.plus(-1), b.plus(-2)
                for j in range(UNITS):
                    if j in beside:
                        beside[j]()
                    if b.valid():
                        weight3(b, j)
                    if j == 0 and prev2.valid():
                        apply3(prev2)
                    if j in (3, 4) and prev.valid():
                        invert3(prev, j - 3)
                    if 6 <= j < 10 and prev.valid():
                        divide3(prev, j - 6)
                    if j >= 8 and nxt.valid():
                        add_bias3(nxt, j - 8)
                if prev.valid():
                    residual3(prev)
            over_sequences(dve, -1, cosformer, end=B)


            def tile4(n, i):
                at = n.count(TBK, i)
                return X[:, at, :] if n.fixed() else X[:, bass.ds(at, 1), :].rearrange("p o d -> p (o d)")

            def moments(n):
                wait(dve, h_done, n.count(1))
                for i in range(TBK):
                    nc.vector.bn_stats(bst4[:, i, :], tile4(n, i)).then_inc(pre_step, 1)
                dve.wait_ge(pre_step, n.count(8, 4))
                pass_on()
                for i in range(TBK):
                    nc.vector.bn_aggr(mv4[:, i, :], bst4[:, i, :]).then_inc(pre_step, 1)

            def apply_pre(n):
                dve.wait_ge(prstd_step, n.count(2, 2))
                wait(dve, hT_ready, n.count(1))
                for i in range(TBK):
                    last = nc.vector.tensor_scalar(xn2[:, i, :], tile4(n, i), mv4[:, i, 0:1], rstd4[:, i:i + 1],
                                                   ALU.subtract, ALU.mult)
                last.then_inc(h_done, 1)

            def residual4(n):
                dve.wait_ge(down4_ready, n.count(1, 1))
                dve.wait_ge(base_step, n.count(2, 2))
                wait(dve, xo_done, n.count(1))
                nc.vector.scalar_tensor_tensor(yo[:, :, :], bank[4 + n.rem][:, :].rearrange("p (t d) -> p t d", d=D), 0.5,
                                               base4[:, n.rem], op0=ALU.mult, op1=ALU.add).then_inc(z_step, 1)
                dve.wait_ge(z_step, n.count(9, 10))
                for i in range(TBK):
                    nc.vector.bn_stats(bst[:, i, :], yo[:, i, :]).then_inc(z_step, 1)
                dve.wait_ge(z_step, n.count(9, 14))
                pass_on()
                for i in range(TBK):
                    nc.vector.bn_aggr(mv[:, i, :], bst[:, i, :]).then_inc(z_step, 1)

            def apply_last(n):
                dve.wait_ge(rstd4_step, n.count(2, 2))
                wait(dve, out_done, n.count(16))
                for i in range(TBK):
                    last = nc.vector.tensor_scalar(xn[:, i, :], yo[:, i, :], mv[:, i, 0:1], rstd[:, i:i + 1],
                                                   ALU.subtract, ALU.mult)
                last.then_inc(xo_done, 1)

            def ffn(n):
                nxt2, prev = n.plus(2), n.plus(-1)
                if nxt2.valid():
                    moments(nxt2)
                    apply_pre(nxt2)
                if prev.valid():
                    residual4(prev)
                    apply_last(prev)

            def prepare(n):
                moments(n)
                apply_pre(n)
            cosformer(Batch(B // 4, 0), {1: lambda: prepare(block4(0)), 5: lambda: prepare(block4(1))})
            ffn(block4(0))
            apply3(Batch(0, B - 1).plus(0))
            dve.wait_ge(xn3_done, B)
            nc.vector.tensor_copy(beat[:, UNITS:UNITS + 1], mhalf[:, 0:1]).then_inc(z_step, 9)
            over_pairs(dve, ffn)

        @block.scalar
        def _(act):
            def load_later(b):
                part = {-1: 0, 0: 1, 1: 2, 14: 3, 15: 4}.get(b.index() if b.fixed() else None)
                if part is None:
                    return
                if part == 0:
                    act.dma_start(b1[:, :, :], t["b1"]).then_inc(w1_in, 16)
                for e in range(2 * part, min(2 * part + 2, EXP)):
                    n = expert(e) - 1
                    act.dma_start(w1[:, e, :], t["w1s"] if n < 0 else t["w1"][n]).then_inc(w1_in, 16)
                    act.dma_start(w2[:, e], (t["w2s"] if n < 0 else t["w2"][n])
                                  .rearrange("(c p) n -> p c n", p=P)).then_inc(w1_in, 16)

            def exponentials(b, j):
                act.wait_ge(sc_ready, b.count(UNITS, j + 1))
                if j % 3 == 0:
                    wait(act, av_ready, b.count(4, j // 3 - 3))
                nc.scalar.activation(ET[:, j, :], bank[j % 2][:, :], ACT.Exp, scale=DK0 ** -0.5).then_inc(exp_done, 1)

            def copy_values(b):
                act.wait_ge(proj_done, b.count(3, 3))
                wait(act, av_ready, b.count(4, -12))
                nc.scalar.activation(V0[:, b.rem, :, :, 0:DK0],
                                     bank[6][:, 0:TPB * D].rearrange("p (t h d) -> p t h d", t=TPB, d=DK0),
                                     ACT.Copy).then_inc(v_copied, 1)

            def copy_av(b, a):
                act.wait_ge(av_ready, b.count(4, 2 * a + 2))
                wait(act, avT_ready, b.count(2, a - 1))
                nc.scalar.activation(av0[:, a], bank[4 + a][:, :], ACT.Copy).then_inc(av_copied, 1)

            def second_part(b):
                act.wait_ge(part_step, b.count(3, 1))
                nc.scalar.activation(parts[:, 1], rem1[:, :, :], ACT.Copy).then_inc(part_step, 1)

            def copy_att(b):
                act.wait_ge(attT_ready, b.count(1, 1))
                wait(act, wo_ready, b.count(1, 0))
                nc.scalar.activation(attT0[:, :], bank[7][:, 0:S], ACT.Copy).then_inc(attT_copied, 1)

            def copy_tokens(b):
                act.wait_ge(xT_ready, b.count(1, 1))
                at = b.count(S)
                x = XT[:, at:at + S] if b.fixed() else XT[:, bass.ds(at, S)]
                nc.scalar.activation(x, bank[7][:, 0:S], ACT.Copy).then_inc(xT_copied, 1)

            def copy_max(b):
                act.wait_ge(nmt_ready, b.count(1, 1))
                nc.scalar.activation(nmt[:, b.rem % 2, :], bank[6][:, 0:S // 2].bitcast(BF16), ACT.Copy).then_inc(nmt_copied, 1)

            def step(b):
                nxt, nxt2, prev = b.plus(1), b.plus(2), b.plus(-1)
                for j in range(UNITS):
                    if j == 3 and nxt2.valid():
                        copy_values(nxt2)
                    if j == 5 and nxt2.valid():
                        second_part(nxt2)
                    if j == 6 and prev.valid():
                        copy_att(prev)
                    if j == 11 and prev.valid():
                        copy_tokens(prev)
                    if j == 11 and nxt.valid():
                        copy_max(nxt)
                    if b.valid():
                        exponentials(b, j)
                    if j == 1 and prev.valid():
                        copy_av(prev, 1)
                    if j == 9 and b.valid():
                        copy_av(b, 0)
                load_later(b)

            act.wait_ge(consts, 1)
            over_sequences(act, -2, step, end=B)

            def coarse(experts):
                for k in experts:
                    nc.scalar.activation(w1_coarse[:, k, :], w1[:, k, :], ACT.Copy).then_inc(w1_split, 1)
            last_b = Batch(0, B - 1).plus(0)
            copy_av(last_b, 1)
            act.wait_ge(max_ready, UNITS * B)
            act.wait_ge(w1_in, (1 + 2 * EXP) * 16)
            coarse(range(0, 3))
            copy_att(last_b)
            coarse(range(3, EXP))
            copy_tokens(last_b)

            act.wait_ge(gate_step, 4)
            nc.scalar.activation(prb2, probs, ACT.Exp).then_inc(gate_exp, 1)

            def moe(n):
                for e in range(EXP):
                    if has(n):
                        for c in range(HC):
                            act.wait_ge(up_ready, n * (EXP * HC) + (e * HC + c + 1))
                            if c == 0:
                                wait(act, down_ready, n * EXP + (e - 2))
                            nc.scalar.activation(hid[:, e % 3, c, :], bank[c][:, :], ACT.Gelu_apprx_tanh,
                                                 bias=b1[:, expert(e), c:c + 1]).then_inc(gelu_done, 1)
                    if isinstance(n, int) and n == 0 and e in (3, 4):
                        half = e - 3
                        act.wait_ge(gateT_ready, half + 1)
                        nc.scalar.activation(gateT[:, 4 * half:4 * half + 4, :].rearrange("p n t -> p (n t)"),
                                             bank[7][:, :], ACT.Copy).then_inc(gateT_copied, 1)
                    if e == 3 and has(n - 1):
                        act.wait_ge(xT2_ready, n)
                        m = n - 1
                        x = XT[:, m * BLK:(m + 1) * BLK] if isinstance(m, int) else XT[:, bass.ds(m * BLK, BLK)]
                        nc.scalar.activation(x, bank[7][:, :], ACT.Copy).then_inc(xT2_copied, 1)
            over_blocks(act, moe, tail=False)

            act.wait_ge(w3_in, 13 * 16)
            act.wait_ge(up_ready, NBLK * EXP * HC)
            for k, w in enumerate((wq, wk, wv)):
                nc.scalar.activation(wqkv[0][:, k, :], w[:, :], ACT.Copy).then_inc(w_coarse, 1)
            def cosformer(b, beside={}):
                nxt, prev = b.plus(1), b.plus(-1)

                def copy_num(b, g):
                    act.wait_ge(num_ready, b.count(8, 2 * g + 2))
                    wait(act, att3_done, b.count(HG, g - 3))
                    nc.scalar.activation(num[:, 2 * g:2 * g + 2, :].rearrange("p c t -> p (c t)"), bank[4][:, :], ACT.Copy).then_inc(num_copied, 1)

                for j in range(UNITS):
                    if j in beside:
                        beside[j]()
                    if j < 8 and nxt.valid():
                        act.wait_ge(p3_ready, nxt.count(UNITS, j + 1))
                        if j == 0:
                            wait(act, s3_ready, nxt.count(UNITS, -UNITS))
                        for k, bias in enumerate((bq, bk)):
                            nc.scalar.activation(QK[:, nxt.rem % 2, k, j, :], bank[j % 2][:, k * S:(k + 1) * S],
                                                 ACT.Relu, bias=bias[:, j:j + 1]).then_inc(relu_done, 1)
                    if j in (0, 2) and prev.valid():
                        copy_num(prev, 2 + j // 2)
                    if j in (7, 9) and b.valid():
                        copy_num(b, (j - 7) // 2)
            act.wait_ge(acc_done, NBLK * EXP - 1)
            cosformer(Batch(-1, 3))
            moe(NBLK)
            act.wait_ge(w3_in, 14 * 16)
            nc.scalar.activation(spread_r[:, :, :], spread, ACT.Copy).then_inc(w_coarse, 1)
            over_sequences(act, 0, cosformer, end=B)

            def activations(n):
                for c in range(HC):
                    act.wait_ge(up4_ready, n.count(HC, c + 1))
                    if c == 0:
                        wait(act, down4_ready, n.count(1, -1))
                    nc.scalar.activation(yT[:, n.rem, c, :], bank[c][:, :], ACT.Silu,
                                         bias=fb1[:, c:c + 1]).then_inc(silu_done, 1)

            def copy_tokens4(n):
                act.wait_ge(hT_ready, n.count(1, 1))
                wait(act, up4_ready, n.count(HC, -HC))
                nc.scalar.activation(hT[:, n.rem, :], bank[7][:, :], ACT.Identity,
                                     bias=bet[:, :], scale=gam[:, :]).then_inc(hT_copied, 1)

            def ffn(n):
                if n.valid():
                    activations(n)
                if n.plus(1).valid():
                    copy_tokens4(n.plus(1))
            act.wait_ge(s3_ready, UNITS * B)
            cosformer(Batch(B // 4, 0), {3: lambda: copy_tokens4(block4(0)), 5: lambda: activations(block4(0))})
            copy_tokens4(block4(1))
            over_pairs(act, ffn)

        @block.gpsimd
        def _(pool):
            zero = pool.to_reg(0.0)

            def split(b):
                pool.wait_ge(part1, b.count(1, 1))
                nc.gpsimd.tensor_tensor(rem1[:, :, :], qk[:, :, :], parts[:, 0], op=ALU.subtract).then_inc(part_step, 1)
                pool.wait_ge(part_step, b.count(3, 2))
                nc.gpsimd.tensor_tensor(parts[:, 2], rem1[:, :, :], parts[:, 1], op=ALU.subtract).then_inc(part_step, 1)

            def select(b, j):
                pool.wait_ge(exp_done, b.count(UNITS, j + 1))
                nc.gpsimd.tensor_tensor(beat[:, j:j + 1], mhalf[:, 0:1], mhalf[:, 0:1], op=ALU.add)
                if j % 3 == 2:
                    e, n = ET[:, j, :].rearrange("p (h q) -> p h q", q=P), 4
                else:
                    e, n = ET[:, j, :].rearrange("p (h q) -> p h q", q=S)[:, :, 0:P], 2
                nc.gpsimd.affine_select(out=e, in_=e, compare_op=ALU.is_ge, fill=zero, base=0,
                                        pattern=[[0, n], [1, P]], channel_multiplier=-1).then_inc(sel_done, 1)

            def deviation(b):
                pool.wait_ge(ln_step, b.count(5, 5))
                nc.gpsimd.tensor_tensor(veps[:, 0:TPB], mv[:, 0:TPB, 1], epsc[:, 0:TPB], op=ALU.add).then_inc(rstd_step, 1)
                pool.wait_ge(rstd_step, b.count(2, 1))
                nc.gpsimd.tensor_tensor(rstd[:, 0:TPB], veps[:, 0:TPB], mhalf[:, 0:TPB], op=ALU.pow).then_inc(rstd_step, 1)

            def keep(b):
                pool.wait_ge(xn_done, b.count(1, 1))
                at = b.count(TPB)
                x = X[:, at:at + TPB, :] if b.fixed() else X[:, bass.ds(at, TPB), :]
                nc.gpsimd.tensor_copy(x, xn[:, 0:TPB, :]).then_inc(xn_kept, 1)

            def step(b):
                nxt2, prev = b.plus(2), b.plus(-1)
                for j in range(UNITS):
                    if b.valid():
                        select(b, j)
                    if j == 2 and nxt2.valid():
                        split(nxt2)
                    if j == 7 and prev.valid():
                        deviation(prev)
                    if j == 10 and prev.valid():
                        keep(prev)

            pool.wait_ge(consts, 1)
            over_sequences(pool, -2, step, end=B)

            def split_block(n):
                wait(pool, up_ready, n * (EXP * HC))
                nc.gpsimd.tensor_tensor(beat[:, 0:1], mhalf[:, 0:1], mhalf[:, 0:1], op=ALU.add)
                x = XT[:, n * BLK:(n + 1) * BLK] if isinstance(n, int) else XT[:, bass.ds(n * BLK, BLK)]
                nc.gpsimd.tensor_copy(xp[:, 0, :], x).then_inc(xp_done, 1)
                pool.wait_ge(xp_done, 2 * n + 1)
                nc.gpsimd.tensor_tensor(beat[:, 1:2], mhalf[:, 0:1], mhalf[:, 0:1], op=ALU.add)
                nc.gpsimd.tensor_tensor(xp[:, 1, :], x, xp[:, 0, :].bitcast(F32), op=ALU.subtract).then_inc(xp_done, 1)

            def fine(experts):
                for k in experts:
                    pool.wait_ge(w1_split, k + 1)
                    nc.gpsimd.tensor_tensor(w1_fine[:, k, :], w1[:, k, :], w1_coarse[:, k, :].bitcast(F32),
                                            op=ALU.subtract).then_inc(w1_fined, 1)

            pool.wait_ge(sc_ready, UNITS * B)
            pool.wait_ge(max_ready, UNITS * B)
            pool.wait_ge(xT_copied, BLK // S)
            split_block(0)
            fine(range(0, 2))
            last_b = Batch(0, B - 1).plus(0)
            deviation(last_b)
            keep(last_b)
            fine(range(2, EXP))

            pool.wait_ge(fq_in, 64)
            for a in range(2):
                nc.gpsimd.tensor_scalar(fd[:, a], fq[:, a], -128.0, None, ALU.add).then_inc(deq_step, 1)
                pool.wait_ge(deq_step, 2 * a + 1)
                w = f1[:, :] if a == 0 else f2[:, :, :].rearrange("p c n -> p (c n)")
                nc.gpsimd.tensor_tensor(w, fd[:, a], fs[:, a], op=ALU.mult).then_inc(deq_step, 1)

            def deviations(ready, at, step_sem, tiles, base, mv=mv, veps=veps, rstd=rstd):
                pool.wait_ge(ready, at)
                nc.gpsimd.tensor_tensor(veps[:, 0:tiles], mv[:, 0:tiles, 1], epsc[:, 0:tiles], op=ALU.add).then_inc(step_sem, 1)
                pool.wait_ge(step_sem, base + 1)
                nc.gpsimd.tensor_tensor(rstd[:, 0:tiles], veps[:, 0:tiles], mhalf[:, 0:tiles], op=ALU.pow).then_inc(step_sem, 1)

            def moe(n):
                if has(n) and not (isinstance(n, int) and n == 0):
                    split_block(n)
                if has(n - 1):
                    deviations(ln2_step, n * 8, rstd2_step, TBK, n * 2 - 2)
                    pool.wait_ge(xn2_done, n)
                    at = (n - 1) * TBK
                    x = X[:, at:at + TBK, :] if isinstance(n, int) else X[:, bass.ds(at, TBK), :]
                    nc.gpsimd.tensor_copy(x, xn[:, :, :]).then_inc(xn2_kept, 1)
                if has(n):
                    wait(pool, down_ready, n * EXP)
                    if isinstance(n, int) and n == 0:
                        pool.wait_ge(gateT_copied, 2)
                    g = gateT[:, n, :] if isinstance(n, int) else gateT[:, bass.ds(n, 1), :].rearrange("p o t -> p (o t)")
                    nc.gpsimd.tensor_copy(gTb[:, :], g).then_inc(gTb_done, 1)
            over_blocks(pool, moe, tail=False)

            pool.wait_ge(down_ready, NBLK * EXP - 1)
            def cosformer(b):
                nxt2, prev = b.plus(2), b.plus(-1)
                if nxt2.valid():
                    wait(pool, p3_ready, nxt2.count(UNITS, -UNITS))
                    at = nxt2.count(S)
                    x = XT[:, at:at + S] if nxt2.fixed() else XT[:, bass.ds(at, S)]
                    hi, lo = xt3[:, nxt2.rem % 2, 0, :], xt3[:, nxt2.rem % 2, 1, :]
                    nc.gpsimd.tensor_copy(hi, x).then_inc(xt3_done, 1)
                    pool.wait_ge(xt3_done, nxt2.count(2, 1))
                    nc.gpsimd.tensor_tensor(beat[:, 0:1], mhalf[:, 0:1], mhalf[:, 0:1], op=ALU.add)
                    nc.gpsimd.tensor_tensor(lo, x, hi.bitcast(F32), op=ALU.subtract).then_inc(xt3_done, 1)
                if prev.valid():
                    deviations(ln3_step, prev.count(6, 6), rstd3_step, TPB, prev.count(2, 0))
            cosformer(Batch(-1, 2))
            for k, w in enumerate((wq, wk)):
                pool.wait_ge(w_coarse, k + 1)
                nc.gpsimd.tensor_tensor(wqkv[1][:, k, :], w[:, :], wqkv[0][:, k, :].bitcast(F32),
                                        op=ALU.subtract).then_inc(w_fine, 1)
            moe(NBLK)
            cosformer(Batch(-1, 3))
            over_sequences(pool, 0, cosformer, end=B)

            pool.wait_ge(s3_ready, UNITS * B)
            nc.gpsimd.tensor_tensor(half_bias[:, :], fb2[:, :], mhalf[:, 0:1].to_broadcast([P, D]), op=ALU.mult).then_inc(bias_step, 1)

            def twice(n):
                at = n.count(TBK)
                x = X[:, at:at + TBK, :] if n.fixed() else X[:, bass.ds(at, TBK), :]
                wait(pool, z_step, n.count(9, -8))
                nc.gpsimd.tensor_tensor(base4[:, n.rem], x, x, op=ALU.add).then_inc(base_step, 1)
                pool.wait_ge(base_step, n.count(2, 1))
                nc.gpsimd.tensor_tensor(base4[:, n.rem], base4[:, n.rem], half_bias[:, None, :].to_broadcast([P, TBK, D]),
                                        op=ALU.subtract).then_inc(base_step, 1)

            def ffn(n):
                nxt2, prev = n.plus(2), n.plus(-1)
                if nxt2.valid():
                    deviations(pre_step, nxt2.count(8, 8), prstd_step, TBK, nxt2.count(2), mv4, veps4, rstd4)
                if n.valid():
                    if n.fixed() and n.index() == 0:
                        pool.wait_ge(bias_step, 1)
                        pool.wait_ge(xn3_done, B)
                    twice(n)
                if prev.valid():
                    deviations(z_step, prev.count(9, 18), rstd4_step, TBK, prev.count(2))
            ffn(block4(-2))
            ffn(block4(-1))
            cosformer(Batch(B // 4, 0))
            ffn(block4(0))
            over_pairs(pool, ffn)


def constants():
    bf16 = mybir.dt.np(BF16)
    half = DK0 // 2
    inv = np.float32(10000.0) ** (np.float32(-2.0) * np.arange(half, dtype=np.float32) / np.float32(DK0))
    ang = np.arange(S, dtype=np.float32)[None, :] * inv[:, None]
    d = np.arange(P) % DK0
    sign = np.where(d % 2 == 0, -1.0, 1.0)[:, None]
    rope = np.stack([np.cos(ang)[d // 2], sign * np.sin(ang)[d // 2]], 1).astype(np.float32)
    at = np.arange(P)
    mask = np.where(at[None, :] <= at[:, None], 0.0, BIG).astype(bf16)
    oneh = np.zeros((P, H0, P))
    for s in range(NS):
        for h in range(H0):
            oneh[H0 * s + h, h] = 1.0
    apart = np.arange(S)[None, :] - at[:, None]
    dtab = np.where(apart >= 0, np.cos(np.pi / (2.0 * S) * apart), 0.0).astype(np.float32)
    spread = np.zeros((P, 8, P), np.float32)
    for h in range(H1):
        spread[32 * (h % 4) + h // 4, h // 2, DH1 * (h % 2):DH1 * (h % 2 + 1)] = 1.0
    rank = np.broadcast_to(np.arange(NE, 0, -1, dtype=np.float32), (P, NE))
    return {"rope": rope, "identf": np.eye(P, dtype=np.float32), "identb": np.eye(P).astype(bf16), "maskb": mask,
            "oneh": oneh.astype(bf16), "dtab": dtab, "rank": np.ascontiguousarray(rank), "spread": spread}


def layout(i):
    x = i["L0_attn_x"].reshape(N, D)
    swap = np.arange(D) ^ 1
    a0 = [i["L0_attn_wq"], i["L0_attn_wq"][swap], i["L0_attn_wk"], i["L0_attn_wk"][swap], i["L0_attn_wv"], i["L0_attn_wo"]]
    b1 = np.concatenate([i["L0_ffn_bfc_s"][None], i["L0_ffn_bfc"]]).reshape(EXP, HC, P).transpose(2, 0, 1)
    b2 = np.zeros((TBK, 32, TBK, D), np.float32)
    for k in range(TBK):
        b2[k, 0, k] = i["L0_ffn_bproj_s"]
        b2[k, 1:EXP, k] = i["L0_ffn_bproj"]
    return {
        "x": x, "xT": x.T, "a0": np.stack([w.T for w in a0], 1),
        "wr": i["L0_ffn_Wr"], "w1s": i["L0_ffn_Wfc_s"], "w1": i["L0_ffn_Wfc"], "w2s": i["L0_ffn_Wproj_s"],
        "w2": i["L0_ffn_Wproj"], "b1": b1, "b2": b2.reshape(P, TBK, D),
        "wq": i["L1_attn_Wq"], "wk": i["L1_attn_Wk"], "wv": i["L1_attn_Wv"], "wo": i["L1_attn_Wo"],
        "bq": i["L1_attn_bq"].reshape(8, P).T, "bk": i["L1_attn_bk"].reshape(8, P).T,
        "bv": i["L1_attn_bv"], "bo": i["L1_attn_bo"],
        "fc1_q": i["L1_ffn_fc1_q"], "fc2_q": i["L1_ffn_fc2_q"], "fc1_scales": i["L1_ffn_fc1_scales"].reshape(-1),
        "fc2_scales": i["L1_ffn_fc2_scales"].reshape(-1), "fb1": i["L1_ffn_fc1_bias"].reshape(HC, P).T,
        "fb2": i["L1_ffn_fc2_bias"], "gam": i["L1_ffn_ln_gamma"].reshape(D, 1), "bet": i["L1_ffn_ln_beta"].reshape(D, 1),
    }


def kernel(**inputs):
    import concourse.bacc as bacc
    from concourse.bass_utils import run_bass_kernel_spmd

    given = layout({k: np.asarray(v) for k, v in inputs.items()}) | constants()
    given = {k: np.ascontiguousarray(v) for k, v in given.items()}
    nc = bacc.Bacc("TRN2", target_bir_lowering=False, num_devices=1)
    t = {k: nc.dram_tensor(f"in_{k}", v.shape, mybir.dt.from_np(v.dtype), kind="ExternalInput").ap()
         for k, v in given.items()}
    t["out"] = nc.dram_tensor("out", (N, D), F32, kind="ExternalOutput").ap()
    build(nc, t)
    r = run_bass_kernel_spmd(nc, [{f"in_{k}": v for k, v in given.items()}], core_ids=[0])
    return r.results[0]["out"].reshape(B, S, D)
```
